# Optimizing a Trainium2 kernel written in Bass

```python
import numpy as np
import jax
import jax.numpy as jnp

def _softmax(x, axis=-1):
    return jax.nn.softmax(x, axis=axis)

def _gelu(x):
    return jax.nn.gelu(x, approximate=True)

def _silu(x):
    return jax.nn.silu(x)

def _sigmoid(x):
    return jax.nn.sigmoid(x)

def _layernorm(x, axis=-1, eps=1e-05):
    m = jnp.mean(x, axis=axis, keepdims=True)
    v = jnp.var(x, axis=axis, keepdims=True)
    return (x - m) / jnp.sqrt(v + eps)

def _scatter_add(tgt, idx, src, axis=0):
    return tgt.at[idx].add(src)

def _segment_sum(src, seg, n):
    return jax.ops.segment_sum(src, seg, n)
kernel_name = 'mk_decoder_postln_d2_seqx_r2_99434d'

def setup_inputs(seed: int=0):
    np.random.seed(seed)
    _w = jnp.asarray

    def _rec_inputs():
        import jax
        import jax.numpy as jnp
        _rk = jax.random.key(seed)
        x = 0.0002417 + 0.9998 * jax.random.normal(jax.random.fold_in(_rk, 1), (8, 224, 512), jnp.float32)
        _lenS = 224 - jax.random.randint(jax.random.fold_in(_rk, 7), (8,), 0, max(1, 224 // 4) + 1, jnp.int32)
        _lenS2 = 750 - jax.random.randint(jax.random.fold_in(_rk, 8), (8,), 0, max(1, 750 // 4) + 1, jnp.int32)
        _ctx_1024P = jax.random.normal(jax.random.fold_in(_rk, 11), (8, 16, 512), jnp.float32)
        _ctx_1024c = jax.random.dirichlet(jax.random.fold_in(_rk, 511), 0.3 * jnp.ones((16,), jnp.float32), (8, 750))
        _ctx_1024t = jnp.einsum('bsk,bkd->bsd', _ctx_1024c, _ctx_1024P)
        _ctx_1024t = _ctx_1024t * jax.lax.rsqrt(jnp.mean(jnp.square(_ctx_1024t)) + 1e-12) * 0.953939
        ctx_1024 = 7.22013e-05 + 1.00017 * (_ctx_1024t + 0.3 * jax.random.normal(jax.random.fold_in(_rk, 611), (8, 750, 512), jnp.float32))
        return (x, ctx_1024)
    x, ctx_1024 = _rec_inputs()

    def _L0_attn_setup():
        import jax, jax.numpy as jnp
        import numpy as np
        NUM_BUCKETS = 63

        def _rp_bucket(N):
            rel = jnp.arange(N)[None, :] - jnp.arange(N)[:, None]
            half = NUM_BUCKETS // 2
            return (jnp.clip(rel, -half, half) + half).astype(jnp.int32)
        key = jax.random.key(seed)
        ks = jax.random.split(key, 7)
        B, N, C, H = (4, 512, 512, 16)
        hd = C // H
        g = lambda k, shp, sc: jax.random.normal(k, shp, jnp.float32) * sc
        return {'x': g(ks[0], (B, N, C), 1.0), 'w_qkv': g(ks[1], (3 * C, C), C ** (-0.5)), 'w_proj': g(ks[2], (C, C), C ** (-0.5)), 'b_proj': jnp.zeros((C,), jnp.float32), 'rpe_q_table': g(ks[3], (H, hd, NUM_BUCKETS), 0.02), 'rpe_k_table': g(ks[4], (H, hd, NUM_BUCKETS), 0.02), 'rpe_v_table': g(ks[5], (H, NUM_BUCKETS, hd), 0.02)}
    _L0_attn_all = _L0_attn_setup()
    _L0_attn_in = {k: v for k, v in _L0_attn_all.items() if k in ('w_qkv', 'w_proj', 'b_proj', 'rpe_q_table', 'rpe_k_table', 'rpe_v_table')}
    del _L0_attn_all

    def _L0_xattn_setup():
        import jax, jax.numpy as jnp
        import numpy as np
        EMBED = 512
        HEADS = 16
        HEAD_DIM = EMBED // HEADS
        key = jax.random.key(seed)
        ks = jax.random.split(key, 8)
        N, L = (4, 1024)
        values = jax.random.normal(ks[0], (N, L, EMBED), dtype=jnp.float32)
        keys_ = jax.random.normal(ks[1], (N, L, EMBED), dtype=jnp.float32)
        queries = jax.random.normal(ks[2], (N, L, EMBED), dtype=jnp.float32)
        s = 1.0 / np.sqrt(HEAD_DIM)
        Wv = jax.random.normal(ks[3], (HEAD_DIM, HEAD_DIM), dtype=jnp.float32) * s
        Wk = jax.random.normal(ks[4], (HEAD_DIM, HEAD_DIM), dtype=jnp.float32) * s
        Wq = jax.random.normal(ks[5], (HEAD_DIM, HEAD_DIM), dtype=jnp.float32) * s
        Wo = jax.random.normal(ks[6], (EMBED, EMBED), dtype=jnp.float32) * (1.0 / np.sqrt(EMBED))
        bo = jnp.zeros((EMBED,), dtype=jnp.float32)
        return {'values': values, 'keys': keys_, 'queries': queries, 'Wv': Wv, 'Wk': Wk, 'Wq': Wq, 'Wo': Wo, 'bo': bo}
    _L0_xattn_all = _L0_xattn_setup()
    _L0_xattn_in = {k: v for k, v in _L0_xattn_all.items() if k in ('Wv', 'Wk', 'Wq', 'Wo', 'bo')}
    del _L0_xattn_all

    def _L0_ffn_setup():
        import jax, jax.numpy as jnp
        import numpy as np
        TOP_K = 2
        CAP_FACTOR = 1.25
        MIN_CAPACITY = 4
        key = jax.random.key(seed)
        k1, k2, k3, k4 = jax.random.split(key, 4)
        B, T, C, E = (8, 1024, 512, 8)
        x = jax.random.normal(k1, (B, T, C), dtype=jnp.float32)
        w_g = jax.random.normal(k2, (E, C), dtype=jnp.float32) * 0.02
        c_fc = jax.random.normal(k3, (E, C, 4 * C), dtype=jnp.float32) * 0.02
        c_proj = jax.random.normal(k4, (E, 4 * C, C), dtype=jnp.float32) * 0.02
        return {'x': x, 'w_g': w_g, 'c_fc': c_fc, 'c_proj': c_proj}
    _L0_ffn_all = _L0_ffn_setup()
    _L0_ffn_in = {k: v for k, v in _L0_ffn_all.items() if k in ('w_g', 'c_fc', 'c_proj')}
    del _L0_ffn_all

    def _L1_attn_setup():
        import jax, jax.numpy as jnp
        import numpy as np
        B, S, H, NH, P = (1, 1024, 512, 16, 2)
        D = H // NH
        SCALE = 1.0 / np.sqrt(D).astype(np.float32)

        def _lin(x, W, b):
            return x @ W + b

        def _split_heads(x):
            return x.reshape(*x.shape[:-2], x.shape[-2], NH, D).swapaxes(-3, -2)

        def _merge_heads(x):
            return x.swapaxes(-3, -2).reshape(*x.shape[:-3], x.shape[-2], H)
        key = jax.random.key(seed)
        ks = jax.random.split(key, 20)
        w = lambda k, i, o: jax.random.normal(k, (i, o), jnp.float32) * 0.02
        inp = {'hidden_states': jax.random.normal(ks[0], (B, S, H), jnp.float32), 'past_states': jax.random.normal(ks[1], (P, B, S, H), jnp.float32), 'Wq': w(ks[2], H, H), 'bq': jnp.zeros((H,), jnp.float32), 'Wk': w(ks[3], H, H), 'bk': jnp.zeros((H,), jnp.float32), 'Wv': w(ks[4], H, H), 'bv': jnp.zeros((H,), jnp.float32), 'Wo': w(ks[5], H, H), 'bo': jnp.zeros((H,), jnp.float32), 'Wrq': w(ks[6], H, H), 'brq': jnp.zeros((H,), jnp.float32), 'Wrk': w(ks[7], H, H), 'brk': jnp.zeros((H,), jnp.float32), 'Wrv': w(ks[8], H, H), 'brv': jnp.zeros((H,), jnp.float32), 'Wg': w(ks[9], 2 * H, H), 'bg': jnp.zeros((H,), jnp.float32)}
        return inp
    _L1_attn_all = _L1_attn_setup()
    _L1_attn_in = {k: v for k, v in _L1_attn_all.items() if k in ('past_states', 'Wq', 'bq', 'Wk', 'bk', 'Wv', 'bv', 'Wo', 'bo', 'Wrq', 'brq', 'Wrk', 'brk', 'Wrv', 'brv', 'Wg', 'bg')}
    del _L1_attn_all

    def _L1_xattn_setup():
        import jax, jax.numpy as jnp
        import numpy as np
        EMBED_DIM = 512
        NUM_HEADS = 16
        HEAD_DIM = EMBED_DIM // NUM_HEADS
        WINDOW = 64

        def apply_rope(x):
            B, H, S, d = x.shape
            half = d // 2
            pos = jnp.arange(S, dtype=x.dtype)
            freqs = 1.0 / 10000.0 ** (jnp.arange(half, dtype=x.dtype) / half)
            ang = pos[:, None] * freqs[None, :]
            cos, sin = (jnp.cos(ang), jnp.sin(ang))
            x1, x2 = (x[..., :half], x[..., half:])
            return jnp.concatenate([x1 * cos - x2 * sin, x1 * sin + x2 * cos], axis=-1)

        def _forward(query, key, value, q_w, q_b, k_w, k_b, v_w, v_b, o_w, o_b):
            B, S_q, D = query.shape
            S_k = key.shape[1]
            H, d, W = (NUM_HEADS, HEAD_DIM, WINDOW)
            q = (query @ q_w.T + q_b).reshape(B, S_q, H, d).transpose(0, 2, 1, 3)
            k = (key @ k_w.T + k_b).reshape(B, S_k, H, d).transpose(0, 2, 1, 3)
            v = (value @ v_w.T + v_b).reshape(B, S_k, H, d).transpose(0, 2, 1, 3)
            q = apply_rope(q) * d ** (-0.5)
            k = apply_rope(k)
            q_pos = jnp.arange(S_q)[:, None]
            offsets = jnp.arange(-W, 1)[None, :]
            idx = q_pos + offsets
            local_mask = (idx < 0) | (idx >= S_k)
            gidx = jnp.clip(idx, 0, S_k - 1)
            k_win = k[:, :, gidx, :]
            v_win = v[:, :, gidx, :]
            scores = jnp.einsum('bhqd,bhqwd->bhqw', q, k_win)
            mask = local_mask[None, None, :, :]
            scores = jnp.where(mask, -jnp.inf, scores)
            m = jnp.max(scores, axis=-1, keepdims=True)
            m = jnp.where(jnp.isfinite(m), m, 0.0)
            e = jnp.exp(scores - m)
            denom = jnp.sum(e, axis=-1, keepdims=True)
            probs = jnp.where(denom > 0, e / jnp.where(denom > 0, denom, 1.0), 0.0)
            ctx = jnp.einsum('bhqw,bhqwd->bhqd', probs, v_win)
            ctx = ctx.transpose(0, 2, 1, 3).reshape(B, S_q, D)
            return ctx @ o_w.T + o_b
        key = jax.random.key(seed)
        ks = jax.random.split(key, 12)
        B, S, D = (1, 1024, EMBED_DIM)
        scale = 1.0 / np.sqrt(D)
        inp = {'query': jax.random.normal(ks[0], (B, S, D), jnp.float32), 'key': jax.random.normal(ks[1], (B, S, D), jnp.float32), 'value': jax.random.normal(ks[2], (B, S, D), jnp.float32), 'q_w': jax.random.normal(ks[3], (D, D), jnp.float32) * scale, 'q_b': jax.random.normal(ks[4], (D,), jnp.float32) * 0.01, 'k_w': jax.random.normal(ks[5], (D, D), jnp.float32) * scale, 'k_b': jax.random.normal(ks[6], (D,), jnp.float32) * 0.01, 'v_w': jax.random.normal(ks[7], (D, D), jnp.float32) * scale, 'v_b': jax.random.normal(ks[8], (D,), jnp.float32) * 0.01, 'o_w': jax.random.normal(ks[9], (D, D), jnp.float32) * scale, 'o_b': jax.random.normal(ks[10], (D,), jnp.float32) * 0.01}
        return inp
    _L1_xattn_all = _L1_xattn_setup()
    _L1_xattn_in = {k: v for k, v in _L1_xattn_all.items() if k in ('q_w', 'q_b', 'k_w', 'k_b', 'v_w', 'v_b', 'o_w', 'o_b')}
    del _L1_xattn_all

    def _L1_ffn_setup():
        import math
        import jax, jax.numpy as jnp
        import numpy as np
        D_MODEL = 512
        D_HIDDEN = 2048
        N_EXPERTS = 8
        TOP_K = 2
        CAPACITY_FACTOR = 1.25
        key = jax.random.key(seed)
        ks = jax.random.split(key, 8)
        s = 0.02
        x = jax.random.normal(ks[0], (4, 1024, D_MODEL), dtype=jnp.float32)
        router_w = jax.random.normal(ks[1], (D_MODEL, N_EXPERTS), dtype=jnp.float32) * s
        router_b = jnp.zeros((N_EXPERTS,), dtype=jnp.float32)
        w1 = jax.random.normal(ks[2], (N_EXPERTS, D_MODEL, D_HIDDEN), dtype=jnp.float32) * s
        b1 = jnp.zeros((N_EXPERTS, D_HIDDEN), dtype=jnp.float32)
        w2 = jax.random.normal(ks[3], (N_EXPERTS, D_HIDDEN, D_MODEL), dtype=jnp.float32) * s
        b2 = jnp.zeros((N_EXPERTS, D_MODEL), dtype=jnp.float32)
        return {'x': x, 'router_w': router_w, 'router_b': router_b, 'w1': w1, 'b1': b1, 'w2': w2, 'b2': b2}
    _L1_ffn_all = _L1_ffn_setup()
    _L1_ffn_in = {k: v for k, v in _L1_ffn_all.items() if k in ('router_w', 'router_b', 'w1', 'b1', 'w2', 'b2')}
    del _L1_ffn_all
    return {'x': x, 'ctx_1024': ctx_1024, 'L0_attn_w_qkv': _L0_attn_in['w_qkv'], 'L0_attn_w_proj': _L0_attn_in['w_proj'], 'L0_attn_b_proj': _L0_attn_in['b_proj'], 'L0_attn_rpe_q_table': _L0_attn_in['rpe_q_table'], 'L0_attn_rpe_k_table': _L0_attn_in['rpe_k_table'], 'L0_attn_rpe_v_table': _L0_attn_in['rpe_v_table'], 'L0_xattn_Wv': _L0_xattn_in['Wv'], 'L0_xattn_Wk': _L0_xattn_in['Wk'], 'L0_xattn_Wq': _L0_xattn_in['Wq'], 'L0_xattn_Wo': _L0_xattn_in['Wo'], 'L0_xattn_bo': _L0_xattn_in['bo'], 'L0_ffn_w_g': _L0_ffn_in['w_g'], 'L0_ffn_c_fc': _L0_ffn_in['c_fc'], 'L0_ffn_c_proj': _L0_ffn_in['c_proj'], 'L1_attn_past_states': _L1_attn_in['past_states'], 'L1_attn_Wq': _L1_attn_in['Wq'], 'L1_attn_bq': _L1_attn_in['bq'], 'L1_attn_Wk': _L1_attn_in['Wk'], 'L1_attn_bk': _L1_attn_in['bk'], 'L1_attn_Wv': _L1_attn_in['Wv'], 'L1_attn_bv': _L1_attn_in['bv'], 'L1_attn_Wo': _L1_attn_in['Wo'], 'L1_attn_bo': _L1_attn_in['bo'], 'L1_attn_Wrq': _L1_attn_in['Wrq'], 'L1_attn_brq': _L1_attn_in['brq'], 'L1_attn_Wrk': _L1_attn_in['Wrk'], 'L1_attn_brk': _L1_attn_in['brk'], 'L1_attn_Wrv': _L1_attn_in['Wrv'], 'L1_attn_brv': _L1_attn_in['brv'], 'L1_attn_Wg': _L1_attn_in['Wg'], 'L1_attn_bg': _L1_attn_in['bg'], 'L1_xattn_q_w': _L1_xattn_in['q_w'], 'L1_xattn_q_b': _L1_xattn_in['q_b'], 'L1_xattn_k_w': _L1_xattn_in['k_w'], 'L1_xattn_k_b': _L1_xattn_in['k_b'], 'L1_xattn_v_w': _L1_xattn_in['v_w'], 'L1_xattn_v_b': _L1_xattn_in['v_b'], 'L1_xattn_o_w': _L1_xattn_in['o_w'], 'L1_xattn_o_b': _L1_xattn_in['o_b'], 'L1_ffn_router_w': _L1_ffn_in['router_w'], 'L1_ffn_router_b': _L1_ffn_in['router_b'], 'L1_ffn_w1': _L1_ffn_in['w1'], 'L1_ffn_b1': _L1_ffn_in['b1'], 'L1_ffn_w2': _L1_ffn_in['w2'], 'L1_ffn_b2': _L1_ffn_in['b2']}

def reference(x, ctx_1024, L0_attn_w_qkv, L0_attn_w_proj, L0_attn_b_proj, L0_attn_rpe_q_table, L0_attn_rpe_k_table, L0_attn_rpe_v_table, L0_xattn_Wv, L0_xattn_Wk, L0_xattn_Wq, L0_xattn_Wo, L0_xattn_bo, L0_ffn_w_g, L0_ffn_c_fc, L0_ffn_c_proj, L1_attn_past_states, L1_attn_Wq, L1_attn_bq, L1_attn_Wk, L1_attn_bk, L1_attn_Wv, L1_attn_bv, L1_attn_Wo, L1_attn_bo, L1_attn_Wrq, L1_attn_brq, L1_attn_Wrk, L1_attn_brk, L1_attn_Wrv, L1_attn_brv, L1_attn_Wg, L1_attn_bg, L1_xattn_q_w, L1_xattn_q_b, L1_xattn_k_w, L1_xattn_k_b, L1_xattn_v_w, L1_xattn_v_b, L1_xattn_o_w, L1_xattn_o_b, L1_ffn_router_w, L1_ffn_router_b, L1_ffn_w1, L1_ffn_b1, L1_ffn_w2, L1_ffn_b2):
    import jax
    import jax.numpy as jnp

    def _L0_attn_ref(x, w_qkv, w_proj, b_proj, rpe_q_table, rpe_k_table, rpe_v_table):
        import jax, jax.numpy as jnp
        import numpy as np
        NUM_BUCKETS = 63

        def _rp_bucket(N):
            rel = jnp.arange(N)[None, :] - jnp.arange(N)[:, None]
            half = NUM_BUCKETS // 2
            return (jnp.clip(rel, -half, half) + half).astype(jnp.int32)
        B, N, C = x.shape
        H = rpe_k_table.shape[0]
        hd = C // H
        scale = hd ** (-0.5)
        qkv = (x @ w_qkv.T).reshape(B, N, 3, H, hd).transpose(2, 0, 3, 1, 4)
        q, k, v = (qkv[0] * scale, qkv[1], qkv[2])
        attn = jnp.einsum('bhid,bhjd->bhij', q, k)
        rp = _rp_bucket(N)
        idx = rp[None, None]
        qL = jnp.einsum('bhid,hdm->bhim', q, rpe_k_table)
        attn = attn + jnp.take_along_axis(qL, idx, axis=-1)
        kL = jnp.einsum('bhjd,hdm->bhjm', k * scale, rpe_q_table)
        attn = attn + jnp.swapaxes(jnp.take_along_axis(kL, idx, axis=-1), 2, 3)
        attn = jax.nn.softmax(attn, axis=-1)
        out = jnp.einsum('bhij,bhjd->bhid', attn, v)
        a_t = attn.transpose(2, 3, 0, 1)
        S = jax.vmap(lambda a, seg: jax.ops.segment_sum(a, seg, num_segments=NUM_BUCKETS))(a_t, rp)
        out = out + jnp.einsum('inbh,hnd->bhid', S, rpe_v_table)
        x_out = out.transpose(0, 2, 1, 3).reshape(B, N, C)
        return x_out @ w_proj.T + b_proj

    def _L0_xattn_ref(values, keys, queries, Wv, Wk, Wq, Wo, bo):
        import jax, jax.numpy as jnp
        import numpy as np
        EMBED = 512
        HEADS = 16
        HEAD_DIM = EMBED // HEADS
        N, L, _ = queries.shape
        v = values.reshape(N, -1, HEADS, HEAD_DIM)
        k = keys.reshape(N, -1, HEADS, HEAD_DIM)
        q = queries.reshape(N, L, HEADS, HEAD_DIM)
        v = jnp.einsum('nlhd,ed->nlhe', v, Wv)
        k = jnp.einsum('nlhd,ed->nlhe', k, Wk)
        q = jnp.einsum('nqhd,ed->nqhe', q, Wq)
        scores = jnp.einsum('nqhd,nkhd->nhqk', q, k) / jnp.sqrt(jnp.float32(EMBED))
        attn = jax.nn.softmax(scores, axis=-1)
        out = jnp.einsum('nhqk,nkhd->nqhd', attn, v).reshape(N, L, EMBED)
        return out @ Wo.T + bo

    def _L0_ffn_ref(x, w_g, c_fc, c_proj):
        import jax, jax.numpy as jnp
        import numpy as np
        TOP_K = 2
        CAP_FACTOR = 1.25
        MIN_CAPACITY = 4
        B, T, C = x.shape
        E = w_g.shape[0]
        N = B * T
        capacity = max(MIN_CAPACITY, int(CAP_FACTOR * N * TOP_K / E))
        xf = x.reshape(N, C)
        logits = xf @ w_g.T
        top_logits, top_idx = jax.lax.top_k(logits, TOP_K)
        router_probs = jax.nn.softmax(top_logits, axis=-1)
        oh = jax.nn.one_hot(top_idx, E, dtype=jnp.int32)
        oh_t = oh.transpose(1, 0, 2).reshape(TOP_K * N, E)
        pos = jnp.cumsum(oh_t, axis=0).reshape(TOP_K, N, E).transpose(1, 0, 2)
        rank = jnp.sum((pos - 1) * oh, axis=-1)
        valid = rank < capacity
        probs_masked = router_probs * valid.astype(router_probs.dtype)
        rank_c = jnp.clip(rank, 0, capacity - 1)
        contrib = xf[:, None, :] * valid[..., None].astype(xf.dtype)
        buf = jnp.zeros((E, capacity, C), dtype=xf.dtype).at[top_idx, rank_c].add(contrib)
        h = jnp.einsum('ecd,edf->ecf', buf, c_fc)
        h = jnp.square(jax.nn.relu(h))
        expert_out = jnp.einsum('ecf,efd->ecd', h, c_proj)
        gathered = expert_out[top_idx, rank_c]
        out = jnp.sum(gathered * probs_masked[..., None], axis=1)
        return out.reshape(B, T, C)

    def _L1_attn_ref(hidden_states, past_states, Wq, bq, Wk, bk, Wv, bv, Wo, bo, Wrq, brq, Wrk, brk, Wrv, brv, Wg, bg):
        import jax, jax.numpy as jnp
        import numpy as np
        B, S, H, NH, P = (1, 1024, 512, 16, 2)
        D = H // NH
        SCALE = 1.0 / np.sqrt(D).astype(np.float32)

        def _lin(x, W, b):
            return x @ W + b

        def _split_heads(x):
            return x.reshape(*x.shape[:-2], x.shape[-2], NH, D).swapaxes(-3, -2)

        def _merge_heads(x):
            return x.swapaxes(-3, -2).reshape(*x.shape[:-3], x.shape[-2], H)
        q = _split_heads(_lin(hidden_states, Wq, bq))
        k = _split_heads(_lin(hidden_states, Wk, bk))
        v = _split_heads(_lin(hidden_states, Wv, bv))
        scores = jnp.einsum('bhsd,bhtd->bhst', q, k) * SCALE
        attn = jax.nn.softmax(scores, axis=-1)
        ctx = jnp.einsum('bhst,bhtd->bhsd', attn, v)
        output = _lin(_merge_heads(ctx), Wo, bo)
        rq = _split_heads(_lin(output, Wrq, brq))
        rk = _split_heads(_lin(past_states, Wrk, brk))
        rv = _split_heads(_lin(past_states, Wrv, brv))
        rscores = jnp.einsum('bhsd,pbhtd->pbhst', rq, rk) * SCALE
        rattn = jax.nn.softmax(rscores, axis=-1)
        rctx = jnp.einsum('pbhst,pbhtd->pbhsd', rattn, rv)
        recursive_output = _merge_heads(rctx).mean(axis=0)
        gate = jax.nn.sigmoid(_lin(jnp.concatenate([output, recursive_output], axis=-1), Wg, bg))
        output = output * (1.0 - gate) + recursive_output * gate
        return output

    def _L1_xattn_ref(query, key, value, q_w, q_b, k_w, k_b, v_w, v_b, o_w, o_b):
        import jax, jax.numpy as jnp
        import numpy as np
        EMBED_DIM = 512
        NUM_HEADS = 16
        HEAD_DIM = EMBED_DIM // NUM_HEADS
        WINDOW = 64

        def apply_rope(x):
            B, H, S, d = x.shape
            half = d // 2
            pos = jnp.arange(S, dtype=x.dtype)
            freqs = 1.0 / 10000.0 ** (jnp.arange(half, dtype=x.dtype) / half)
            ang = pos[:, None] * freqs[None, :]
            cos, sin = (jnp.cos(ang), jnp.sin(ang))
            x1, x2 = (x[..., :half], x[..., half:])
            return jnp.concatenate([x1 * cos - x2 * sin, x1 * sin + x2 * cos], axis=-1)

        def _forward(query, key, value, q_w, q_b, k_w, k_b, v_w, v_b, o_w, o_b):
            B, S_q, D = query.shape
            S_k = key.shape[1]
            H, d, W = (NUM_HEADS, HEAD_DIM, WINDOW)
            q = (query @ q_w.T + q_b).reshape(B, S_q, H, d).transpose(0, 2, 1, 3)
            k = (key @ k_w.T + k_b).reshape(B, S_k, H, d).transpose(0, 2, 1, 3)
            v = (value @ v_w.T + v_b).reshape(B, S_k, H, d).transpose(0, 2, 1, 3)
            q = apply_rope(q) * d ** (-0.5)
            k = apply_rope(k)
            q_pos = jnp.arange(S_q)[:, None]
            offsets = jnp.arange(-W, 1)[None, :]
            idx = q_pos + offsets
            local_mask = (idx < 0) | (idx >= S_k)
            gidx = jnp.clip(idx, 0, S_k - 1)
            k_win = k[:, :, gidx, :]
            v_win = v[:, :, gidx, :]
            scores = jnp.einsum('bhqd,bhqwd->bhqw', q, k_win)
            mask = local_mask[None, None, :, :]
            scores = jnp.where(mask, -jnp.inf, scores)
            m = jnp.max(scores, axis=-1, keepdims=True)
            m = jnp.where(jnp.isfinite(m), m, 0.0)
            e = jnp.exp(scores - m)
            denom = jnp.sum(e, axis=-1, keepdims=True)
            probs = jnp.where(denom > 0, e / jnp.where(denom > 0, denom, 1.0), 0.0)
            ctx = jnp.einsum('bhqw,bhqwd->bhqd', probs, v_win)
            ctx = ctx.transpose(0, 2, 1, 3).reshape(B, S_q, D)
            return ctx @ o_w.T + o_b
        return _forward(query, key, value, q_w, q_b, k_w, k_b, v_w, v_b, o_w, o_b)

    def _L1_ffn_ref(x, router_w, router_b, w1, b1, w2, b2):
        import math
        import jax, jax.numpy as jnp
        import numpy as np
        D_MODEL = 512
        D_HIDDEN = 2048
        N_EXPERTS = 8
        TOP_K = 2
        CAPACITY_FACTOR = 1.25
        B, T, D = x.shape
        N = B * T
        E = N_EXPERTS
        capacity = max(1, math.ceil(N / E * CAPACITY_FACTOR))
        x_flat = x.reshape(N, D)
        logits = x_flat.astype(jnp.float32) @ router_w + router_b
        gates = jax.nn.softmax(logits, axis=-1)
        _, topk_idx = jax.lax.top_k(gates, TOP_K)
        expert_mask = jax.nn.one_hot(topk_idx, E, dtype=jnp.int32).sum(1)
        pos = jnp.cumsum(expert_mask, axis=0) - 1
        expert_mask = expert_mask * (pos < capacity)
        valid = expert_mask > 0
        pos_c = jnp.where(valid, pos, capacity)
        e_idx = jnp.broadcast_to(jnp.arange(E), (N, E))
        dispatched = x_flat[:, None, :] * valid[:, :, None].astype(x.dtype)
        buf = jnp.zeros((E, capacity + 1, D), x.dtype).at[e_idx.ravel(), pos_c.ravel()].add(dispatched.reshape(N * E, D))
        buf = buf[:, :capacity]
        h = jax.nn.gelu(jnp.einsum('ecd,edh->ech', buf, w1) + b1[:, None, :], approximate=False)
        out = jnp.einsum('ech,ehd->ecd', h, w2) + b2[:, None, :]
        pos_g = jnp.minimum(pos_c, capacity - 1)
        gathered = out[e_idx, pos_g]
        weights = (gates * valid).astype(x.dtype)
        y = jnp.einsum('ned,ne->nd', gathered, weights)
        return y.reshape(B, T, D)
    x = _layernorm(x + _L0_attn_ref(x, L0_attn_w_qkv, L0_attn_w_proj, L0_attn_b_proj, L0_attn_rpe_q_table, L0_attn_rpe_k_table, L0_attn_rpe_v_table), axis=-1)
    x = _layernorm(x + _L0_xattn_ref(ctx_1024, ctx_1024, x, L0_xattn_Wv, L0_xattn_Wk, L0_xattn_Wq, L0_xattn_Wo, L0_xattn_bo), axis=-1)
    x = _layernorm(x + _L0_ffn_ref(x, L0_ffn_w_g, L0_ffn_c_fc, L0_ffn_c_proj), axis=-1)
    x = _layernorm(x + _L1_attn_ref(x, L1_attn_past_states, L1_attn_Wq, L1_attn_bq, L1_attn_Wk, L1_attn_bk, L1_attn_Wv, L1_attn_bv, L1_attn_Wo, L1_attn_bo, L1_attn_Wrq, L1_attn_brq, L1_attn_Wrk, L1_attn_brk, L1_attn_Wrv, L1_attn_brv, L1_attn_Wg, L1_attn_bg), axis=-1)
    x = _layernorm(x + _L1_xattn_ref(x, ctx_1024, ctx_1024, L1_xattn_q_w, L1_xattn_q_b, L1_xattn_k_w, L1_xattn_k_b, L1_xattn_v_w, L1_xattn_v_b, L1_xattn_o_w, L1_xattn_o_b), axis=-1)
    x = _layernorm(x + _L1_ffn_ref(x, L1_ffn_router_w, L1_ffn_router_b, L1_ffn_w1, L1_ffn_b1, L1_ffn_w2, L1_ffn_b2), axis=-1)
    return x

_drawn_inputs = setup_inputs


def setup_inputs(seed=0):
    import zlib

    import numpy as np

    out = dict(_drawn_inputs(seed))
    spreads = {'L0_attn_b_proj': (0.0, 0.1),
     'L0_xattn_bo': (0.0, 0.1),
     'L1_attn_bq': (0.0, 0.8),
     'L1_attn_bk': (0.0, 2.0),
     'L1_attn_bv': (0.0, 0.363),
     'L1_attn_bo': (0.0, 0.1),
     'L1_attn_brq': (0.0, 0.8),
     'L1_attn_brk': (0.0, 2.0),
     'L1_attn_brv': (0.0, 0.427),
     'L1_attn_bg': (0.0, 0.8),
     'L1_ffn_router_b': (0.0, 0.1),
     'L1_ffn_b1': (0.0, 0.673),
     'L1_ffn_b2': (0.0, 0.369)}
    factors = {'L0_attn_rpe_q_table': 4.94,
     'L0_attn_rpe_k_table': 8.0,
     'L0_attn_rpe_v_table': 3.207,
     'L1_attn_past_states': 8.0,
     'L1_attn_Wq': 8.0,
     'L1_attn_Wk': 8.0,
     'L1_attn_Wrq': 8.0,
     'L1_attn_Wrk': 8.0,
     'L1_attn_Wrv': 8.0,
     'L1_attn_Wg': 8.0,
     'L1_xattn_q_b': 21.603,
     'L1_xattn_k_b': 32.337,
     'L1_xattn_v_b': 6.256,
     'L1_xattn_o_b': 5.607}
    for name, (base, spread) in spreads.items():
        noise = np.random.default_rng([zlib.crc32(name.encode()), seed]).standard_normal(out[name].shape)
        drawn = base * np.exp(spread * noise) if base else spread * noise
        out[name] = jnp.asarray(drawn.astype(out[name].dtype))
    for name, factor in factors.items():
        out[name] = (out[name] * factor).astype(out[name].dtype)
    return out
```

```python
import concourse.bass as bass
from concourse import mybir
from concourse.alu_op_type import AluOpType as ALU
from contextlib import ExitStack
import numpy as np

FP32 = mybir.dt.float32
U32 = mybir.dt.uint32
ACT = mybir.ActivationFunctionType
X = mybir.AxisListType.X

B, T, D = 8, 224, 512
NTOK = B * T
H, HD = 16, 32
HG = 4
TP = 112
NA = T // TP
C = D // 128
CTXN = 750
PASTN = 1024
NE, FF = 8, 2048
CAP0, CAP1 = 560, 280
EPS = 1e-5
HALF = 31
NBUCK = 2 * HALF + 1
PADW = T + 2 * HALF
NEG = -1.0e30


class Event:

    def __init__(self, sem, per, primed=True):
        self.sem, self.per, self.primed = sem, per, primed

    def now(self, it, k):
        return (it + self.primed) * self.per + k

    def before(self, it, k=None):
        return it * self.per + (self.per if k is None else k)

    def end(self, steps):
        return (steps + self.primed) * self.per


class Chain:

    def __init__(self, eng, sem, it, per):
        self.eng, self.sem, self.it, self.per, self.n = eng, sem, it, per, 0

    def done(self, ins):
        ins.then_inc(self.sem, 1)
        self.n += 1

    def last(self):
        return self.it * self.per + self.n

    def close(self):
        assert self.n == self.per, (self.n, self.per)


class Room:

    def __init__(self, nc, ctx, stage):
        self.nc, self.ctx, self.stage, self.sems = nc, ctx, stage, []
        ctx.callback(self.leave)

    def sb(self, name, shape, dt=FP32):
        return self.ctx.enter_context(self.nc.sbuf_tensor(f"{self.stage}_{name}", shape, dt))

    def ps(self, name, shape, dt=FP32):
        return self.ctx.enter_context(self.nc.psum_tensor(f"{self.stage}_{name}", shape, dt))

    def sem(self, name):
        self.sems.append(self.nc.alloc_semaphore(name=f"{self.stage}_{name}"))
        return self.sems[-1]

    def leave(self):
        self.nc.clear_and_free_semaphores(self.sems)
        self.nc.all_engine_barrier()

    def event(self, name, per, primed=True):
        return Event(self.sem(name), max(per, 1), primed)


def chunked(w):
    return w.rearrange("(c p) n -> p c n", p=min(128, w.shape[0]))


def rows_of(b, parts):
    return b.rearrange("(o n) -> o n", o=1).broadcast_to([parts, b.shape[0]])


def token_stage(nc, stage, steps, n, tk, cols, consts, xT=None, zs=None, wz=None, bz=None,
                gate=False, res=None, norm=False, y_out=None, y_in=None, fm=(), tm=()):
    nt, ncol = n // tk, n // cols
    nz = 0 if zs is None else (2 if gate else 1)
    jobs = [("tpz", z, a) for z in range(nz) for a in range(nt)]
    if nz:
        jobs += [("lin", 0, a) for a in range(nt)]
    if xT is None:
        jobs += [("tpy", 0, a) for a in range(nt)]
    jobs += [("fm", w, (c, s)) for c in range(C) for w in range(len(fm)) for s in range(ncol)]
    jobs += [("tm", w, a) for w in range(len(tm)) for a in range(nt)]
    if not fm and not tm:
        jobs = [j for j in jobs if j[0] != "tpy"]
    NJ = len(jobs)
    RING = min(6, NJ)
    on_act = [j[0] in ("tpz", "tpy") or (j[0] == "tm" and tm[j[1]][1] is None) for j in jobs]
    place = {j: i for i, j in enumerate(jobs)}

    def nth(m):
        return sum(1 for k in range(m + 1) if on_act[k] == on_act[m])

    with ExitStack() as ctx:
        r = Room(nc, ctx, stage)
        ident = r.sb("ident", [128, 128])
        nload = len(zs) if nz else 0
        z_sb = [r.sb(f"z{i}", [tk, nt, D]) for i in range(nload)]
        zT = [r.sb(f"zT{i}", [128, C, n]) for i in range(nz)]
        wz_sb = r.sb("wz", [128, C * nz, D]) if nz else None
        bz_sb = r.sb("bz", [tk, D]) if nz else None
        res_sb = r.sb("res", [tk, nt, D]) if res is not None else None
        y = r.sb("y", [tk, nt, D]) if xT is None else None
        t = r.sb("t", [tk, nt, D]) if nz else None
        stats, mv = r.sb("stats", [tk, nt, 6]), r.sb("mv", [tk, nt, 2])
        std, rstd, eps = r.sb("std", [tk, nt]), r.sb("rstd", [tk, nt]), r.sb("eps", [128, 1])
        yT = r.sb("yT", [128, C, n])
        fm_w = [r.sb(f"fw{i}", [128, f[0].shape[0] // 128, f[0].shape[1]]) for i, f in enumerate(fm)]
        fm_b = [r.sb(f"fb{i}", [128, C]) if f[1] is not None else None for i, f in enumerate(fm)]
        fm_o = [r.sb(f"fo{i}", [128, C, n]) for i, f in enumerate(fm)]
        tm_w = [r.sb(f"tw{i}", [128, f[0].shape[0] // 128, f[0].shape[1]]) for i, f in enumerate(tm)]
        tm_b = [r.sb(f"tb{i}", [tk, f[2]]) if f[1] is not None else None for i, f in enumerate(tm)]
        tm_o = [r.sb(f"to{i}", [tk, nt, f[2]]) for i, f in enumerate(tm)]
        roped = [i for i, f in enumerate(fm) if f[3] == 2]
        if roped:
            trig = [r.sb(f"trig{i}", [128, n]) for i in range(2)]
        ring = [r.ps(f"ring{i}", [128, 512]) for i in range(RING)]

        stored_fm = [i for i, f in enumerate(fm) if f[4] is not None]
        w_loaded, eps_set = r.sem("w_loaded"), r.sem("eps_set")
        z_loaded = r.event("z_loaded", 16 * nload * nt)
        res_loaded = r.event("res_loaded", 16)
        src_loaded = r.event("src_loaded", 16)
        mm_done = r.event("mm_done", NJ)
        act_out = r.event("act_out", sum(on_act))
        dve_out = r.event("dve_out", NJ - sum(on_act))
        y_ready = r.event("y_ready", nt)
        var_ready, std_ready = r.event("var_ready", nt), r.event("std_ready", 1)
        mean_ready = r.event("mean_ready", nt)
        gate_ready = r.event("gate_ready", nt)
        rope_ready = r.event("rope_ready", C * len(roped))
        y_stored = r.event("y_stored", 16, False)
        fm_stored = r.event("fm_stored", 16 * len(stored_fm), False)
        tm_stored = r.event("tm_stored", 16 * len(tm) * nt, False)
        y_free, fm_free, tm_free = (r.event(s, 1) for s in ("y_free", "fm_free", "tm_free"))
        dve_step = r.sem("dve_step")
        block = ctx.enter_context(nc.Block())
        out_of = lambda m: act_out if on_act[m] else dve_out

        fixed = [(ident[:, :], consts["ident"])]
        if nz:
            fixed += [(wz_sb[:, :, :], chunked(wz)), (bz_sb[:, :], rows_of(bz, tk))]
        for i, f in enumerate(fm):
            fixed.append((fm_w[i][:, :, :], chunked(f[0])))
            if f[1] is not None:
                fixed.append((fm_b[i][:, :], f[1].rearrange("(p c) -> p c", p=128)))
        for i, f in enumerate(tm):
            fixed.append((tm_w[i][:, :, :], chunked(f[0])))
            if f[1] is not None:
                fixed.append((tm_b[i][:, :], rows_of(f[1], tk)))
        if roped:
            fixed += [(trig[k][:, :], fm[roped[0]][2][k]) for k in range(2)]

        @block.sync
        def _(sp):
            for e in (z_loaded, res_loaded, src_loaded):
                sp.sem_inc(e.sem, e.per)
            for dst, src in fixed:
                sp.dma_start(dst, src).then_inc(w_loaded, 16)
            with sp.Fori(0, steps) as it:
                if nz:
                    sp.wait_ge(y_ready.sem, y_ready.before(it))
                    sp.nop(nofuse=True)
                    for i, src in enumerate(zs):
                        for a in range(nt):
                            sp.dma_start(z_sb[i][:, a, :].rearrange("p (g d) -> p g d", g=C) if src[0] else z_sb[i][:, a, :],
                                         src[1](it, a)).then_inc(z_loaded.sem, 16)
                if res is not None:
                    sp.wait_ge(y_ready.sem, y_ready.before(it))
                    sp.dma_start(res_sb[:, :, :], res(it)).then_inc(res_loaded.sem, 16)
                if y_in is not None:
                    sp.wait_ge(mm_done.sem, mm_done.before(it, place[("tpy", 0, nt - 1)] + 1))
                    sp.nop(nofuse=True)
                    sp.dma_start(y[:, :, :], y_in(it)).then_inc(src_loaded.sem, 16)
                if xT is not None:
                    sp.wait_ge(mm_done.sem, mm_done.before(it))
                    sp.nop(nofuse=True)
                    sp.dma_start(yT[:, :, :], xT(it)).then_inc(src_loaded.sem, 16)

        @block.gpsimd
        def _(pool):
            pool.memset(eps[:, :], EPS).then_inc(eps_set, 1)
            for e in (y_free, fm_free, tm_free):
                pool.sem_inc(e.sem, e.per)
            with pool.Fori(0, steps) as it:
                if y_out is not None:
                    pool.wait_ge(y_ready.sem, y_ready.now(it, nt))
                    pool.nop(nofuse=True)
                    pool.dma_start(y_out(it), y[:, :, :]).then_inc(y_stored.sem, 16)
                for i in stored_fm:
                    if i in roped:
                        pool.wait_ge(rope_ready.sem, rope_ready.now(it, rope_ready.per))
                        pool.nop(nofuse=True)
                    else:
                        m = place[("fm", i, (C - 1, ncol - 1))]
                        pool.wait_ge(dve_out.sem, dve_out.now(it, nth(m)))
                        pool.nop(nofuse=True)
                    pool.dma_start(fm[i][4](it), fm_o[i][:, :, :]).then_inc(fm_stored.sem, 16)
                for i in range(len(tm)):
                    for a in range(nt):
                        m = place[("tm", i, a)]
                        pool.wait_ge(out_of(m).sem, out_of(m).now(it, nth(m)))
                        src = tm_o[i][:, a, :]
                        if tm[i][2] == D:
                            src = src.rearrange("p (g d) -> p g d", g=C)
                        pool.dma_start(tm[i][3](it, a), src).then_inc(tm_stored.sem, 16)
                if y_out is not None:
                    pool.wait_ge(y_stored.sem, y_stored.now(it, 16))
                    pool.sem_inc(y_free.sem, 1)
                if stored_fm:
                    pool.wait_ge(fm_stored.sem, fm_stored.now(it, fm_stored.per))
                    pool.sem_inc(fm_free.sem, 1)
                if tm:
                    pool.wait_ge(tm_stored.sem, tm_stored.now(it, tm_stored.per))
                    pool.sem_inc(tm_free.sem, 1)

        @block.tensor
        def _(pe):
            pe.sem_inc(mm_done.sem, NJ)
            pe.wait_ge(w_loaded, 16 * len(fixed))
            with pe.Fori(0, steps) as it:
                for m, (kind, w, i) in enumerate(jobs):
                    bank = ring[m % RING]
                    if m >= RING:
                        e = out_of(m - RING)
                        pe.wait_ge(e.sem, e.now(it, nth(m - RING)))
                    else:
                        k = max(k for k in range(NJ) if k % RING == m)
                        e = out_of(k)
                        pe.wait_ge(e.sem, e.before(it, nth(k)))
                    if kind == "tpz":
                        if gate and w == 1:
                            pe.wait_ge(mean_ready.sem, mean_ready.now(it, i + 1))
                        else:
                            pe.wait_ge(z_loaded.sem, z_loaded.now(it, z_loaded.per))
                        for c in range(C):
                            ins = nc.tensor.transpose(bank[:, c * tk:(c + 1) * tk],
                                                      z_sb[w][:, i, c * 128:(c + 1) * 128], ident[:tk, :tk])
                    elif kind == "lin":
                        pe.wait_ge(act_out.sem, act_out.now(it, nth(place[("tpz", nz - 1, i)])))
                        for k in range(C * nz):
                            ins = nc.tensor.matmul(bank[:tk, :], zT[k // C][:, k % C, i * tk:(i + 1) * tk],
                                                   wz_sb[:, k, :], start=(k == 0), stop=(k == C * nz - 1))
                    elif kind == "tpy":
                        if y_in is not None:
                            pe.wait_ge(src_loaded.sem, src_loaded.now(it, 16))
                        else:
                            pe.wait_ge(y_ready.sem, y_ready.now(it, i + 1))
                        for c in range(C):
                            ins = nc.tensor.transpose(bank[:, c * tk:(c + 1) * tk],
                                                      y[:, i, c * 128:(c + 1) * 128], ident[:tk, :tk])
                    else:
                        if xT is not None:
                            pe.wait_ge(src_loaded.sem, src_loaded.now(it, 16))
                        else:
                            pe.wait_ge(act_out.sem, act_out.now(it, nth(place[("tpy", 0, nt - 1)])))
                        if kind == "fm":
                            c, s = i
                            whole = fm[w][0].shape[0] == D
                            for k in range(C) if whole else [c]:
                                lhsT = fm_w[w][:, k, c * 128:(c + 1) * 128] if whole else fm_w[w][:, 0, :]
                                ins = nc.tensor.matmul(bank[:, :cols], lhsT, yT[:, k, s * cols:(s + 1) * cols],
                                                       start=(k == 0 or not whole), stop=(k == C - 1 or not whole))
                        elif tm[w][0].shape[0] == 128:
                            for k in range(C):
                                ins = nc.tensor.matmul(bank[:tk, k * 128:(k + 1) * 128],
                                                       yT[:, k, i * tk:(i + 1) * tk], tm_w[w][:, 0, :],
                                                       start=True, stop=True)
                        else:
                            for k in range(C):
                                ins = nc.tensor.matmul(bank[:tk, :tm[w][2]], yT[:, k, i * tk:(i + 1) * tk],
                                                       tm_w[w][:, k, :], start=(k == 0), stop=(k == C - 1))
                    ins.then_inc(mm_done.sem, 1)

        @block.scalar
        def _(act):
            for e in (act_out, std_ready, gate_ready):
                act.sem_inc(e.sem, e.per)
            act.wait_ge(eps_set, 1)
            with act.Fori(0, steps) as it:
                for m, (kind, w, i) in enumerate(jobs):
                    bank = ring[m % RING]
                    if kind in ("tpz", "tpy"):
                        act.wait_ge(mm_done.sem, mm_done.now(it, m + 1))
                        dst = zT[w] if kind == "tpz" else yT
                        nc.scalar.activation(dst[:, :, i * tk:(i + 1) * tk],
                                             bank[:, :C * tk].rearrange("p (c t) -> p c t", c=C),
                                             ACT.Copy).then_inc(act_out.sem, 1)
                    elif on_act[m]:
                        if i == 0:
                            act.wait_ge(tm_free.sem, tm_free.before(it))
                        act.wait_ge(mm_done.sem, mm_done.now(it, m + 1))
                        nc.scalar.activation(tm_o[w][:, i, :], bank[:tk, :tm[w][2]],
                                             ACT.Copy).then_inc(act_out.sem, 1)
                    elif kind == "lin" and gate:
                        act.wait_ge(dve_out.sem, dve_out.now(it, nth(m)))
                        nc.scalar.activation(t[:, i, :], t[:, i, :], ACT.Sigmoid).then_inc(gate_ready.sem, 1)
                    if norm and kind == "lin" and i == nt - 1:
                        act.wait_ge(var_ready.sem, var_ready.now(it, nt))
                        nc.scalar.activation(std[:, :], mv[:, :, 1], ACT.Sqrt, bias=eps[:tk, :]).then_inc(std_ready.sem, 1)

        per = (nt if gate else 0) + (3 * nt if gate else 0) + (nt if res is not None else 0) \
            + (nt + 1 if norm else 0)

        @block.vector
        def _(dve):
            for e in (dve_out, y_ready, var_ready, mean_ready, rope_ready):
                dve.sem_inc(e.sem, e.per)
            dve.wait_ge(w_loaded, 16 * len(fixed))
            with dve.Fori(0, steps) as it:
                own = Chain(dve, dve_step, it, per)
                if gate:
                    dve.wait_ge(z_loaded.sem, z_loaded.now(it, z_loaded.per))
                    for a in range(nt):
                        own.done(nc.vector.tensor_tensor(z_sb[1][:, a, :], z_sb[1][:, a, :], z_sb[2][:, a, :], ALU.add))
                    for a in range(nt):
                        dve.wait_ge(dve_step, own.it * own.per + a + 1)
                        nc.vector.tensor_scalar(z_sb[1][:, a, :], z_sb[1][:, a, :], 0.5, None,
                                                ALU.mult).then_inc(mean_ready.sem, 1)
                for m, (kind, w, i) in enumerate(jobs):
                    if on_act[m]:
                        continue
                    bank = ring[m % RING]
                    dve.wait_ge(mm_done.sem, mm_done.now(it, m + 1))
                    if kind == "lin":
                        nc.vector.tensor_tensor(t[:, i, :], bank[:tk, :], bz_sb[:, :], ALU.add).then_inc(dve_out.sem, 1)
                        if i == 0:
                            if y_out is not None:
                                dve.wait_ge(y_free.sem, y_free.before(it))
                            if res is not None:
                                dve.wait_ge(res_loaded.sem, res_loaded.now(it, 16))
                        if gate:
                            if i == 0:
                                dve.wait_ge(mean_ready.sem, mean_ready.now(it, nt))
                            own.done(nc.vector.tensor_tensor(y[:, i, :], z_sb[1][:, i, :], z_sb[0][:, i, :], ALU.subtract))
                            dve.wait_ge(gate_ready.sem, gate_ready.now(it, i + 1))
                            dve.wait_ge(dve_step, own.last())
                            own.done(nc.vector.tensor_tensor(t[:, i, :], y[:, i, :], t[:, i, :], ALU.mult))
                            dve.wait_ge(dve_step, own.last())
                            own.done(nc.vector.tensor_tensor(t[:, i, :], t[:, i, :], z_sb[0][:, i, :], ALU.add))
                            dve.wait_ge(dve_step, own.last())
                        else:
                            dve.wait_ge(dve_out.sem, dve_out.now(it, nth(m)))
                        if res is not None:
                            own.done(nc.vector.tensor_tensor(t[:, i, :], t[:, i, :], res_sb[:, i, :], ALU.add))
                            dve.wait_ge(dve_step, own.last())
                        if norm:
                            own.done(nc.vector.bn_stats(stats[:, i, :], t[:, i, :]))
                            dve.wait_ge(dve_step, own.last())
                            dve.nop(nofuse=True)
                            nc.vector.bn_aggr(mv[:, i, :], stats[:, i, :]).then_inc(var_ready.sem, 1)
                        else:
                            nc.vector.tensor_copy(y[:, i, :], t[:, i, :]).then_inc(y_ready.sem, 1)
                        if norm and i == nt - 1:
                            dve.wait_ge(std_ready.sem, std_ready.now(it, 1))
                            own.done(nc.vector.reciprocal(rstd[:, :], std[:, :]))
                            dve.wait_ge(dve_step, own.last())
                            for a in range(nt):
                                nc.vector.tensor_scalar(y[:, a, :], t[:, a, :], mv[:, a, 0:1], rstd[:, a:a + 1],
                                                        ALU.subtract, ALU.mult).then_inc(y_ready.sem, 1)
                    elif kind == "fm":
                        c, s = i
                        if c == 0 and s == 0 and w == 0 and stored_fm:
                            dve.wait_ge(fm_free.sem, fm_free.before(it))
                        dst = fm_o[w][:, c, s * cols:(s + 1) * cols]
                        if fm[w][3] is not None:
                            nc.vector.scalar_tensor_tensor(dst, bank[:, :cols], fm_b[w][:, c:c + 1],
                                                           trig[fm[w][3] - 1][:, :], ALU.add, ALU.mult).then_inc(dve_out.sem, 1)
                            if fm[w][3] == 2:
                                dve.wait_ge(dve_out.sem, dve_out.now(it, nth(m)))
                                nc.vector.tensor_tensor(dst, dst, fm_o[w - 1][:, c, :], ALU.add).then_inc(rope_ready.sem, 1)
                        elif fm[w][1] is not None:
                            nc.vector.tensor_scalar(dst, bank[:, :cols], fm_b[w][:, c:c + 1], fm[w][2],
                                                    ALU.add, ALU.mult).then_inc(dve_out.sem, 1)
                        else:
                            nc.vector.tensor_scalar(dst, bank[:, :cols], fm[w][2], None, ALU.mult).then_inc(dve_out.sem, 1)
                    else:
                        if i == 0 and w == 0:
                            dve.wait_ge(tm_free.sem, tm_free.before(it))
                        nc.vector.tensor_tensor(tm_o[w][:, i, :], bank[:tk, :tm[w][2]], tm_b[w][:, :],
                                                ALU.add).then_inc(dve_out.sem, 1)
                own.close()


def attention(nc, stage, npast, nk, kt, q, k, v, out, consts, shared=False, mask=None, rpe=None):
    ntk = nk // kt
    nb = 2 if ntk > 4 else 1
    ncb, tpb = nk // nb, ntk // nb
    units = [(u, h, a) for u in range(2) for h in range(4) for a in range(NA)]
    NU = len(units)
    add_bias = mask is not None or rpe is not None
    steps = npast * B * 2
    with ExitStack() as ctx:
        r = Room(nc, ctx, stage)
        ident = r.sb("ident", [128, 128])
        qT = [r.sb(f"qT{u}", [128, T]) for u in range(2)]
        kT = [r.sb(f"kT{u}", [128, nk]) for u in range(2)]
        vs = [r.sb(f"v{u}", [kt, ntk, 128]) for u in range(2)]
        if rpe:
            P = [r.sb(f"P{u}", [TP, NA, 4, nk]) for u in range(2)]
        else:
            P = [r.sb(f"P{i}", [TP, nk]) for i in range(2)]
        PT = [r.sb(f"PT{i}", [kt, ntk, TP]) for i in range(2)]
        Z = [r.sb(f"Z{i}", [TP, nk]) for i in range(2)] if add_bias else None
        nmax, sums, rinv = (r.sb(s, [TP, NU]) for s in ("nmax", "sums", "rinv"))
        o_sb = [r.sb(f"o{u}", [TP, NA, 128]) for u in range(2)]
        S = [r.ps(f"S{i}", [TP, nb, 512]) for i in range(2)]
        PTp = r.ps("PTp", [128, nb, 512])
        O = [r.ps(f"O{i}", [TP, 512]) for i in range(2)]
        if mask is not None:
            mask_sb = r.sb("mask", [TP, NA, nk])
        if rpe:
            tabs_dram, tabv_dram, bands, pband = rpe
            tab = [[r.sb(f"tab{u}{s}", [128, 256]) for s in range(2)] for u in range(2)]
            tabv = [r.sb(f"tabv{u}", [NBUCK, 128]) for u in range(2)]
            far = r.sb("far", [TP, 2, NA, T])
            zero = r.sb("zero", [TP, 2, 287])
            L = [[r.sb(f"L{u}{s}", [TP, NA, 4, 64]) for s in range(2)] for u in range(2)]
            Bias = [[r.sb(f"B{u}{s}", [TP, NA, 4, T]) for s in range(2)] for u in range(2)]
            Bd = [r.sb(f"Bd{u}", [TP, NA, 4, 64]) for u in range(2)]
            bT = [r.sb(f"bT{i}", [64, 4, TP]) for i in range(2)]
            junk = r.sb("junk", [TP, 4, T])
            Lp = [r.ps(f"Lp{i}", [TP, 512]) for i in range(2)]
            Vp = r.ps("Vp", [TP, 512])
        sides = [(u, s, a) for u in range(2) for s in range(2) for a in range(NA)]
        tails = [(u, a) for u in range(2) for a in range(NA)]

        fixed_loaded = r.sem("fixed_loaded")
        q_loaded, k_loaded, v_loaded = (r.event(s, 32) for s in ("q_loaded", "k_loaded", "v_loaded"))
        q_loaded = [r.event(f"qk_loaded{u}", 32 + (32 if rpe else 0)) for u in range(2)]
        v_loaded = [r.event(f"v_loaded{u}", 16 + (16 if rpe else 0)) for u in range(2)]
        s_done = r.event("s_done", NU)
        max_done = r.event("max_done", NU)
        exp_done = r.event("exp_done", NU)
        pt_done = r.event("pt_done", NU)
        pt_act, pt_dve = r.event("pt_act", NU), r.event("pt_dve", NU)
        av_done = r.event("av_done", NU)
        o_done = r.event("o_done", NU)
        out_stored = r.event("out_stored", 32, False)
        out_free = r.event("out_free", 1)
        dve_step = r.sem("dve_step")
        if rpe:
            zeroed, zero_set = r.sem("zeroed"), r.sem("zero_set")
            l_done, l_out = r.event("l_done", 8), r.event("l_out", 8)
            band_stored = [r.event(f"band_stored{u}", 16 * 4, False) for u in range(2)]
            bias_loaded = r.event("bias_loaded", 16 * 8)
            bias_done = r.event("bias_done", 1)
            p_stored = [r.event(f"p_stored{u}", 16 * 2) for u in range(2)]
            pband_loaded = r.event("pband_loaded", 16 * 4)
            tail_done = r.event("tail_done", 4)
            bt_done, bt_out = r.event("bt_done", 4), r.event("bt_out", 4)
            v2_done, v2_out = r.event("v2_done", 4), r.event("v2_out", 4)
        final = v2_out if rpe else o_done
        fin_u = final.per // 2
        block = ctx.enter_context(nc.Block())
        nfixed = 1 + (mask is not None) + (rpe is not None)

        @block.sync
        def _(sp):
            sp.dma_start(ident[:, :], consts["ident"]).then_inc(fixed_loaded, 16)
            if mask is not None:
                sp.dma_start(mask_sb[:, :, :], mask).then_inc(fixed_loaded, 16)
            if rpe:
                sp.dma_start(far[:, :, :, :], consts["far"]).then_inc(fixed_loaded, 16)
                sp.wait_ge(zero_set, 1)
                for buf in [b for side in bands for b in side] + pband:
                    for h in range(4):
                        sp.dma_start(buf[h].rearrange("(p a w) -> p a w", p=TP, a=2), zero[:, :, :]).then_inc(zeroed, 16)
                sp.wait_ge(zeroed, 16 * 4 * 6)
                for e in [bias_loaded, pband_loaded] + p_stored:
                    sp.sem_inc(e.sem, e.per)
            for e in q_loaded + v_loaded:
                sp.sem_inc(e.sem, e.per)

            def step(it, pp, b, h2):
                for u in range(2):
                    g = b * HG + h2 * 2 + u
                    gk = pp * HG + h2 * 2 + u if shared else g
                    sp.wait_ge(av_done.sem, av_done.before(it, NU // 2 * (u + 1)))
                    sp.nop(nofuse=True)
                    sp.dma_start(qT[u][:, :], q[bass.ds(g * 128, 128), :]).then_inc(q_loaded[u].sem, 16)
                    sp.dma_start(kT[u][:, :], k[bass.ds(gk * 128, 128), :]).then_inc(q_loaded[u].sem, 16)
                    if rpe:
                        for s in range(2):
                            sp.dma_start(tab[u][s][:, :], tabs_dram[s][bass.ds((h2 * 2 + u) * 128, 128), :]).then_inc(q_loaded[u].sem, 16)
                        sp.wait_ge(v2_done.sem, v2_done.before(it, 2 * (u + 1)))
                        sp.nop(nofuse=True)
                        sp.dma_start(tabv[u][:, :], tabv_dram[bass.ds((h2 * 2 + u) * NBUCK, NBUCK), :]).then_inc(v_loaded[u].sem, 16)
                    sp.dma_start(vs[u][:, :, :], v[bass.ds(gk, 1), :, :].rearrange("o (t p) d -> p (o t) d", p=kt)).then_inc(v_loaded[u].sem, 16)
                if rpe:
                    for j, (u, s, a) in enumerate(sides):
                        sp.wait_ge(band_stored[u].sem, band_stored[u].now(it, 64))
                        sp.wait_ge(o_done.sem, o_done.before(it))
                        sp.nop(nofuse=True)
                        for_rows = bands[u][s][:, 0:T * PADW].rearrange("h (i w) -> i h w", w=PADW)
                        sp.dma_start(Bias[u][s][:, a, :, :], for_rows[a * TP:(a + 1) * TP, :, HALF:HALF + T]).then_inc(bias_loaded.sem, 16)
                    for j, (u, a) in enumerate(tails):
                        sp.wait_ge(exp_done.sem, exp_done.now(it, NU // 2 * (u + 1)))
                        sp.nop(nofuse=True)
                        rows = pband[u][:, 0:T * PADW].rearrange("h (i w) -> i h w", w=PADW)
                        sp.dma_start(rows[a * TP:(a + 1) * TP, :, HALF:HALF + T], P[u][:, a, :, :]).then_inc(p_stored[u].sem, 16)
                    for j, (u, a) in enumerate(tails):
                        sp.wait_ge(p_stored[u].sem, p_stored[u].now(it, 32))
                        sp.nop(nofuse=True)
                        diag = pband[u][:, :].rearrange("h (i w) -> i h w", w=PADW + 1)
                        sp.wait_ge(bt_done.sem, bt_done.before(it, j + 1))
                        sp.nop(nofuse=True)
                        sp.dma_start(Bd[u][:, a, :, 0:NBUCK], diag[a * TP:(a + 1) * TP, :, 0:NBUCK]).then_inc(pband_loaded.sem, 16)

            if npast > 1:
                with sp.Fori(0, npast) as pp:
                    with sp.Fori(0, B) as b:
                        with sp.Fori(0, 2) as h2:
                            step(pp * (2 * B) + b * 2 + h2, pp, b, h2)
            else:
                with sp.Fori(0, B) as b:
                    with sp.Fori(0, 2) as h2:
                        step(b * 2 + h2, 0, b, h2)

        @block.gpsimd
        def _(pool):
            if rpe:
                pool.memset(zero[:, :, :], 0.0).then_inc(zero_set, 1)
                pool.wait_ge(zeroed, 16 * 4 * 6)
            pool.sem_inc(out_free.sem, 1)

            with pool.Fori(0, steps) as it:
                if rpe:
                    pool.wait_ge(bias_loaded.sem, bias_loaded.before(it))
                    pool.nop(nofuse=True)
                    for j, (u, s, a) in enumerate(sides):
                        pool.wait_ge(l_out.sem, l_out.now(it, j + 1))
                        pool.nop(nofuse=True)
                        diag = bands[u][s][:, :].rearrange("h (i w) -> i h w", w=PADW + 1)
                        pool.dma_start(diag[a * TP:(a + 1) * TP, :, 0:NBUCK], L[u][s][:, a, :, 0:NBUCK]).then_inc(band_stored[u].sem, 16)
                for u in range(2):
                    pool.wait_ge(final.sem, final.now(it, fin_u * (u + 1)))
                    pool.nop(nofuse=True)
                    pool.dma_start(out[bass.ds(it * 2 + u, 1), :, :].rearrange("o (a p) d -> p (o a) d", p=TP),
                                   o_sb[u][:, :, :]).then_inc(out_stored.sem, 16)
                pool.wait_ge(out_stored.sem, out_stored.now(it, 32))
                pool.sem_inc(out_free.sem, 1)

        @block.tensor
        def _(pe):
            for e in (s_done, pt_done, av_done) + ((l_done, bt_done, v2_done) if rpe else ()):
                pe.sem_inc(e.sem, e.per)
            pe.wait_ge(fixed_loaded, 16 * nfixed)

            def scores(it, n):
                u, h, a = units[n]
                if n % 8 == 0:
                    pe.wait_ge(q_loaded[u].sem, q_loaded[u].now(it, q_loaded[u].per))
                if rpe and n == 0:
                    pe.wait_ge(bias_done.sem, bias_done.now(it, 1))
                if n >= 2:
                    pe.wait_ge(exp_done.sem, exp_done.now(it, n - 1))
                else:
                    pe.wait_ge(exp_done.sem, exp_done.before(it, NU - 1 + n))
                rows = slice(32 * h, 32 * h + 32)
                for s in range(nb):
                    ins = nc.tensor.matmul(S[n % 2][:, s, 0:ncb], qT[u][rows, a * TP:(a + 1) * TP],
                                           kT[u][rows, s * ncb:(s + 1) * ncb], start=True, stop=not rpe,
                                           skip_group_check=bool(rpe))
                if rpe:
                    for t in range(NA):
                        ins = nc.tensor.matmul(S[n % 2][:, 0, t * TP:(t + 1) * TP], Bias[u][1][:, t, h, a * TP:(a + 1) * TP],
                                               ident[:TP, :TP], start=False, stop=(t == NA - 1), skip_group_check=True)
                ins.then_inc(s_done.sem, 1)

            def transposes(it, n):
                u, h, a = units[n]
                pe.wait_ge(exp_done.sem, exp_done.now(it, n + 1))
                e_act = pt_act.now(it, n) if n else pt_act.before(it)
                e_dve = pt_dve.now(it, n) if n else pt_dve.before(it)
                pe.wait_ge(pt_act.sem, e_act)
                if nb == 2:
                    pe.wait_ge(pt_dve.sem, e_dve)
                src = P[u][:, a, h, :] if rpe else P[n % 2]
                for t in range(ntk):
                    ins = nc.tensor.transpose(PTp[:kt, t // tpb, (t % tpb) * TP:(t % tpb + 1) * TP],
                                              src[:, t * kt:(t + 1) * kt], ident[:TP, :TP])
                ins.then_inc(pt_done.sem, 1)

            def values(it, n):
                u, h, a = units[n]
                if n % 8 == 0:
                    pe.wait_ge(v_loaded[u].sem, v_loaded[u].now(it, v_loaded[u].per))
                pe.wait_ge(pt_act.sem, pt_act.now(it, n + 1))
                if nb == 2:
                    pe.wait_ge(pt_dve.sem, pt_dve.now(it, n + 1))
                pe.wait_ge(o_done.sem, o_done.now(it, n - 1) if n >= 2 else o_done.before(it, NU - 1 + n))
                for t in range(ntk):
                    ins = nc.tensor.matmul(O[n % 2][:, 0:HD], PT[n % 2][:, t, :], vs[u][:, t, h * HD:(h + 1) * HD],
                                           start=(t == 0), stop=(t == ntk - 1))
                ins.then_inc(av_done.sem, 1)

            with pe.Fori(0, steps) as it:
                if rpe:
                    for j, (u, s, a) in enumerate(sides):
                        if j % 4 == 0:
                            pe.wait_ge(q_loaded[u].sem, q_loaded[u].now(it, q_loaded[u].per))
                        if j >= 2:
                            pe.wait_ge(l_out.sem, l_out.now(it, j - 1))
                        else:
                            pe.wait_ge(bt_out.sem, bt_out.before(it, 3 + j))
                        nc.tensor.matmul(Lp[j % 2][:, 0:256], (qT, kT)[s][u][:, a * TP:(a + 1) * TP], tab[u][s][:, :],
                                         start=True, stop=True).then_inc(l_done.sem, 1)
                scores(it, 0)
                scores(it, 1)
                for n in range(NU):
                    transposes(it, n)
                    if n + 2 < NU:
                        scores(it, n + 2)
                    values(it, n)
                if rpe:
                    for j, (u, a) in enumerate(tails):
                        pe.wait_ge(tail_done.sem, tail_done.now(it, j + 1))
                        pe.wait_ge(l_out.sem, l_out.now(it, 8)) if j < 2 else pe.wait_ge(bt_out.sem, bt_out.now(it, j - 1))
                        pe.nop(nofuse=True)
                        for h in range(4):
                            ins = nc.tensor.transpose(Lp[j % 2][:NBUCK, h * TP:(h + 1) * TP], Bd[u][:, a, h, 0:NBUCK], ident[:TP, :TP])
                        ins.then_inc(bt_done.sem, 1)
                        pe.wait_ge(bt_out.sem, bt_out.now(it, j + 1))
                        pe.wait_ge(v2_out.sem, v2_out.now(it, j) if j else v2_out.before(it))
                        for h in range(4):
                            ins = nc.tensor.matmul(Vp[:, h * HD:(h + 1) * HD], bT[j % 2][:NBUCK, h, :],
                                                   tabv[u][:, h * HD:(h + 1) * HD], start=True, stop=True)
                        ins.then_inc(v2_done.sem, 1)

        @block.scalar
        def _(act):
            for e in (exp_done, pt_act) + ((l_out, bt_out) if rpe else ()):
                act.sem_inc(e.sem, e.per)

            def exponential(it, n):
                u, h, a = units[n]
                act.wait_ge(max_done.sem, max_done.now(it, n + 1))
                if rpe:
                    if n == 0:
                        for e in p_stored:
                            act.wait_ge(e.sem, e.before(it))
                        act.wait_ge(tail_done.sem, tail_done.before(it))
                    dst, src = P[u][:, a, h, :], Z[n % 2][:, :]
                else:
                    act.wait_ge(pt_done.sem, pt_done.now(it, n - 1) if n >= 2 else pt_done.before(it, NU - 1 + n))
                    dst = P[n % 2][:, :].rearrange("p (s c) -> p s c", s=nb)
                    src = Z[n % 2][:, :].rearrange("p (s c) -> p s c", s=nb) if add_bias else S[n % 2][:, :, 0:ncb]
                if n == 0:
                    act.wait_ge(o_done.sem, o_done.before(it))
                nc.scalar.activation(dst, src, ACT.Exp, bias=nmax[:, n:n + 1],
                                     accum_out=sums[:, n:n + 1]).then_inc(exp_done.sem, 1)

            with act.Fori(0, steps) as it:
                if rpe:
                    for j, (u, s, a) in enumerate(sides):
                        act.wait_ge(l_done.sem, l_done.now(it, j + 1))
                        if j == 0:
                            act.wait_ge(bias_done.sem, bias_done.before(it))
                        nc.scalar.activation(L[u][s][:, a, :, 0:NBUCK],
                                             Lp[j % 2][:, 0:256].rearrange("p (h m) -> p h m", h=4)[:, :, 0:NBUCK],
                                             ACT.Copy, scale=1.0 if s == 0 else float(HD ** -0.5)).then_inc(l_out.sem, 1)
                exponential(it, 0)
                exponential(it, 1)
                for n in range(NU):
                    act.wait_ge(pt_done.sem, pt_done.now(it, n + 1))
                    act.wait_ge(av_done.sem, av_done.now(it, n - 1) if n >= 2 else av_done.before(it, NU - 1 + n))
                    nc.scalar.activation(PT[n % 2][:, 0:tpb, :], PTp[:kt, 0, 0:tpb * TP].rearrange("p (t c) -> p t c", t=tpb),
                                         ACT.Copy).then_inc(pt_act.sem, 1)
                    if n + 2 < NU:
                        exponential(it, n + 2)
                if rpe:
                    for j, (u, a) in enumerate(tails):
                        act.wait_ge(bt_done.sem, bt_done.now(it, j + 1))
                        act.wait_ge(v2_done.sem, v2_done.now(it, j - 1) if j >= 2 else v2_done.before(it, 3 + j))
                        nc.scalar.activation(bT[j % 2][:NBUCK, :, :], Lp[j % 2][:NBUCK, 0:4 * TP].rearrange("p (h c) -> p h c", h=4),
                                             ACT.Copy).then_inc(bt_out.sem, 1)

        per = NU * (2 if add_bias else 1) + (64 + 32 + 12 if rpe else 0)

        @block.vector
        def _(dve):
            for e in (max_done, pt_dve, o_done) + ((bias_done, tail_done, v2_out) if rpe else ()):
                dve.sem_inc(e.sem, e.per)
            dve.wait_ge(fixed_loaded, 16 * nfixed)

            def maximum(it, own, n):
                u, h, a = units[n]
                dve.wait_ge(s_done.sem, s_done.now(it, n + 1))
                dve.wait_ge(exp_done.sem, exp_done.now(it, n - 1) if n >= 2 else exp_done.before(it, NU - 1 + n))
                if add_bias:
                    bias = mask_sb[:, a, :] if mask is not None else Bias[u][0][:, a, h, :]
                    own.done(nc.vector.tensor_tensor(Z[n % 2][:, :], S[n % 2][:, 0, 0:nk], bias, ALU.add))
                    dve.wait_ge(dve_step, own.last())
                    src = Z[n % 2][:, :]
                    nc.vector.tensor_reduce(nmax[:, n:n + 1], src, X, ALU.max, negate=True).then_inc(max_done.sem, 1)
                else:
                    nc.vector.tensor_reduce(nmax[:, n:n + 1], S[n % 2][:, :, 0:ncb], mybir.AxisListType.XY, ALU.max,
                                            negate=True).then_inc(max_done.sem, 1)

            beyond = [[(0, TP - HALF), (0, T - HALF)], [(HALF, T), (TP + HALF, T)]]

            with dve.Fori(0, steps) as it:
                own = Chain(dve, dve_step, it, per)
                if rpe:
                    dve.wait_ge(bias_loaded.sem, bias_loaded.now(it, bias_loaded.per))
                    dve.wait_ge(l_out.sem, l_out.now(it, 8))
                    for u, s, a in sides:
                        for h in range(4):
                            for w in range(2):
                                lo, hi = beyond[w][a]
                                m = w * (NBUCK - 1)
                                dst = Bias[u][s][:, a, h, lo:hi]
                                if w:
                                    dve.wait_ge(dve_step, own.last())
                                ins = nc.vector.scalar_tensor_tensor(dst, far[:, w, a, lo:hi], L[u][s][:, a, h, m:m + 1], dst,
                                                                     ALU.mult, ALU.add)
                                own.done(ins)
                    dve.wait_ge(dve_step, own.last())
                    dve.sem_inc(bias_done.sem, 1)
                maximum(it, own, 0)
                maximum(it, own, 1)
                for n in range(NU):
                    u, h, a = units[n]
                    if nb == 2:
                        dve.wait_ge(pt_done.sem, pt_done.now(it, n + 1))
                        dve.wait_ge(av_done.sem, av_done.now(it, n - 1) if n >= 2 else av_done.before(it, NU - 1 + n))
                        nc.vector.tensor_copy(PT[n % 2][:, tpb:, :], PTp[:kt, 1, 0:tpb * TP].rearrange("p (t c) -> p t c", t=tpb)).then_inc(pt_dve.sem, 1)
                    if n + 2 < NU:
                        maximum(it, own, n + 2)
                    dve.wait_ge(exp_done.sem, exp_done.now(it, n + 1))
                    if n == 0 and rpe:
                        dve.wait_ge(v2_out.sem, v2_out.before(it))
                    own.done(nc.vector.reciprocal(rinv[:, n:n + 1], sums[:, n:n + 1]))
                    if n % 8 == 0:
                        dve.wait_ge(out_free.sem, out_free.before(it))
                    dve.wait_ge(dve_step, own.last())
                    dve.wait_ge(av_done.sem, av_done.now(it, n + 1))
                    nc.vector.tensor_scalar(o_sb[u][:, a, h * HD:(h + 1) * HD], O[n % 2][:, 0:HD], rinv[:, n:n + 1], None,
                                            ALU.mult).then_inc(o_done.sem, 1)
                if rpe:
                    dve.wait_ge(pband_loaded.sem, pband_loaded.now(it, pband_loaded.per))
                    for j, (u, a) in enumerate(tails):
                        for h in range(4):
                            for w in range(2):
                                lo, hi = beyond[w][a]
                                m = w * (NBUCK - 1)
                                dve.wait_ge(dve_step, own.last() - 3)
                                ins = nc.vector.tensor_tensor_reduce(
                                    out=junk[:, own.n % 4, lo:hi], in0=P[u][:, a, h, lo:hi], in1=far[:, w, a, lo:hi], scale=1.0,
                                    scalar=Bd[u][:, a, h, m:m + 1], op0=ALU.mult, op1=ALU.add, accum_out=Bd[u][:, a, h, m:m + 1])
                                own.done(ins)
                        dve.wait_ge(dve_step, own.last())
                        dve.sem_inc(tail_done.sem, 1)
                    for j, (u, a) in enumerate(tails):
                        dve.wait_ge(v2_done.sem, v2_done.now(it, j + 1))
                        if j == 0:
                            dve.wait_ge(o_done.sem, o_done.now(it, NU))
                        for h in range(4):
                            dst = o_sb[u][:, a, h * HD:(h + 1) * HD]
                            n = units.index((u, h, a))
                            ins = nc.vector.scalar_tensor_tensor(dst, Vp[:, h * HD:(h + 1) * HD], rinv[:, n:n + 1], dst, ALU.mult, ALU.add)
                            if h < 3:
                                own.done(ins)
                        ins.then_inc(v2_out.sem, 1)
                own.close()


def route(nc, stage, first_layer, logits, cap, consts, table, slots, weights):
    NT, NB = NTOK // 128, (2 if first_layer else 1) * (NTOK // 128)
    OUT = 16384.0
    with ExitStack() as ctx:
        r = Room(nc, ctx, stage)
        lg, gates = r.sb("lg", [128, NT, NE]), r.sb("gates", [128, NT, NE])
        top, topi = r.sb("top", [128, NT, NE]), r.sb("topi", [128, NT, NE], U32)
        topf = r.sb("topf", [128, NT, NE])
        m, s = r.sb("m", [128, NT]), r.sb("s", [128, NT])
        iota, tri, ones = r.sb("iota", [128, NT, NE]), r.sb("tri", [128, 128]), r.sb("ones", [128, 128])
        tok = r.sb("tok", [128, NT], U32)
        hot = r.sb("hot", [128, 2, NT, NE])
        both = r.sb("both", [128, 2, NT, NE])
        pre = r.sb("pre", [128, NB + 1, NE])
        rank = r.sb("rank", [128, 2, NT, NE])
        place, ok, slot = r.sb("place", [128, 2, NT]), r.sb("ok", [128, 2, NT]), r.sb("slot", [128, 2, NT])
        sc_f, sc_i = r.sb("sc_f", [128, 2, NT]), r.sb("sc_i", [128, 2, NT], U32)
        ga_i = r.sb("ga_i", [128, NT, 2], U32)
        wt = r.sb("wt", [128, NT, 2])
        zero = r.sb("zero", [112, NE * cap // 112], U32)
        pos = r.ps("pos", [128, NB, NE])
        loaded, zero_set, zeroed, counted = (r.sem(x) for x in ("loaded", "zero_set", "zeroed", "counted"))
        dve_step, exp_in, exp_out, hot_ready = (r.sem(x) for x in ("dve_step", "exp_in", "exp_out", "hot_ready"))
        ready, scattered, kept = r.sem("ready"), r.sem("scattered"), r.sem("kept")
        block = ctx.enter_context(nc.Block())

        @block.sync
        def _(sp):
            sp.dma_start(lg[:, :, :], logits.rearrange("(t p) e -> p t e", p=128)).then_inc(loaded, 16)
            sp.dma_start(iota[:, :, :], consts["iota"]).then_inc(loaded, 16)
            sp.dma_start(tri[:, :], consts["tri"]).then_inc(loaded, 16)
            sp.dma_start(tok[:, :], consts["tok"]).then_inc(loaded, 16)
            sp.wait_ge(zero_set, 1)
            sp.dma_start(table.rearrange("(p n) o -> p (n o)", p=112), zero[:, :]).then_inc(zeroed, 16)
            sp.wait_ge(ready, 1)
            sp.dma_start(slots.rearrange("t p k -> p t k"), ga_i[:, :, :]).then_inc(kept, 16)
            sp.dma_start(weights.rearrange("t p k -> p t k"), wt[:, :, :]).then_inc(kept, 16)
            sp.wait_ge(kept, 32)

        @block.gpsimd
        def _(pool):
            pool.memset(zero[:, :], 0).then_inc(zero_set, 1)
            pool.memset(ones[:, :], 1.0).then_inc(zero_set, 1)
            pool.wait_ge(zeroed, 16)
            pool.wait_ge(ready, 1)
            for k in range(2):
                for t in range(NT):
                    pool.indirect_dma_start(out=table, out_offset=bass.IndirectOffsetOnAxis(ap=sc_i[:, k, t:t + 1], axis=0),
                                            in_=tok[:, t:t + 1], in_offset=None, bounds_check=NE * cap - 1,
                                            oob_is_err=False).then_inc(scattered, 16)
            pool.wait_ge(scattered, 16 * 2 * NT)

        @block.tensor
        def _(pe):
            pe.wait_ge(zero_set, 2)
            pe.wait_ge(hot_ready, 1)
            src = hot[:, :, :, :].rearrange("p k t e -> p (k t e)") if first_layer else both[:, 0, :, :].rearrange("p t e -> p (t e)")
            out = pos[:, :, :].rearrange("p t e -> p (t e)")
            nc.tensor.matmul(out, tri[:, :], src, start=True, stop=False)
            nc.tensor.matmul(out, ones[:, :], pre[:, 0:NB, :].rearrange("p t e -> p (t e)"), start=False, stop=True).then_inc(counted, 1)

        @block.scalar
        def _(act):
            act.wait_ge(exp_in, 1)
            src = s[:, :] if first_layer else gates[:, :, :]
            nc.scalar.activation(src, src, ACT.Exp).then_inc(exp_out, 1)

        @block.vector
        def _(dve):
            step = [0]

            def then(ins):
                ins.then_inc(dve_step, 1)
                step[0] += 1
                dve.wait_ge(dve_step, step[0])

            dve.wait_ge(loaded, 64)
            if first_layer:
                chosen = lg
            else:
                then(nc.vector.tensor_reduce(m[:, :], lg[:, :, :], X, ALU.max))
                nc.vector.tensor_tensor(gates[:, :, :], lg[:, :, :], m[:, :].unsqueeze(2).broadcast_to([128, NT, NE]),
                                        ALU.subtract).then_inc(exp_in, 1)
                dve.wait_ge(exp_out, 1)
                then(nc.vector.tensor_reduce(s[:, :], gates[:, :, :], X, ALU.add))
                then(nc.vector.reciprocal(m[:, :], s[:, :]))
                then(nc.vector.tensor_tensor(gates[:, :, :], gates[:, :, :], m[:, :].unsqueeze(2).broadcast_to([128, NT, NE]), ALU.mult))
                chosen = gates
            for t in range(NT):
                then(nc.vector.max(top[:, t, :], chosen[:, t, :]))
                then(nc.vector.max_index(topi[:, t, :], top[:, t, :], chosen[:, t, :]))
            then(nc.vector.tensor_copy(topf[:, :, :], topi[:, :, :]))
            for k in range(2):
                then(nc.vector.tensor_tensor(hot[:, k, :, :], iota[:, :, :], topf[:, :, k:k + 1].broadcast_to([128, NT, NE]), ALU.is_equal))
            if not first_layer:
                then(nc.vector.tensor_tensor(both[:, 0, :, :], hot[:, 0, :, :], hot[:, 1, :, :], ALU.add))
            blocks = [hot[:, j // NT, j % NT, :] if first_layer else both[:, 0, j, :] for j in range(NB)]
            then(nc.vector.memset(pre[:, 0, :], 0.0))
            for j in range(NB):
                ins = nc.vector.tensor_tensor(pre[:, j + 1, :], pre[:, j, :], blocks[j], ALU.add)
                if j < NB - 1:
                    then(ins)
            ins.then_inc(hot_ready, 1)
            if first_layer:
                nc.vector.tensor_tensor(s[:, :], top[:, :, 1], top[:, :, 0], ALU.subtract).then_inc(exp_in, 1)
                dve.wait_ge(exp_out, 1)
                then(nc.vector.tensor_scalar(m[:, :], s[:, :], 1.0, None, ALU.add))
                then(nc.vector.reciprocal(wt[:, :, 0], m[:, :]))
                then(nc.vector.tensor_tensor(wt[:, :, 1], s[:, :], wt[:, :, 0], ALU.mult))
            else:
                then(nc.vector.tensor_copy(wt[:, :, :], top[:, :, 0:2]))
            dve.wait_ge(counted, 1)
            for k in range(2):
                p = pos[:, k * NT:(k + 1) * NT, :] if first_layer else pos[:, :, :]
                then(nc.vector.tensor_tensor(rank[:, k, :, :], p, hot[:, k, :, :], ALU.mult))
                then(nc.vector.tensor_reduce(place[:, k, :], rank[:, k, :, :], X, ALU.add))
            then(nc.vector.tensor_scalar(place[:, :, :], place[:, :, :], -1.0, None, ALU.add))
            then(nc.vector.tensor_scalar(ok[:, :, :], place[:, :, :], float(cap), None, ALU.is_lt))
            for k in range(2):
                then(nc.vector.scalar_tensor_tensor(slot[:, k, :], topf[:, :, k], float(cap), place[:, k, :], ALU.mult, ALU.add))
            then(nc.vector.scalar_tensor_tensor(sc_f[:, :, :], slot[:, :, :], -OUT, ok[:, :, :], ALU.add, ALU.mult))
            then(nc.vector.tensor_scalar(sc_i[:, :, :], sc_f[:, :, :], OUT, None, ALU.add))
            then(nc.vector.tensor_tensor(slot[:, :, :], slot[:, :, :], ok[:, :, :], ALU.mult))
            for k in range(2):
                then(nc.vector.tensor_copy(ga_i[:, :, k], slot[:, k, :]))
                ins = nc.vector.tensor_tensor(wt[:, :, k], wt[:, :, k], ok[:, k, :], ALU.mult)
                if k == 0:
                    then(ins)
            ins.then_inc(ready, 1)


def experts(nc, stage, cap, tiles, x, w1, w2, b1, b2, table, out, consts):
    gelu = b1 is not None
    FC = FF // 128
    nh = 2 if cap > 512 else 1
    hc = cap // nh
    jobs = [("tp", i) for i in range(len(tiles))] + [("h", (f, s)) for f in range(FC) for s in range(nh)] \
        + [("o", i) for i in range(len(tiles))]
    NJ, RING, NTL = len(jobs), 6, len(tiles)
    on_act = [j[0] != "o" for j in jobs]
    nth = lambda m: sum(1 for k in range(m + 1) if on_act[k] == on_act[m])
    first_o = NJ - NTL
    with ExitStack() as ctx:
        r = Room(nc, ctx, stage)
        ident = r.sb("ident", [128, 128])
        idx = r.sb("idx", [128, NTL], U32)
        xg = r.sb("xg", [TP, NTL, D])
        xT = r.sb("xT", [128, C, cap])
        w1s, w2s = r.sb("w1", [128, C, FF]), r.sb("w2", [128, FC, D])
        hT = r.sb("hT", [128, FC, cap])
        o = r.sb("o", [TP, NTL, D])
        if gelu:
            b1s, b2s = r.sb("b1", [128, FC]), r.sb("b2", [TP, D])
        ring = [r.ps(f"ring{i}", [128, 512]) for i in range(RING)]
        fixed = r.sem("fixed")
        idx_loaded, gathered = r.event("idx_loaded", 16 * NTL, False), r.event("gathered", 16 * NTL, False)
        w1_loaded, w2_loaded = r.event("w1_loaded", 16 * (C + gelu)), r.event("w2_loaded", 16 * (4 + gelu))
        mm_done = r.event("mm_done", NJ)
        act_out, dve_out = r.event("act_out", NJ - NTL), r.event("dve_out", NTL)
        squared = r.event("squared", FC * nh)
        stored = r.event("stored", 16 * NTL)
        block = ctx.enter_context(nc.Block())

        @block.sync
        def _(sp):
            sp.dma_start(ident[:, :], consts["ident"]).then_inc(fixed, 16)
            for e in (w1_loaded, w2_loaded):
                sp.sem_inc(e.sem, e.per)
            with sp.Fori(0, NE) as it:
                sp.wait_ge(mm_done.sem, mm_done.before(it, first_o))
                sp.nop(nofuse=True)
                for c in range(C):
                    sp.dma_start(w1s[:, c, :], w1[bass.ds(it * D + c * 128, 128), :]).then_inc(w1_loaded.sem, 16)
                if gelu:
                    sp.wait_ge(act_out.sem, act_out.before(it))
                    sp.nop(nofuse=True)
                    sp.dma_start(b1s[:, :], b1[bass.ds(it * 128, 128), :]).then_inc(w1_loaded.sem, 16)
                sp.wait_ge(mm_done.sem, mm_done.before(it))
                sp.nop(nofuse=True)
                for c in range(4):
                    sp.dma_start(w2s[:, c * 4:(c + 1) * 4, :],
                                 w2[bass.ds(it * FF + c * 512, 512), :].rearrange("(f p) n -> p f n", p=128)).then_inc(w2_loaded.sem, 16)
                if gelu:
                    sp.wait_ge(dve_out.sem, dve_out.before(it))
                    sp.nop(nofuse=True)
                    sp.dma_start(b2s[:, :], b2[bass.ds(it, 1), :].broadcast_to([TP, D])).then_inc(w2_loaded.sem, 16)

        @block.gpsimd
        def _(pool):

            def gather(it):
                for i, (r0, n) in enumerate(tiles):
                    pool.dma_start(idx[:n, i:i + 1], table[bass.ds(it * cap + r0, n), :]).then_inc(idx_loaded.sem, 16)
                pool.wait_ge(idx_loaded.sem, idx_loaded.now(it, idx_loaded.per))
                pool.wait_ge(mm_done.sem, mm_done.before(it, NTL))
                pool.nop(nofuse=True)
                for i, (r0, n) in enumerate(tiles):
                    pool.indirect_dma_start(out=xg[:n, i, :], out_offset=None, in_=x,
                                            in_offset=bass.IndirectOffsetOnAxis(ap=idx[:n, i:i + 1], axis=0)).then_inc(gathered.sem, 16)
                pool.wait_ge(gathered.sem, gathered.now(it, gathered.per))
                pool.nop(nofuse=True)

            with pool.Fori(0, NE) as it:
                gather(it)

        @block.tensor
        def _(pe):
            pe.sem_inc(mm_done.sem, NJ)
            pe.wait_ge(fixed, 16)
            with pe.Fori(0, NE) as it:
                for m, (kind, i) in enumerate(jobs):
                    bank = ring[m % RING]
                    if m >= RING:
                        k, v = m - RING, 1
                    else:
                        k, v = max(k for k in range(NJ) if k % RING == m), 0
                    e = act_out if on_act[k] else dve_out
                    pe.wait_ge(e.sem, e.now(it, nth(k)) if v else e.before(it, nth(k)))
                    if kind == "tp":
                        n = tiles[i][1]
                        pe.wait_ge(gathered.sem, gathered.now(it, gathered.per))
                        pe.nop(nofuse=True)
                        for c in range(C):
                            ins = nc.tensor.transpose(bank[:, c * n:(c + 1) * n], xg[:n, i, c * 128:(c + 1) * 128], ident[:n, :n])
                    elif kind == "h":
                        f, s = i
                        if m == NTL:
                            pe.wait_ge(w1_loaded.sem, w1_loaded.now(it, w1_loaded.per))
                            pe.wait_ge(act_out.sem, act_out.now(it, NTL))
                        for c in range(C):
                            ins = nc.tensor.matmul(bank[:, :hc], w1s[:, c, f * 128:(f + 1) * 128], xT[:, c, s * hc:(s + 1) * hc],
                                                   start=(c == 0), stop=(c == C - 1))
                    else:
                        r0, n = tiles[i]
                        if m == first_o:
                            pe.wait_ge(w2_loaded.sem, w2_loaded.now(it, w2_loaded.per))
                            e = act_out if gelu else squared
                            pe.wait_ge(e.sem, e.now(it, e.per))
                        for f in range(FC):
                            ins = nc.tensor.matmul(bank[:n, :], hT[:, f, r0:r0 + n], w2s[:, f, :], start=(f == 0), stop=(f == FC - 1))
                    ins.then_inc(mm_done.sem, 1)

        @block.scalar
        def _(act):
            act.sem_inc(act_out.sem, act_out.per)
            act.sem_inc(stored.sem, stored.per)
            with act.Fori(0, NE) as it:
                for m, (kind, i) in enumerate(jobs):
                    bank = ring[m % RING]
                    if kind == "o":
                        r0, n = tiles[i]
                        act.wait_ge(dve_out.sem, dve_out.now(it, i + 1))
                        act.dma_start(out[bass.ds(it * cap + r0, n), :], o[:n, i, :]).then_inc(stored.sem, 16)
                        continue
                    act.wait_ge(mm_done.sem, mm_done.now(it, m + 1))
                    if kind == "tp":
                        r0, n = tiles[i]
                        nc.scalar.activation(xT[:, :, r0:r0 + n], bank[:, :C * n].rearrange("p (c t) -> p c t", c=C),
                                             ACT.Copy).then_inc(act_out.sem, 1)
                    elif gelu:
                        f, s = i
                        if m == NTL:
                            act.wait_ge(w1_loaded.sem, w1_loaded.now(it, w1_loaded.per))
                        nc.scalar.activation(hT[:, f, s * hc:(s + 1) * hc], bank[:, :hc], ACT.Gelu,
                                             bias=b1s[:, f:f + 1]).then_inc(act_out.sem, 1)
                    else:
                        f, s = i
                        nc.scalar.activation(hT[:, f, s * hc:(s + 1) * hc], bank[:, :hc], ACT.Relu).then_inc(act_out.sem, 1)
            act.wait_ge(stored.sem, stored.end(NE))

        @block.vector
        def _(dve):
            dve.sem_inc(dve_out.sem, dve_out.per)
            dve.sem_inc(squared.sem, squared.per)
            with dve.Fori(0, NE) as it:
                for m, (kind, i) in enumerate(jobs):
                    if kind == "h" and not gelu:
                        f, s = i
                        dve.wait_ge(act_out.sem, act_out.now(it, m + 1))
                        dst = hT[:, f, s * hc:(s + 1) * hc]
                        nc.vector.tensor_tensor(dst, dst, dst, ALU.mult).then_inc(squared.sem, 1)
                    elif kind == "o":
                        r0, n = tiles[i]
                        dve.wait_ge(mm_done.sem, mm_done.now(it, m + 1))
                        if i == 0:
                            dve.wait_ge(stored.sem, stored.before(it))
                        if gelu:
                            if i == 0:
                                dve.wait_ge(w2_loaded.sem, w2_loaded.now(it, w2_loaded.per))
                            nc.vector.tensor_tensor(o[:n, i, :], ring[m % RING][:n, :], b2s[:n, :], ALU.add).then_inc(dve_out.sem, 1)
                        else:
                            nc.vector.tensor_copy(o[:n, i, :], ring[m % RING][:n, :]).then_inc(dve_out.sem, 1)


def combine(nc, stage, x, rows, slots, weights, out):
    steps = NTOK // 128 // 2
    with ExitStack() as ctx:
        r = Room(nc, ctx, stage)
        xs = [r.sb(f"x{u}", [128, D]) for u in range(2)]
        idx = [r.sb(f"idx{u}", [128, 2], U32) for u in range(2)]
        wt = [r.sb(f"wt{u}", [128, 2]) for u in range(2)]
        g = [[r.sb(f"g{u}{k}", [128, D]) for k in range(2)] for u in range(2)]
        y = [r.sb(f"y{u}", [128, D]) for u in range(2)]
        t = [r.sb(f"t{u}", [128, D]) for u in range(2)]
        stats, mv = r.sb("stats", [128, 2, 6]), r.sb("mv", [128, 2, 2])
        std, rstd, eps = r.sb("std", [128, 2]), r.sb("rstd", [128, 2]), r.sb("eps", [128, 1])
        eps_set = r.sem("eps_set")
        idx_loaded, x_loaded = [[r.event(f"{s}{u}", per) for u in range(2)] for s, per in (("idx_loaded", 16), ("x_loaded", 32))]
        gathered = [r.event(f"gathered{u}", 32, False) for u in range(2)]
        y_ready, var_ready, std_ready, stored = (r.event(s, p) for s, p in (("y_ready", 2), ("var_ready", 2), ("std_ready", 2), ("stored", 32)))
        dve_step = r.sem("dve_step")
        block = ctx.enter_context(nc.Block())

        @block.sync
        def _(sp):
            for e in idx_loaded + x_loaded:
                sp.sem_inc(e.sem, e.per)
            with sp.Fori(0, steps) as it:
                for u in range(2):
                    sp.wait_ge(y_ready.sem, y_ready.before(it, u + 1))
                    sp.dma_start(idx[u][:, :], slots[bass.ds(it * 2 + u, 1), :, :].rearrange("t p k -> (t p) k")).then_inc(idx_loaded[u].sem, 16)
                    sp.dma_start(wt[u][:, :], weights[bass.ds(it * 2 + u, 1), :, :].rearrange("t p k -> (t p) k")).then_inc(x_loaded[u].sem, 16)
                    sp.dma_start(xs[u][:, :], x[bass.ds((it * 2 + u) * 128, 128), :]).then_inc(x_loaded[u].sem, 16)

        @block.gpsimd
        def _(pool):
            pool.memset(eps[:, :], EPS).then_inc(eps_set, 1)
            with pool.Fori(0, steps) as it:
                for u in range(2):
                    pool.wait_ge(idx_loaded[u].sem, idx_loaded[u].now(it, 16))
                    pool.wait_ge(y_ready.sem, y_ready.before(it, u + 1))
                    pool.nop(nofuse=True)
                    for k in range(2):
                        pool.indirect_dma_start(out=g[u][k][:, :], out_offset=None, in_=rows,
                                                in_offset=bass.IndirectOffsetOnAxis(ap=idx[u][:, k:k + 1], axis=0)).then_inc(gathered[u].sem, 16)

        @block.scalar
        def _(act):
            for e in (std_ready, stored):
                act.sem_inc(e.sem, e.per)
            act.wait_ge(eps_set, 1)
            with act.Fori(0, steps) as it:
                for u in range(2):
                    act.wait_ge(var_ready.sem, var_ready.now(it, u + 1))
                    nc.scalar.activation(std[:, u:u + 1], mv[:, u, 1:2], ACT.Sqrt, bias=eps[:, :]).then_inc(std_ready.sem, 1)
                    act.wait_ge(y_ready.sem, y_ready.now(it, u + 1))
                    act.dma_start(out[bass.ds((it * 2 + u) * 128, 128), :], y[u][:, :]).then_inc(stored.sem, 16)
            act.wait_ge(stored.sem, stored.end(steps))

        @block.vector
        def _(dve):
            for e in (y_ready, var_ready):
                dve.sem_inc(e.sem, e.per)
            with dve.Fori(0, steps) as it:
                own = Chain(dve, dve_step, it, 8)
                for u in range(2):
                    dve.wait_ge(x_loaded[u].sem, x_loaded[u].now(it, 32))
                    dve.wait_ge(gathered[u].sem, gathered[u].now(it, 32))
                    own.done(nc.vector.scalar_tensor_tensor(t[u][:, :], g[u][0][:, :], wt[u][:, 0:1], xs[u][:, :], ALU.mult, ALU.add))
                    dve.wait_ge(dve_step, own.last())
                    own.done(nc.vector.scalar_tensor_tensor(t[u][:, :], g[u][1][:, :], wt[u][:, 1:2], t[u][:, :], ALU.mult, ALU.add))
                    dve.wait_ge(dve_step, own.last())
                    own.done(nc.vector.bn_stats(stats[:, u, :], t[u][:, :]))
                    dve.wait_ge(dve_step, own.last())
                    dve.nop(nofuse=True)
                    nc.vector.bn_aggr(mv[:, u, :], stats[:, u, :]).then_inc(var_ready.sem, 1)
                    dve.wait_ge(std_ready.sem, std_ready.now(it, u + 1))
                    own.done(nc.vector.reciprocal(rstd[:, u:u + 1], std[:, u:u + 1]))
                    dve.wait_ge(dve_step, own.last())
                    if u == 0:
                        dve.wait_ge(stored.sem, stored.before(it))
                    nc.vector.tensor_scalar(y[u][:, :], t[u][:, :], mv[:, u, 0:1], rstd[:, u:u + 1],
                                            ALU.subtract, ALU.mult).then_inc(y_ready.sem, 1)


def decoder(nc, a, out, kind="Internal", upto=99):
    def scratch(name, shape, dt=FP32):
        return nc.dram_tensor(f"scr_{name}", shape, dt, kind=kind).ap() if kind != "Internal" else nc.dram_tensor(f"scr_{name}", shape, dt).ap()

    G = B * HG
    qT, kT, v = scratch("qT", [G * 128, T]), scratch("kT", [G * 128, T]), scratch("v", [G, T, 128])
    cq = scratch("cq", [G * 128, T])
    ck, cv = scratch("ck", [G * 128, CTXN]), scratch("cv", [G, CTXN, 128])
    pk, pv = scratch("pk", [2 * HG * 128, PASTN]), scratch("pv", [2 * HG, PASTN, 128])
    wk, wv = scratch("wk", [G * 128, T]), scratch("wv", [G, T, 128])
    ctx0, ctx1, ctx2 = (scratch(s, [G, T, 128]) for s in ("ctx0", "ctx1", "ctx2"))
    ctx3, ctx4 = scratch("ctx3", [2 * G, T, 128]), scratch("ctx4", [G, T, 128])
    x1, x2, x3, o1, x4, x5 = (scratch(s, [NTOK, D]) for s in ("x1", "x2", "x3", "o1", "x4", "x5"))
    lg0, lg1 = scratch("lg0", [NTOK, NE]), scratch("lg1", [NTOK, NE])
    table0, table1 = scratch("table0", [NE * CAP0, 1], U32), scratch("table1", [NE * CAP1, 1], U32)
    slots0, slots1 = (scratch(s, [NTOK // 128, 128, 2], U32) for s in ("slots0", "slots1"))
    wts0, wts1 = (scratch(s, [NTOK // 128, 128, 2]) for s in ("wts0", "wts1"))
    rows0, rows1 = scratch("rows0", [NE * CAP0, D]), scratch("rows1", [NE * CAP1, D])
    bands = [[nc.dram_tensor(f"band{u}{s}", [4, T * (PADW + 1)], FP32).ap() for s in range(2)] for u in range(2)]
    pband = [nc.dram_tensor(f"pband{u}", [4, T * (PADW + 1)], FP32).ap() for u in range(2)]

    def heads_T(dst, n=T):
        return lambda it: dst[bass.ds(it * D, D), :].rearrange("(c p) t -> p c t", p=128)

    def heads_v(dst, tk):
        return lambda it, t: dst[bass.ds(it * HG, HG), t * tk:(t + 1) * tk, :].rearrange("g p d -> p g d")

    def grouped(src, off=0):
        return (True, lambda it, t: src[bass.ds(it * HG + off, HG), t * TP:(t + 1) * TP, :].rearrange("g p d -> p g d"))

    def rows(src):
        return lambda it: src[bass.ds(it * T, T), :].rearrange("(a p) d -> p a d", p=TP)

    def tile_rows(src):
        return (False, lambda it, t: src[bass.ds(it * T + t * TP, TP), :])

    def router(dst):
        return lambda it, t: dst[bass.ds(it * T + t * TP, TP), :]

    def cols_of(src):
        return lambda it: src[bass.ds(it * D, D), :].rearrange("(c p) t -> p c t", p=128)

    s32 = float(HD ** -0.5)
    stages = [
        lambda: token_stage(nc, "qkv0", B, T, TP, T, a, xT=cols_of(a["xT"]),
                            fm=[(a["wq0"], None, s32, None, heads_T(qT)), (a["wk0"], None, 1.0, None, heads_T(kT))],
                            tm=[(a["wv0"], None, D, heads_v(v, TP))]),
        lambda: attention(nc, "att0", 1, T, TP, qT, kT, v, ctx0, a,
                          rpe=((a["rpe_k"], a["rpe_q"]), a["rpe_v"], bands, pband)),
        lambda: token_stage(nc, "out0", B, T, TP, T, a, zs=[grouped(ctx0)], wz=a["wo0"], bz=a["bo0"], res=rows(a["x"]),
                            norm=True, y_out=rows(x1), fm=[(a["xq0"], None, float(D ** -0.5), None, heads_T(cq))]),
        lambda: token_stage(nc, "ckv0", B, CTXN, 125, 375, a, xT=cols_of(a["ctxT"]),
                            fm=[(a["xk0"], None, 1.0, None, heads_T(ck))], tm=[(a["xv0"], None, D, heads_v(cv, 125))]),
        lambda: attention(nc, "xat0", 1, CTXN, 125, cq, ck, cv, ctx1, a),
        lambda: token_stage(nc, "out1", B, T, TP, T, a, zs=[grouped(ctx1)], wz=a["xo0"], bz=a["xbo0"], res=rows(x1),
                            norm=True, y_out=rows(x2), tm=[(a["wg0"], None, NE, router(lg0))]),
        lambda: route(nc, "rte0", True, lg0, CAP0, a, table0, slots0, wts0),
        lambda: experts(nc, "exp0", CAP0, [(i * TP, TP) for i in range(5)], x2, a["fc0"], a["pj0"], None, None, table0, rows0, a),
        lambda: combine(nc, "cmb0", x2, rows0, slots0, wts0, x3),
        lambda: token_stage(nc, "qkv1", B, T, TP, T, a, y_in=rows(x3),
                            fm=[(a["Wq"], a["bq"], s32, None, heads_T(qT)), (a["Wk"], a["bk"], 1.0, None, heads_T(kT))],
                            tm=[(a["Wv"], a["bv"], D, heads_v(v, TP))]),
        lambda: attention(nc, "att1", 1, T, TP, qT, kT, v, ctx2, a),
        lambda: token_stage(nc, "out2", B, T, TP, T, a, zs=[grouped(ctx2)], wz=a["Wo"], bz=a["bo"], y_out=rows(o1),
                            fm=[(a["Wrq"], a["brq"], s32, None, heads_T(cq))]),
        lambda: token_stage(nc, "pkv1", 2, PASTN, 128, 512, a, xT=cols_of(a["pastT"]),
                            fm=[(a["Wrk"], a["brk"], 1.0, None, heads_T(pk))], tm=[(a["Wrv"], a["brv"], D, heads_v(pv, 128))]),
        lambda: attention(nc, "rec1", 2, PASTN, 128, cq, pk, pv, ctx3, a, shared=True),
        lambda: token_stage(nc, "out3", B, T, TP, T, a, zs=[tile_rows(o1), grouped(ctx3), grouped(ctx3, G)], wz=a["Wg"], bz=a["bg"],
                            gate=True, res=rows(x3), norm=True, y_out=rows(x4),
                            fm=[(a["lq"], a["lqb"], None, 1, None), (a["lqr"], a["lqrb"], a["trig_q"], 2, heads_T(qT))]),
        lambda: token_stage(nc, "wkv1", B, T, TP, T, a, xT=cols_of(a["ctx224T"]),
                            fm=[(a["lk"], a["lkb"], None, 1, None), (a["lkr"], a["lkrb"], a["trig_k"], 2, heads_T(wk))],
                            tm=[(a["lv"], a["lvb"], D, heads_v(wv, TP))]),
        lambda: attention(nc, "win1", 1, T, TP, qT, wk, wv, ctx4, a, mask=a["window"]),
        lambda: token_stage(nc, "out4", B, T, TP, T, a, zs=[grouped(ctx4)], wz=a["lo"], bz=a["lob"], res=rows(x4),
                            norm=True, y_out=rows(x5), tm=[(a["rw1"], a["rb1"], NE, router(lg1))]),
        lambda: route(nc, "rte1", False, lg1, CAP1, a, table1, slots1, wts1),
        lambda: experts(nc, "exp1", CAP1, [(0, TP), (TP, TP), (2 * TP, 56)], x5, a["w1"], a["w2"], a["b1"], a["b2"], table1, rows1, a),
        lambda: combine(nc, "cmb1", x5, rows1, slots1, wts1, out),
    ]
    for stage in stages[:upto]:
        stage()


def shape_constants():
    i = np.arange(T)
    rel = i[None, :] - i[:, None]
    tiled = lambda m: np.ascontiguousarray(m.reshape(NA, TP, T).transpose(1, 0, 2))
    far = np.stack([tiled(rel < -HALF), tiled(rel > HALF)], 1)
    window = tiled(np.where((rel <= 0) & (rel >= -64), 0.0, NEG))
    half = HD // 2
    freqs = (1.0 / 10000.0 ** (np.arange(half, dtype=np.float32) / half)).astype(np.float32)
    ang = (np.arange(T, dtype=np.float32)[:, None] * freqs[None, :]).astype(np.float32)
    cos = np.tile(np.cos(ang).T, (8, 1))
    sin = np.sin(ang).T
    sin = np.tile(np.concatenate([-sin, sin], 0), (4, 1))
    s = HD ** -0.5
    return {
        "ident": np.eye(128), "tri": np.triu(np.ones((128, 128))), "far": far, "window": window,
        "trig_q": np.stack([cos * s, sin * s]), "trig_k": np.stack([cos, sin]),
        "iota": np.broadcast_to(np.arange(NE), (128, NTOK // 128, NE)),
        "tok": np.arange(NTOK).reshape(-1, 128).T,
    }


def laid_out(x, n):
    T2 = lambda w: w.T
    turned = lambda w: w.reshape(B if w.shape[0] == B else 2, w.shape[1], D).transpose(0, 2, 1).reshape(-1, w.shape[1])
    bias = lambda b: b.reshape(C, 128).T.reshape(-1)
    swap = (np.arange(D).reshape(H, 2, HD // 2)[:, ::-1]).reshape(-1)

    def blocks(w):
        m = np.zeros((128, 128), w.dtype)
        for h in range(4):
            m[h * HD:(h + 1) * HD, h * HD:(h + 1) * HD] = w.T
        return m

    w = n["L0_attn_w_qkv"]

    def per_head(t):
        m = np.zeros((HG, 4, HD, 4, 64), t.dtype)
        for h in range(4):
            m[:, h, :, h, :NBUCK] = t.reshape(HG, 4, HD, NBUCK)[:, h]
        return m.reshape(HG * 128, 256)

    d = {
        "x": x.reshape(NTOK, D), "xT": turned(x), "ctxT": turned(n["ctx_1024"]), "ctx224T": turned(n["ctx_1024"][:, :T]),
        "pastT": turned(n["L1_attn_past_states"].reshape(2, PASTN, D)),
        "wq0": T2(w[:D]), "wk0": T2(w[D:2 * D]), "wv0": T2(w[2 * D:]),
        "wo0": T2(n["L0_attn_w_proj"]), "bo0": n["L0_attn_b_proj"],
        "rpe_k": per_head(n["L0_attn_rpe_k_table"]), "rpe_q": per_head(n["L0_attn_rpe_q_table"]),
        "rpe_v": n["L0_attn_rpe_v_table"].reshape(HG, 4, NBUCK, HD).transpose(0, 2, 1, 3).reshape(HG * NBUCK, 128),
        "xq0": blocks(n["L0_xattn_Wq"]), "xk0": blocks(n["L0_xattn_Wk"]), "xv0": blocks(n["L0_xattn_Wv"]),
        "xo0": T2(n["L0_xattn_Wo"]), "xbo0": n["L0_xattn_bo"],
        "wg0": T2(n["L0_ffn_w_g"]), "fc0": n["L0_ffn_c_fc"].reshape(NE * D, FF), "pj0": n["L0_ffn_c_proj"].reshape(NE * FF, D),
        "lo": T2(n["L1_xattn_o_w"]), "lob": n["L1_xattn_o_b"], "lv": T2(n["L1_xattn_v_w"]), "lvb": n["L1_xattn_v_b"],
        "rw1": n["L1_ffn_router_w"], "rb1": n["L1_ffn_router_b"],
        "w1": n["L1_ffn_w1"].reshape(NE * D, FF), "w2": n["L1_ffn_w2"].reshape(NE * FF, D),
        "b1": n["L1_ffn_b1"].reshape(NE, FF // 128, 128).transpose(0, 2, 1).reshape(NE * 128, FF // 128), "b2": n["L1_ffn_b2"],
    }
    for s in ("Wq", "Wk", "Wv", "Wo", "Wrq", "Wrk", "Wrv", "Wg"):
        d[s] = n["L1_attn_" + s]
    for s in ("bq", "bk", "brq", "brk"):
        d[s] = bias(n["L1_attn_" + s])
    for s in ("bv", "bo", "brv", "bg"):
        d[s] = n["L1_attn_" + s]
    for s in ("q", "k"):
        wt, b = n[f"L1_xattn_{s}_w"], n[f"L1_xattn_{s}_b"]
        d["l" + s], d["l" + s + "b"] = T2(wt), bias(b)
        d["l" + s + "r"], d["l" + s + "rb"] = T2(wt[swap]), bias(b[swap])
    return d


def kernel(**inputs):
    import numpy as _np
    import concourse.bacc as _bacc
    from concourse import mybir as _mybir
    from concourse.bass_utils import run_bass_kernel_spmd as _run

    n = {k: _np.asarray(v) for k, v in inputs.items()}
    nc = _bacc.Bacc("TRN2", target_bir_lowering=False, num_devices=1)
    arrays, handles = {}, {}
    consts = {k: v.astype(_np.uint32 if k == "tok" else _np.float32) for k, v in shape_constants().items()}
    for name, v in {**laid_out(n["x"], n), **consts}.items():
        v = _np.ascontiguousarray(v)
        arrays["in_" + name] = v
        handles[name] = nc.dram_tensor("in_" + name, v.shape, _mybir.dt.from_np(v.dtype), kind="ExternalInput").ap()
    out = nc.dram_tensor("out_dram", (NTOK, D), FP32, kind="ExternalOutput").ap()
    decoder(nc, handles, out)
    r = _run(nc, [arrays], core_ids=[0])
    return r.results[0]["out_dram"].reshape(B, T, D)
```

```python
import concourse.bass as bass
from concourse import mybir
from concourse.alu_op_type import AluOpType as ALU
from contextlib import ExitStack
import numpy as np

FP32 = mybir.dt.float32
BF16 = mybir.dt.bfloat16
U32 = mybir.dt.uint32
ACT = mybir.ActivationFunctionType
X = mybir.AxisListType.X

B, T, D = 8, 224, 512
NTOK = B * T
H, HD = 16, 32
HG = 4
TP = 112
NA = T // TP
C = D // 128
CTXN = 750
PASTN = 1024
NE, FF = 8, 2048
CAP0, CAP1 = 560, 280
EPS = 1e-5
HALF = 31
NBUCK = 2 * HALF + 1
PADW = T + 2 * HALF
NEG = -1.0e30
VW = H * (HD + 1)


class Event:

    def __init__(self, sem, per, primed=True):
        self.sem, self.per, self.primed = sem, per, primed

    def now(self, it, k):
        return (it + self.primed) * self.per + k

    def before(self, it, k=None):
        return it * self.per + (self.per if k is None else k)

    def end(self, steps):
        return (steps + self.primed) * self.per


class Chain:

    def __init__(self, eng, sem, it, per):
        self.eng, self.sem, self.it, self.per, self.n = eng, sem, it, per, 0

    def done(self, ins):
        ins.then_inc(self.sem, 1)
        self.n += 1

    def last(self):
        return self.it * self.per + self.n

    def close(self):
        assert self.n == self.per, (self.n, self.per)


class Room:

    def __init__(self, nc, ctx, stage):
        self.nc, self.ctx, self.stage, self.sems = nc, ctx, stage, []
        ctx.callback(self.leave)

    def sb(self, name, shape, dt=FP32):
        return self.ctx.enter_context(self.nc.sbuf_tensor(f"{self.stage}_{name}", shape, dt))

    def ps(self, name, shape, dt=FP32):
        return self.ctx.enter_context(self.nc.psum_tensor(f"{self.stage}_{name}", shape, dt))

    def sem(self, name):
        self.sems.append(self.nc.alloc_semaphore(name=f"{self.stage}_{name}"))
        return self.sems[-1]

    def leave(self):
        self.nc.clear_and_free_semaphores(self.sems)
        self.nc.all_engine_barrier()

    def event(self, name, per, primed=True):
        return Event(self.sem(name), max(per, 1), primed)


def chunked(w):
    return w.rearrange("(c p) n -> p c n", p=min(128, w.shape[0]))


def rows_of(b, parts):
    return b.rearrange("(o n) -> o n", o=1).broadcast_to([parts, b.shape[0]])


def token_stage(nc, stage, steps, n, tk, cols, consts, xT=None, zs=None, wz=None, bz=None,
                gate=False, res=None, norm=False, y_out=None, y_in=None, fm=(), tm=()):
    nt, ncol = n // tk, n // cols
    nz = 0 if zs is None else (2 if gate else 1)
    jobs = [("tpz", z, a) for z in range(nz) for a in range(nt)]
    if nz:
        jobs += [("lin", 0, a) for a in range(nt)]
    if xT is None:
        jobs += [("tpy", 0, a) for a in range(nt)]
    jobs += [("fm", w, (c, s)) for c in range(C) for w in range(len(fm)) for s in range(ncol)]
    jobs += [("tm", w, a) for w in range(len(tm)) for a in range(nt)]
    if not fm and not tm:
        jobs = [j for j in jobs if j[0] != "tpy"]
    NJ = len(jobs)
    RING = min(6, NJ)
    on_act = [j[0] in ("tpz", "tpy") or (j[0] == "tm" and tm[j[1]][1] is None) for j in jobs]
    place = {j: i for i, j in enumerate(jobs)}

    def nth(m):
        return sum(1 for k in range(m + 1) if on_act[k] == on_act[m])

    with ExitStack() as ctx:
        r = Room(nc, ctx, stage)
        ident = r.sb("ident", [128, 128])
        nload = len(zs) if nz else 0
        z_sb = [r.sb(f"z{i}", [tk, nt, D]) for i in range(nload)]
        zT = [r.sb(f"zT{i}", [128, C, n]) for i in range(nz)]
        wz_sb = r.sb("wz", [128, C * nz, D]) if nz else None
        bz_sb = r.sb("bz", [tk, D]) if nz else None
        res_sb = r.sb("res", [tk, nt, D]) if res is not None else None
        y = r.sb("y", [tk, nt, D]) if xT is None else None
        t = r.sb("t", [tk, nt, D]) if nz else None
        stats, mv = r.sb("stats", [tk, nt, 6]), r.sb("mv", [tk, nt, 2])
        std, rstd, eps = r.sb("std", [tk, nt]), r.sb("rstd", [tk, nt]), r.sb("eps", [128, 1])
        yT = r.sb("yT", [128, C, n])
        fm_w = [r.sb(f"fw{i}", [128, f[0].shape[0] // 128, f[0].shape[1]]) for i, f in enumerate(fm)]
        fm_b = [r.sb(f"fb{i}", [128, C]) if f[1] is not None else None for i, f in enumerate(fm)]
        fm_o = [r.sb(f"fo{i}", [128, C, n]) for i, f in enumerate(fm)]
        tm_w = [r.sb(f"tw{i}", [128, f[0].shape[0] // 128, f[0].shape[1]]) for i, f in enumerate(tm)]
        tm_b = [r.sb(f"tb{i}", [tk, min(D, f[2])]) if f[1] is not None else None for i, f in enumerate(tm)]
        tm_o = [r.sb(f"to{i}", [tk, nt, f[2]]) for i, f in enumerate(tm)]
        split = [i for i, f in enumerate(fm) if isinstance(f[4], tuple)]
        parts = {i: [r.sb(f"part{i}{k}", [128, C, n], BF16) for k in range(3)] for i in split}
        roped = [i for i, f in enumerate(fm) if f[3] == 2]
        if roped:
            trig = [r.sb(f"trig{i}", [128, n]) for i in range(2)]
        ring = [r.ps(f"ring{i}", [128, 512]) for i in range(RING)]

        stored_fm = [i for i, f in enumerate(fm) if f[4] is not None]
        w_loaded, eps_set = r.sem("w_loaded"), r.sem("eps_set")
        z_loaded = r.event("z_loaded", 16 * nload * nt)
        res_loaded = r.event("res_loaded", 16)
        src_loaded = r.event("src_loaded", 16)
        mm_done = r.event("mm_done", NJ)
        act_out = r.event("act_out", sum(on_act))
        dve_out = r.event("dve_out", NJ - sum(on_act))
        y_ready = r.event("y_ready", nt)
        var_ready, std_ready = r.event("var_ready", nt), r.event("std_ready", 1)
        mean_ready = r.event("mean_ready", nt)
        gate_ready = r.event("gate_ready", nt)
        rope_ready = r.event("rope_ready", C * len(roped))
        y_stored = r.event("y_stored", 16, False)
        fm_stored = r.event("fm_stored", 16 * (len(stored_fm) + 2 * len(split)), False)
        part_act, part_dve = (r.event(s, 2 * len(split)) for s in ("part_act", "part_dve"))
        tm_stored = r.event("tm_stored", 16 * len(tm) * nt, False)
        y_free, fm_free, tm_free = (r.event(s, 1) for s in ("y_free", "fm_free", "tm_free"))
        dve_step = r.sem("dve_step")
        block = ctx.enter_context(nc.Block())
        out_of = lambda m: act_out if on_act[m] else dve_out

        fixed = [(ident[:, :], consts["ident"])]
        if nz:
            fixed += [(wz_sb[:, :, :], chunked(wz)), (bz_sb[:, :], rows_of(bz, tk))]
        for i, f in enumerate(fm):
            fixed.append((fm_w[i][:, :, :], chunked(f[0])))
            if f[1] is not None:
                fixed.append((fm_b[i][:, :], f[1].rearrange("(p c) -> p c", p=128)))
        for i, f in enumerate(tm):
            fixed.append((tm_w[i][:, :, :], chunked(f[0])))
            if f[1] is not None:
                fixed.append((tm_b[i][:, :], rows_of(f[1], tk)))
        if roped:
            fixed += [(trig[k][:, :], fm[roped[0]][2][k]) for k in range(2)]

        def by_head(w, i, bank):
            if tm[w][2] < VW:
                return tm_o[w][:, i, :], bank[:tk, :tm[w][2]]
            return (tm_o[w][:, i, :].rearrange("p (h d) -> p h d", h=H)[:, :, 0:HD],
                    bank[:tk, :].rearrange("p (h d) -> p h d", h=H))

        @block.sync
        def _(sp):
            for e in (z_loaded, res_loaded, src_loaded):
                sp.sem_inc(e.sem, e.per)
            for dst, src in fixed:
                sp.dma_start(dst, src).then_inc(w_loaded, 16)
            with sp.Fori(0, steps) as it:
                if nz:
                    sp.wait_ge(y_ready.sem, y_ready.before(it))
                    sp.nop(nofuse=True)
                    for i, src in enumerate(zs):
                        for a in range(nt):
                            sp.dma_start(z_sb[i][:, a, :].rearrange("p (g d) -> p g d", g=C) if src[0] else z_sb[i][:, a, :],
                                         src[1](it, a)).then_inc(z_loaded.sem, 16)
                if res is not None:
                    sp.wait_ge(y_ready.sem, y_ready.before(it))
                    sp.dma_start(res_sb[:, :, :], res(it)).then_inc(res_loaded.sem, 16)
                if y_in is not None:
                    sp.wait_ge(mm_done.sem, mm_done.before(it, place[("tpy", 0, nt - 1)] + 1))
                    sp.nop(nofuse=True)
                    sp.dma_start(y[:, :, :], y_in(it)).then_inc(src_loaded.sem, 16)
                if xT is not None:
                    sp.wait_ge(mm_done.sem, mm_done.before(it))
                    sp.nop(nofuse=True)
                    sp.dma_start(yT[:, :, :], xT(it)).then_inc(src_loaded.sem, 16)

        @block.gpsimd
        def _(pool):
            pool.memset(eps[:, :], EPS).then_inc(eps_set, 1)
            for i, f in enumerate(tm):
                if f[2] == VW:
                    pool.memset(tm_o[i][:, :, :], 1.0).then_inc(eps_set, 1)
            for e in (y_free, fm_free, tm_free):
                pool.sem_inc(e.sem, e.per)
            with pool.Fori(0, steps) as it:
                if y_out is not None:
                    pool.wait_ge(y_ready.sem, y_ready.now(it, nt))
                    pool.nop(nofuse=True)
                    pool.dma_start(y_out(it), y[:, :, :]).then_inc(y_stored.sem, 16)
                for i in stored_fm:
                    if i in split:
                        k = split.index(i)
                        pool.wait_ge(part_dve.sem, part_dve.now(it, 2 * k + 2))
                        pool.nop(nofuse=True)
                        for part, dst in zip(parts[i], fm[i][4]):
                            pool.dma_start(dst(it), part[:, :, :]).then_inc(fm_stored.sem, 16)
                        continue
                    if i in roped:
                        pool.wait_ge(rope_ready.sem, rope_ready.now(it, rope_ready.per))
                        pool.nop(nofuse=True)
                    else:
                        m = place[("fm", i, (C - 1, ncol - 1))]
                        pool.wait_ge(dve_out.sem, dve_out.now(it, nth(m)))
                        pool.nop(nofuse=True)
                    pool.dma_start(fm[i][4](it), fm_o[i][:, :, :]).then_inc(fm_stored.sem, 16)
                for i in range(len(tm)):
                    for a in range(nt):
                        m = place[("tm", i, a)]
                        pool.wait_ge(out_of(m).sem, out_of(m).now(it, nth(m)))
                        src = tm_o[i][:, a, :]
                        if tm[i][2] >= D:
                            src = src.rearrange("p (g d) -> p g d", g=C)
                        pool.dma_start(tm[i][3](it, a), src).then_inc(tm_stored.sem, 16)
                if y_out is not None:
                    pool.wait_ge(y_stored.sem, y_stored.now(it, 16))
                    pool.sem_inc(y_free.sem, 1)
                if stored_fm:
                    pool.wait_ge(fm_stored.sem, fm_stored.now(it, fm_stored.per))
                    pool.sem_inc(fm_free.sem, 1)
                if tm:
                    pool.wait_ge(tm_stored.sem, tm_stored.now(it, tm_stored.per))
                    pool.sem_inc(tm_free.sem, 1)

        @block.tensor
        def _(pe):
            pe.sem_inc(mm_done.sem, NJ)
            pe.wait_ge(w_loaded, 16 * len(fixed))
            with pe.Fori(0, steps) as it:
                for m, (kind, w, i) in enumerate(jobs):
                    bank = ring[m % RING]
                    if m >= RING:
                        e = out_of(m - RING)
                        pe.wait_ge(e.sem, e.now(it, nth(m - RING)))
                    else:
                        k = max(k for k in range(NJ) if k % RING == m)
                        e = out_of(k)
                        pe.wait_ge(e.sem, e.before(it, nth(k)))
                    if kind == "tpz":
                        if gate and w == 1:
                            pe.wait_ge(mean_ready.sem, mean_ready.now(it, i + 1))
                        else:
                            pe.wait_ge(z_loaded.sem, z_loaded.now(it, z_loaded.per))
                        for c in range(C):
                            ins = nc.tensor.transpose(bank[:, c * tk:(c + 1) * tk],
                                                      z_sb[w][:, i, c * 128:(c + 1) * 128], ident[:tk, :tk])
                    elif kind == "lin":
                        pe.wait_ge(act_out.sem, act_out.now(it, nth(place[("tpz", nz - 1, i)])))
                        for k in range(C * nz):
                            ins = nc.tensor.matmul(bank[:tk, :], zT[k // C][:, k % C, i * tk:(i + 1) * tk],
                                                   wz_sb[:, k, :], start=(k == 0), stop=(k == C * nz - 1))
                    elif kind == "tpy":
                        if y_in is not None:
                            pe.wait_ge(src_loaded.sem, src_loaded.now(it, 16))
                        else:
                            pe.wait_ge(y_ready.sem, y_ready.now(it, i + 1))
                        for c in range(C):
                            ins = nc.tensor.transpose(bank[:, c * tk:(c + 1) * tk],
                                                      y[:, i, c * 128:(c + 1) * 128], ident[:tk, :tk])
                    else:
                        if xT is not None:
                            pe.wait_ge(src_loaded.sem, src_loaded.now(it, 16))
                        else:
                            pe.wait_ge(act_out.sem, act_out.now(it, nth(place[("tpy", 0, nt - 1)])))
                        if kind == "fm":
                            c, s = i
                            whole = fm[w][0].shape[0] == D
                            for k in range(C) if whole else [c]:
                                lhsT = fm_w[w][:, k, c * 128:(c + 1) * 128] if whole else fm_w[w][:, 0, :]
                                ins = nc.tensor.matmul(bank[:, :cols], lhsT, yT[:, k, s * cols:(s + 1) * cols],
                                                       start=(k == 0 or not whole), stop=(k == C - 1 or not whole))
                        elif tm[w][0].shape[0] == 128:
                            for k in range(C):
                                ins = nc.tensor.matmul(bank[:tk, k * 128:(k + 1) * 128],
                                                       yT[:, k, i * tk:(i + 1) * tk], tm_w[w][:, 0, :],
                                                       start=True, stop=True)
                        else:
                            for k in range(C):
                                ins = nc.tensor.matmul(bank[:tk, :min(D, tm[w][2])], yT[:, k, i * tk:(i + 1) * tk],
                                                       tm_w[w][:, k, :], start=(k == 0), stop=(k == C - 1))
                    ins.then_inc(mm_done.sem, 1)

        @block.scalar
        def _(act):
            for e in (act_out, std_ready, gate_ready, part_act):
                act.sem_inc(e.sem, e.per)
            n_set = 1 + sum(f[2] == VW for f in tm)
            act.wait_ge(eps_set, n_set)
            with act.Fori(0, steps) as it:
                for m, (kind, w, i) in enumerate(jobs):
                    bank = ring[m % RING]
                    if kind in ("tpz", "tpy"):
                        act.wait_ge(mm_done.sem, mm_done.now(it, m + 1))
                        dst = zT[w] if kind == "tpz" else yT
                        nc.scalar.activation(dst[:, :, i * tk:(i + 1) * tk],
                                             bank[:, :C * tk].rearrange("p (c t) -> p c t", c=C),
                                             ACT.Copy).then_inc(act_out.sem, 1)
                    elif on_act[m]:
                        if i == 0:
                            act.wait_ge(tm_free.sem, tm_free.before(it))
                        act.wait_ge(mm_done.sem, mm_done.now(it, m + 1))
                        dst, src = by_head(w, i, bank)
                        nc.scalar.activation(dst, src, ACT.Copy).then_inc(act_out.sem, 1)
                    elif kind == "lin" and gate:
                        act.wait_ge(dve_out.sem, dve_out.now(it, nth(m)))
                        nc.scalar.activation(t[:, i, :], t[:, i, :], ACT.Sigmoid).then_inc(gate_ready.sem, 1)
                    if norm and kind == "lin" and i == nt - 1:
                        act.wait_ge(var_ready.sem, var_ready.now(it, nt))
                        nc.scalar.activation(std[:, :], mv[:, :, 1], ACT.Sqrt, bias=eps[:tk, :]).then_inc(std_ready.sem, 1)
                for k, i in enumerate(split):
                    if i in roped:
                        act.wait_ge(rope_ready.sem, rope_ready.now(it, rope_ready.per))
                    else:
                        act.wait_ge(dve_out.sem, dve_out.now(it, nth(place[("fm", i, (C - 1, ncol - 1))])))
                    if k == 0:
                        act.wait_ge(fm_free.sem, fm_free.before(it))
                    nc.scalar.activation(parts[i][0][:, :, :], fm_o[i][:, :, :], ACT.Copy).then_inc(part_act.sem, 1)
                    act.wait_ge(part_dve.sem, part_dve.now(it, 2 * k + 1))
                    nc.scalar.activation(parts[i][1][:, :, :], fm_o[i][:, :, :], ACT.Copy).then_inc(part_act.sem, 1)

        per = (nt if gate else 0) + (3 * nt if gate else 0) + (nt if res is not None else 0) \
            + (nt + 1 if norm else 0)

        @block.vector
        def _(dve):
            for e in (dve_out, y_ready, var_ready, mean_ready, rope_ready, part_dve):
                dve.sem_inc(e.sem, e.per)
            dve.wait_ge(w_loaded, 16 * len(fixed))
            dve.wait_ge(eps_set, 1 + sum(f[2] == VW for f in tm))
            with dve.Fori(0, steps) as it:
                own = Chain(dve, dve_step, it, per)
                if gate:
                    dve.wait_ge(z_loaded.sem, z_loaded.now(it, z_loaded.per))
                    for a in range(nt):
                        own.done(nc.vector.tensor_tensor(z_sb[1][:, a, :], z_sb[1][:, a, :], z_sb[2][:, a, :], ALU.add))
                    for a in range(nt):
                        dve.wait_ge(dve_step, own.it * own.per + a + 1)
                        nc.vector.tensor_scalar(z_sb[1][:, a, :], z_sb[1][:, a, :], 0.5, None,
                                                ALU.mult).then_inc(mean_ready.sem, 1)
                for m, (kind, w, i) in enumerate(jobs):
                    if on_act[m]:
                        continue
                    bank = ring[m % RING]
                    dve.wait_ge(mm_done.sem, mm_done.now(it, m + 1))
                    if kind == "lin":
                        nc.vector.tensor_tensor(t[:, i, :], bank[:tk, :], bz_sb[:, :], ALU.add).then_inc(dve_out.sem, 1)
                        if i == 0:
                            if y_out is not None:
                                dve.wait_ge(y_free.sem, y_free.before(it))
                            if res is not None:
                                dve.wait_ge(res_loaded.sem, res_loaded.now(it, 16))
                        if gate:
                            if i == 0:
                                dve.wait_ge(mean_ready.sem, mean_ready.now(it, nt))
                            own.done(nc.vector.tensor_tensor(y[:, i, :], z_sb[1][:, i, :], z_sb[0][:, i, :], ALU.subtract))
                            dve.wait_ge(gate_ready.sem, gate_ready.now(it, i + 1))
                            dve.wait_ge(dve_step, own.last())
                            own.done(nc.vector.tensor_tensor(t[:, i, :], y[:, i, :], t[:, i, :], ALU.mult))
                            dve.wait_ge(dve_step, own.last())
                            own.done(nc.vector.tensor_tensor(t[:, i, :], t[:, i, :], z_sb[0][:, i, :], ALU.add))
                            dve.wait_ge(dve_step, own.last())
                        else:
                            dve.wait_ge(dve_out.sem, dve_out.now(it, nth(m)))
                        if res is not None:
                            own.done(nc.vector.tensor_tensor(t[:, i, :], t[:, i, :], res_sb[:, i, :], ALU.add))
                            dve.wait_ge(dve_step, own.last())
                        if norm:
                            own.done(nc.vector.bn_stats(stats[:, i, :], t[:, i, :]))
                            dve.wait_ge(dve_step, own.last())
                            dve.nop(nofuse=True)
                            nc.vector.bn_aggr(mv[:, i, :], stats[:, i, :]).then_inc(var_ready.sem, 1)
                        else:
                            nc.vector.tensor_copy(y[:, i, :], t[:, i, :]).then_inc(y_ready.sem, 1)
                        if norm and i == nt - 1:
                            dve.wait_ge(std_ready.sem, std_ready.now(it, 1))
                            own.done(nc.vector.reciprocal(rstd[:, :], std[:, :]))
                            dve.wait_ge(dve_step, own.last())
                            for a in range(nt):
                                nc.vector.tensor_scalar(y[:, a, :], t[:, a, :], mv[:, a, 0:1], rstd[:, a:a + 1],
                                                        ALU.subtract, ALU.mult).then_inc(y_ready.sem, 1)
                    elif kind == "fm":
                        c, s = i
                        if c == 0 and s == 0 and w == 0 and stored_fm:
                            dve.wait_ge(fm_free.sem, fm_free.before(it))
                        dst = fm_o[w][:, c, s * cols:(s + 1) * cols]
                        if fm[w][3] is not None:
                            nc.vector.scalar_tensor_tensor(dst, bank[:, :cols], fm_b[w][:, c:c + 1],
                                                           trig[fm[w][3] - 1][:, :], ALU.add, ALU.mult).then_inc(dve_out.sem, 1)
                            if fm[w][3] == 2:
                                dve.wait_ge(dve_out.sem, dve_out.now(it, nth(m)))
                                nc.vector.tensor_tensor(dst, dst, fm_o[w - 1][:, c, :], ALU.add).then_inc(rope_ready.sem, 1)
                        elif fm[w][1] is not None:
                            nc.vector.tensor_scalar(dst, bank[:, :cols], fm_b[w][:, c:c + 1], fm[w][2],
                                                    ALU.add, ALU.mult).then_inc(dve_out.sem, 1)
                        else:
                            nc.vector.tensor_scalar(dst, bank[:, :cols], fm[w][2], None, ALU.mult).then_inc(dve_out.sem, 1)
                    else:
                        if i == 0 and w == 0:
                            dve.wait_ge(tm_free.sem, tm_free.before(it))
                        dst, src = by_head(w, i, bank)
                        b = tm_b[w][:, :]
                        if tm[w][2] == VW:
                            b = b.rearrange("p (h d) -> p h d", h=H)
                        nc.vector.tensor_tensor(dst, src, b, ALU.add).then_inc(dve_out.sem, 1)
                for k, i in enumerate(split):
                    for j in range(2):
                        dve.wait_ge(part_act.sem, part_act.now(it, 2 * k + j + 1))
                        dst = fm_o[i] if j == 0 else parts[i][2]
                        nc.vector.tensor_tensor(dst[:, :, :], fm_o[i][:, :, :], parts[i][j][:, :, :],
                                                ALU.subtract).then_inc(part_dve.sem, 1)
                own.close()


def attention(nc, stage, npast, nk, kt, q, k, v, out, consts, shared=False, mask=None, rpe=None):
    ntk = nk // kt
    nb = 2 if ntk > 4 else 1
    ncb, tpb = nk // nb, ntk // nb
    units = [(u, h, a) for u in range(2) for h in range(4) for a in range(NA)]
    NU = len(units)
    add_bias = mask is not None or rpe is not None
    steps = npast * B * 2
    with ExitStack() as ctx:
        r = Room(nc, ctx, stage)
        ident = r.sb("ident", [128, 128])
        qT = [r.sb(f"qT{u}", [128, T]) for u in range(2)]
        kT = [r.sb(f"kT{u}", [128, nk]) for u in range(2)]
        vs = [r.sb(f"v{u}", [kt, ntk, 128]) for u in range(2)]
        if rpe:
            P = [r.sb(f"P{u}", [TP, NA, 4, nk]) for u in range(2)]
        else:
            P = [r.sb(f"P{i}", [TP, nk]) for i in range(2)]
        PT = [r.sb(f"PT{i}", [kt, ntk, TP]) for i in range(2)]
        Z = [r.sb(f"Z{i}", [TP, nk]) for i in range(2)] if add_bias else None
        nmax, sums, rinv = (r.sb(s, [TP, NU]) for s in ("nmax", "sums", "rinv"))
        o_sb = [r.sb(f"o{u}", [TP, NA, 128]) for u in range(2)]
        S = [r.ps(f"S{i}", [TP, nb, 512]) for i in range(2)]
        PTp = r.ps("PTp", [128, nb, 512])
        O = [r.ps(f"O{i}", [TP, 512]) for i in range(2)]
        if mask is not None:
            mask_sb = r.sb("mask", [TP, NA, nk])
        if rpe:
            tabs_dram, tabv_dram, bands, pband = rpe
            tab = [[r.sb(f"tab{u}{s}", [128, 256]) for s in range(2)] for u in range(2)]
            tabv = [r.sb(f"tabv{u}", [NBUCK, 128]) for u in range(2)]
            far = r.sb("far", [TP, 2, NA, T])
            zero = r.sb("zero", [TP, 2, 287])
            L = [[r.sb(f"L{u}{s}", [TP, NA, 4, 64]) for s in range(2)] for u in range(2)]
            Bias = [[r.sb(f"B{u}{s}", [TP, NA, 4, T]) for s in range(2)] for u in range(2)]
            Bd = [r.sb(f"Bd{u}", [TP, NA, 4, 64]) for u in range(2)]
            bT = [r.sb(f"bT{i}", [64, 4, TP]) for i in range(2)]
            junk = r.sb("junk", [TP, 4, T])
            Lp = [r.ps(f"Lp{i}", [TP, 512]) for i in range(2)]
            Vp = r.ps("Vp", [TP, 512])
        sides = [(u, s, a) for u in range(2) for s in range(2) for a in range(NA)]
        tails = [(u, a) for u in range(2) for a in range(NA)]

        fixed_loaded = r.sem("fixed_loaded")
        q_loaded, k_loaded, v_loaded = (r.event(s, 32) for s in ("q_loaded", "k_loaded", "v_loaded"))
        q_loaded = [r.event(f"qk_loaded{u}", 32 + (32 if rpe else 0)) for u in range(2)]
        v_loaded = [r.event(f"v_loaded{u}", 16 + (16 if rpe else 0)) for u in range(2)]
        s_done = r.event("s_done", NU)
        max_done = r.event("max_done", NU)
        exp_done = r.event("exp_done", NU)
        pt_done = r.event("pt_done", NU)
        pt_act, pt_dve = r.event("pt_act", NU), r.event("pt_dve", NU)
        av_done = r.event("av_done", NU)
        o_done = r.event("o_done", NU)
        out_stored = r.event("out_stored", 32, False)
        out_free = r.event("out_free", 1)
        dve_step = r.sem("dve_step")
        if rpe:
            zeroed, zero_set = r.sem("zeroed"), r.sem("zero_set")
            l_done, l_out = r.event("l_done", 8), r.event("l_out", 8)
            band_stored = [r.event(f"band_stored{u}", 16 * 4, False) for u in range(2)]
            bias_loaded = r.event("bias_loaded", 16 * 8)
            bias_done = r.event("bias_done", 1)
            p_stored = [r.event(f"p_stored{u}", 16 * 2) for u in range(2)]
            pband_loaded = r.event("pband_loaded", 16 * 4)
            tail_done = r.event("tail_done", 4)
            bt_done, bt_out = r.event("bt_done", 4), r.event("bt_out", 4)
            v2_done, v2_out = r.event("v2_done", 4), r.event("v2_out", 4)
        final = v2_out if rpe else o_done
        fin_u = final.per // 2
        block = ctx.enter_context(nc.Block())
        nfixed = 1 + (mask is not None) + (rpe is not None)

        @block.sync
        def _(sp):
            sp.dma_start(ident[:, :], consts["ident"]).then_inc(fixed_loaded, 16)
            if mask is not None:
                sp.dma_start(mask_sb[:, :, :], mask).then_inc(fixed_loaded, 16)
            if rpe:
                sp.dma_start(far[:, :, :, :], consts["far"]).then_inc(fixed_loaded, 16)
                sp.wait_ge(zero_set, 1)
                for buf in [b for side in bands for b in side] + pband:
                    for h in range(4):
                        sp.dma_start(buf[h].rearrange("(p a w) -> p a w", p=TP, a=2), zero[:, :, :]).then_inc(zeroed, 16)
                sp.wait_ge(zeroed, 16 * 4 * 6)
                for e in [bias_loaded, pband_loaded] + p_stored:
                    sp.sem_inc(e.sem, e.per)
            for e in q_loaded + v_loaded:
                sp.sem_inc(e.sem, e.per)

            def step(it, pp, b, h2):
                for u in range(2):
                    g = b * HG + h2 * 2 + u
                    gk = pp * HG + h2 * 2 + u if shared else g
                    sp.wait_ge(av_done.sem, av_done.before(it, NU // 2 * (u + 1)))
                    sp.nop(nofuse=True)
                    sp.dma_start(qT[u][:, :], q[bass.ds(g * 128, 128), :]).then_inc(q_loaded[u].sem, 16)
                    sp.dma_start(kT[u][:, :], k[bass.ds(gk * 128, 128), :]).then_inc(q_loaded[u].sem, 16)
                    if rpe:
                        for s in range(2):
                            sp.dma_start(tab[u][s][:, :], tabs_dram[s][bass.ds((h2 * 2 + u) * 128, 128), :]).then_inc(q_loaded[u].sem, 16)
                        sp.wait_ge(v2_done.sem, v2_done.before(it, 2 * (u + 1)))
                        sp.nop(nofuse=True)
                        sp.dma_start(tabv[u][:, :], tabv_dram[bass.ds((h2 * 2 + u) * NBUCK, NBUCK), :]).then_inc(v_loaded[u].sem, 16)
                    sp.dma_start(vs[u][:, :, :], v[bass.ds(gk, 1), :, :].rearrange("o (t p) d -> p (o t) d", p=kt)).then_inc(v_loaded[u].sem, 16)
                if rpe:
                    for j, (u, s, a) in enumerate(sides):
                        sp.wait_ge(band_stored[u].sem, band_stored[u].now(it, 64))
                        sp.wait_ge(o_done.sem, o_done.before(it))
                        sp.nop(nofuse=True)
                        for_rows = bands[u][s][:, 0:T * PADW].rearrange("h (i w) -> i h w", w=PADW)
                        sp.dma_start(Bias[u][s][:, a, :, :], for_rows[a * TP:(a + 1) * TP, :, HALF:HALF + T]).then_inc(bias_loaded.sem, 16)
                    for j, (u, a) in enumerate(tails):
                        sp.wait_ge(exp_done.sem, exp_done.now(it, NU // 2 * (u + 1)))
                        sp.nop(nofuse=True)
                        rows = pband[u][:, 0:T * PADW].rearrange("h (i w) -> i h w", w=PADW)
                        sp.dma_start(rows[a * TP:(a + 1) * TP, :, HALF:HALF + T], P[u][:, a, :, :]).then_inc(p_stored[u].sem, 16)
                    for j, (u, a) in enumerate(tails):
                        sp.wait_ge(p_stored[u].sem, p_stored[u].now(it, 32))
                        sp.nop(nofuse=True)
                        diag = pband[u][:, :].rearrange("h (i w) -> i h w", w=PADW + 1)
                        sp.wait_ge(bt_done.sem, bt_done.before(it, j + 1))
                        sp.nop(nofuse=True)
                        sp.dma_start(Bd[u][:, a, :, 0:NBUCK], diag[a * TP:(a + 1) * TP, :, 0:NBUCK]).then_inc(pband_loaded.sem, 16)

            if npast > 1:
                with sp.Fori(0, npast) as pp:
                    with sp.Fori(0, B) as b:
                        with sp.Fori(0, 2) as h2:
                            step(pp * (2 * B) + b * 2 + h2, pp, b, h2)
            else:
                with sp.Fori(0, B) as b:
                    with sp.Fori(0, 2) as h2:
                        step(b * 2 + h2, 0, b, h2)

        @block.gpsimd
        def _(pool):
            if rpe:
                pool.memset(zero[:, :, :], 0.0).then_inc(zero_set, 1)
                pool.wait_ge(zeroed, 16 * 4 * 6)
            pool.sem_inc(out_free.sem, 1)

            with pool.Fori(0, steps) as it:
                if rpe:
                    pool.wait_ge(bias_loaded.sem, bias_loaded.before(it))
                    pool.nop(nofuse=True)
                    for j, (u, s, a) in enumerate(sides):
                        pool.wait_ge(l_out.sem, l_out.now(it, j + 1))
                        pool.nop(nofuse=True)
                        diag = bands[u][s][:, :].rearrange("h (i w) -> i h w", w=PADW + 1)
                        pool.dma_start(diag[a * TP:(a + 1) * TP, :, 0:NBUCK], L[u][s][:, a, :, 0:NBUCK]).then_inc(band_stored[u].sem, 16)
                for u in range(2):
                    pool.wait_ge(final.sem, final.now(it, fin_u * (u + 1)))
                    pool.nop(nofuse=True)
                    pool.dma_start(out[bass.ds(it * 2 + u, 1), :, :].rearrange("o (a p) d -> p (o a) d", p=TP),
                                   o_sb[u][:, :, :]).then_inc(out_stored.sem, 16)
                pool.wait_ge(out_stored.sem, out_stored.now(it, 32))
                pool.sem_inc(out_free.sem, 1)

        @block.tensor
        def _(pe):
            for e in (s_done, pt_done, av_done) + ((l_done, bt_done, v2_done) if rpe else ()):
                pe.sem_inc(e.sem, e.per)
            pe.wait_ge(fixed_loaded, 16 * nfixed)

            def scores(it, n):
                u, h, a = units[n]
                if n % 8 == 0:
                    pe.wait_ge(q_loaded[u].sem, q_loaded[u].now(it, q_loaded[u].per))
                if rpe and n == 0:
                    pe.wait_ge(bias_done.sem, bias_done.now(it, 1))
                if n >= 2:
                    pe.wait_ge(exp_done.sem, exp_done.now(it, n - 1))
                else:
                    pe.wait_ge(exp_done.sem, exp_done.before(it, NU - 1 + n))
                rows = slice(32 * h, 32 * h + 32)
                for s in range(nb):
                    ins = nc.tensor.matmul(S[n % 2][:, s, 0:ncb], qT[u][rows, a * TP:(a + 1) * TP],
                                           kT[u][rows, s * ncb:(s + 1) * ncb], start=True, stop=not rpe,
                                           skip_group_check=bool(rpe))
                if rpe:
                    for t in range(NA):
                        ins = nc.tensor.matmul(S[n % 2][:, 0, t * TP:(t + 1) * TP], Bias[u][1][:, t, h, a * TP:(a + 1) * TP],
                                               ident[:TP, :TP], start=False, stop=(t == NA - 1), skip_group_check=True)
                ins.then_inc(s_done.sem, 1)

            def transposes(it, n):
                u, h, a = units[n]
                pe.wait_ge(exp_done.sem, exp_done.now(it, n + 1))
                e_act = pt_act.now(it, n) if n else pt_act.before(it)
                e_dve = pt_dve.now(it, n) if n else pt_dve.before(it)
                pe.wait_ge(pt_act.sem, e_act)
                if nb == 2:
                    pe.wait_ge(pt_dve.sem, e_dve)
                src = P[u][:, a, h, :] if rpe else P[n % 2]
                for t in range(ntk):
                    ins = nc.tensor.transpose(PTp[:kt, t // tpb, (t % tpb) * TP:(t % tpb + 1) * TP],
                                              src[:, t * kt:(t + 1) * kt], ident[:TP, :TP])
                ins.then_inc(pt_done.sem, 1)

            def values(it, n):
                u, h, a = units[n]
                if n % 8 == 0:
                    pe.wait_ge(v_loaded[u].sem, v_loaded[u].now(it, v_loaded[u].per))
                pe.wait_ge(pt_act.sem, pt_act.now(it, n + 1))
                if nb == 2:
                    pe.wait_ge(pt_dve.sem, pt_dve.now(it, n + 1))
                pe.wait_ge(o_done.sem, o_done.now(it, n - 1) if n >= 2 else o_done.before(it, NU - 1 + n))
                for t in range(ntk):
                    ins = nc.tensor.matmul(O[n % 2][:, 0:HD], PT[n % 2][:, t, :], vs[u][:, t, h * HD:(h + 1) * HD],
                                           start=(t == 0), stop=(t == ntk - 1))
                ins.then_inc(av_done.sem, 1)

            with pe.Fori(0, steps) as it:
                if rpe:
                    for j, (u, s, a) in enumerate(sides):
                        if j % 4 == 0:
                            pe.wait_ge(q_loaded[u].sem, q_loaded[u].now(it, q_loaded[u].per))
                        if j >= 2:
                            pe.wait_ge(l_out.sem, l_out.now(it, j - 1))
                        else:
                            pe.wait_ge(bt_out.sem, bt_out.before(it, 3 + j))
                        nc.tensor.matmul(Lp[j % 2][:, 0:256], (qT, kT)[s][u][:, a * TP:(a + 1) * TP], tab[u][s][:, :],
                                         start=True, stop=True).then_inc(l_done.sem, 1)
                scores(it, 0)
                scores(it, 1)
                for n in range(NU):
                    transposes(it, n)
                    if n + 2 < NU:
                        scores(it, n + 2)
                    values(it, n)
                if rpe:
                    for j, (u, a) in enumerate(tails):
                        pe.wait_ge(tail_done.sem, tail_done.now(it, j + 1))
                        pe.wait_ge(l_out.sem, l_out.now(it, 8)) if j < 2 else pe.wait_ge(bt_out.sem, bt_out.now(it, j - 1))
                        pe.nop(nofuse=True)
                        for h in range(4):
                            ins = nc.tensor.transpose(Lp[j % 2][:NBUCK, h * TP:(h + 1) * TP], Bd[u][:, a, h, 0:NBUCK], ident[:TP, :TP])
                        ins.then_inc(bt_done.sem, 1)
                        pe.wait_ge(bt_out.sem, bt_out.now(it, j + 1))
                        pe.wait_ge(v2_out.sem, v2_out.now(it, j) if j else v2_out.before(it))
                        for h in range(4):
                            ins = nc.tensor.matmul(Vp[:, h * HD:(h + 1) * HD], bT[j % 2][:NBUCK, h, :],
                                                   tabv[u][:, h * HD:(h + 1) * HD], start=True, stop=True)
                        ins.then_inc(v2_done.sem, 1)

        @block.scalar
        def _(act):
            for e in (exp_done, pt_act) + ((l_out, bt_out) if rpe else ()):
                act.sem_inc(e.sem, e.per)

            def exponential(it, n):
                u, h, a = units[n]
                act.wait_ge(max_done.sem, max_done.now(it, n + 1))
                if rpe:
                    if n == 0:
                        for e in p_stored:
                            act.wait_ge(e.sem, e.before(it))
                        act.wait_ge(tail_done.sem, tail_done.before(it))
                    dst, src = P[u][:, a, h, :], Z[n % 2][:, :]
                else:
                    act.wait_ge(pt_done.sem, pt_done.now(it, n - 1) if n >= 2 else pt_done.before(it, NU - 1 + n))
                    dst = P[n % 2][:, :].rearrange("p (s c) -> p s c", s=nb)
                    src = Z[n % 2][:, :].rearrange("p (s c) -> p s c", s=nb) if add_bias else S[n % 2][:, :, 0:ncb]
                if n == 0:
                    act.wait_ge(o_done.sem, o_done.before(it))
                nc.scalar.activation(dst, src, ACT.Exp, bias=nmax[:, n:n + 1],
                                     accum_out=sums[:, n:n + 1]).then_inc(exp_done.sem, 1)

            with act.Fori(0, steps) as it:
                if rpe:
                    for j, (u, s, a) in enumerate(sides):
                        act.wait_ge(l_done.sem, l_done.now(it, j + 1))
                        if j == 0:
                            act.wait_ge(bias_done.sem, bias_done.before(it))
                        nc.scalar.activation(L[u][s][:, a, :, 0:NBUCK],
                                             Lp[j % 2][:, 0:256].rearrange("p (h m) -> p h m", h=4)[:, :, 0:NBUCK],
                                             ACT.Copy, scale=1.0 if s == 0 else float(HD ** -0.5)).then_inc(l_out.sem, 1)
                exponential(it, 0)
                exponential(it, 1)
                for n in range(NU):
                    act.wait_ge(pt_done.sem, pt_done.now(it, n + 1))
                    act.wait_ge(av_done.sem, av_done.now(it, n - 1) if n >= 2 else av_done.before(it, NU - 1 + n))
                    nc.scalar.activation(PT[n % 2][:, 0:tpb, :], PTp[:kt, 0, 0:tpb * TP].rearrange("p (t c) -> p t c", t=tpb),
                                         ACT.Copy).then_inc(pt_act.sem, 1)
                    if n + 2 < NU:
                        exponential(it, n + 2)
                if rpe:
                    for j, (u, a) in enumerate(tails):
                        act.wait_ge(bt_done.sem, bt_done.now(it, j + 1))
                        act.wait_ge(v2_done.sem, v2_done.now(it, j - 1) if j >= 2 else v2_done.before(it, 3 + j))
                        nc.scalar.activation(bT[j % 2][:NBUCK, :, :], Lp[j % 2][:NBUCK, 0:4 * TP].rearrange("p (h c) -> p h c", h=4),
                                             ACT.Copy).then_inc(bt_out.sem, 1)

        per = NU * (2 if add_bias else 1) + (64 + 32 + 12 if rpe else 0)

        @block.vector
        def _(dve):
            for e in (max_done, pt_dve, o_done) + ((bias_done, tail_done, v2_out) if rpe else ()):
                dve.sem_inc(e.sem, e.per)
            dve.wait_ge(fixed_loaded, 16 * nfixed)

            def maximum(it, own, n):
                u, h, a = units[n]
                dve.wait_ge(s_done.sem, s_done.now(it, n + 1))
                dve.wait_ge(exp_done.sem, exp_done.now(it, n - 1) if n >= 2 else exp_done.before(it, NU - 1 + n))
                if add_bias:
                    bias = mask_sb[:, a, :] if mask is not None else Bias[u][0][:, a, h, :]
                    own.done(nc.vector.tensor_tensor(Z[n % 2][:, :], S[n % 2][:, 0, 0:nk], bias, ALU.add))
                    dve.wait_ge(dve_step, own.last())
                    src = Z[n % 2][:, :]
                    nc.vector.tensor_reduce(nmax[:, n:n + 1], src, X, ALU.max, negate=True).then_inc(max_done.sem, 1)
                else:
                    nc.vector.tensor_reduce(nmax[:, n:n + 1], S[n % 2][:, :, 0:ncb], mybir.AxisListType.XY, ALU.max,
                                            negate=True).then_inc(max_done.sem, 1)

            beyond = [[(0, TP - HALF), (0, T - HALF)], [(HALF, T), (TP + HALF, T)]]

            with dve.Fori(0, steps) as it:
                own = Chain(dve, dve_step, it, per)
                if rpe:
                    dve.wait_ge(bias_loaded.sem, bias_loaded.now(it, bias_loaded.per))
                    dve.wait_ge(l_out.sem, l_out.now(it, 8))
                    for u, s, a in sides:
                        for h in range(4):
                            for w in range(2):
                                lo, hi = beyond[w][a]
                                m = w * (NBUCK - 1)
                                dst = Bias[u][s][:, a, h, lo:hi]
                                if w:
                                    dve.wait_ge(dve_step, own.last())
                                ins = nc.vector.scalar_tensor_tensor(dst, far[:, w, a, lo:hi], L[u][s][:, a, h, m:m + 1], dst,
                                                                     ALU.mult, ALU.add)
                                own.done(ins)
                    dve.wait_ge(dve_step, own.last())
                    dve.sem_inc(bias_done.sem, 1)
                maximum(it, own, 0)
                maximum(it, own, 1)
                for n in range(NU):
                    u, h, a = units[n]
                    if nb == 2:
                        dve.wait_ge(pt_done.sem, pt_done.now(it, n + 1))
                        dve.wait_ge(av_done.sem, av_done.now(it, n - 1) if n >= 2 else av_done.before(it, NU - 1 + n))
                        nc.vector.tensor_copy(PT[n % 2][:, tpb:, :], PTp[:kt, 1, 0:tpb * TP].rearrange("p (t c) -> p t c", t=tpb)).then_inc(pt_dve.sem, 1)
                    if n + 2 < NU:
                        maximum(it, own, n + 2)
                    dve.wait_ge(exp_done.sem, exp_done.now(it, n + 1))
                    if n == 0 and rpe:
                        dve.wait_ge(v2_out.sem, v2_out.before(it))
                    own.done(nc.vector.reciprocal(rinv[:, n:n + 1], sums[:, n:n + 1]))
                    if n % 8 == 0:
                        dve.wait_ge(out_free.sem, out_free.before(it))
                    dve.wait_ge(dve_step, own.last())
                    dve.wait_ge(av_done.sem, av_done.now(it, n + 1))
                    nc.vector.tensor_scalar(o_sb[u][:, a, h * HD:(h + 1) * HD], O[n % 2][:, 0:HD], rinv[:, n:n + 1], None,
                                            ALU.mult).then_inc(o_done.sem, 1)
                if rpe:
                    dve.wait_ge(pband_loaded.sem, pband_loaded.now(it, pband_loaded.per))
                    for j, (u, a) in enumerate(tails):
                        for h in range(4):
                            for w in range(2):
                                lo, hi = beyond[w][a]
                                m = w * (NBUCK - 1)
                                dve.wait_ge(dve_step, own.last() - 3)
                                ins = nc.vector.tensor_tensor_reduce(
                                    out=junk[:, own.n % 4, lo:hi], in0=P[u][:, a, h, lo:hi], in1=far[:, w, a, lo:hi], scale=1.0,
                                    scalar=Bd[u][:, a, h, m:m + 1], op0=ALU.mult, op1=ALU.add, accum_out=Bd[u][:, a, h, m:m + 1])
                                own.done(ins)
                        dve.wait_ge(dve_step, own.last())
                        dve.sem_inc(tail_done.sem, 1)
                    for j, (u, a) in enumerate(tails):
                        dve.wait_ge(v2_done.sem, v2_done.now(it, j + 1))
                        if j == 0:
                            dve.wait_ge(o_done.sem, o_done.now(it, NU))
                        for h in range(4):
                            dst = o_sb[u][:, a, h * HD:(h + 1) * HD]
                            n = units.index((u, h, a))
                            ins = nc.vector.scalar_tensor_tensor(dst, Vp[:, h * HD:(h + 1) * HD], rinv[:, n:n + 1], dst, ALU.mult, ALU.add)
                            if h < 3:
                                own.done(ins)
                        ins.then_inc(v2_out.sem, 1)
                own.close()


class Flow:

    def __init__(self, sem, k):
        self.sem, self.k = sem, k

    def at(self, it, n, j):
        return it * (8 * self.k) + ((n + 8) * self.k + j)


def split_attention(nc, stage, npast, nk, kt, q, k, v, out, consts, shared=False, mask=None):
    nt = nk // kt
    nb = 2 if nk > 512 else 1
    ncb = nk // nb
    chunks = [list(range(c, min(c + 4, nt))) for c in range(0, nt, 4)]
    NC = len(chunks)
    steps = npast * B * 2
    V1 = HD + 1
    with ExitStack() as ctx:
        r = Room(nc, ctx, stage)
        identb = r.sb("identb", [128, 128], BF16)
        Q = [[r.sb(f"Q{u}{s}", [128, 4, T], BF16) for s in range(2)] for u in range(2)]
        K = [[r.sb(f"K{u}{s}", [128, 4, nk], BF16) for s in range(2)] for u in range(2)]
        V = [r.sb(f"V{u}", [kt, nt, 4, V1]) for u in range(2)]
        PT = [r.sb(f"PT{i}", [kt, nt, T]) for i in range(2)]
        nmax = [r.sb(f"nmax{i}", [TP, NA]) for i in range(2)]
        shift = [r.sb(f"shift{i}", [TP, NA, 2], BF16) for i in range(2)]
        rinv = r.sb("rinv", [TP, 2, NA])
        OT = [r.sb(f"OT{i}", [128, TP]) for i in range(2)]
        o_sb = [r.sb(f"o{u}", [TP, NA, 128]) for u in range(2)]
        S = r.ps("S", [TP, nb, 512])
        ST = [r.ps(f"ST{c}", [kt, (len(ts) + 1) // 2, 512]) for c, ts in enumerate(chunks)]
        if NC == 1:
            ST = [ST[0], r.ps("ST1", [kt, 1, 512])]
        O = r.ps("O", [128, 512])
        R = r.ps("R", [128, 1024], BF16)
        Oq = R[:, 512:1024].bitcast(FP32)
        if mask is not None:
            mask_f = r.sb("mask_f", [TP, NA, nk])
            maskT_f = r.sb("maskT_f", [kt, nt, T])
            mask_q, mask_k = r.sb("mask_q", [TP, NA, nk], BF16), r.sb("mask_k", [kt, nt, T], BF16)
        ident = r.sb("ident", [128, 128])
        fixed_loaded, fixed_made, ones_set = r.sem("fixed_loaded"), r.sem("fixed_made"), r.sem("ones_set")
        qk_loaded = [r.event(f"qk_loaded{u}", 16 * 12) for u in range(2)]
        v_loaded = [r.event(f"v_loaded{u}", 16) for u in range(2)]
        s_done = Flow(r.sem("s_done"), NA)
        max_done = Flow(r.sem("max_done"), NA)
        shift_done = Flow(r.sem("shift_done"), 1)
        row_done = Flow(r.sem("row_done"), 1)
        row_out = Flow(r.sem("row_out"), 1)
        st_done = Flow(r.sem("st_done"), NC)
        exp_done = Flow(r.sem("exp_done"), NC)
        av_done = Flow(r.sem("av_done"), 1)
        ot_out = Flow(r.sem("ot_out"), NA)
        o_done = Flow(r.sem("o_done"), 1)
        o_out = Flow(r.sem("o_out"), 1)
        cast_done, rinv_done = Flow(r.sem("cast_done"), 1), Flow(r.sem("rinv_done"), 1)
        out_stored = [r.event(f"out_stored{u}", 16, False) for u in range(2)]
        out_free = [r.event(f"out_free{u}", 1) for u in range(2)]
        block = ctx.enter_context(nc.Block())
        n_fixed = 1 + 2 * (mask is not None)

        @block.sync
        def _(sp):
            sp.dma_start(ident[:, :], consts["ident"]).then_inc(fixed_loaded, 16)
            if mask is not None:
                sp.dma_start(mask_f[:, :, :], mask[0]).then_inc(fixed_loaded, 16)
                sp.dma_start(maskT_f[:, :, :], mask[1]).then_inc(fixed_loaded, 16)
            for e in qk_loaded + v_loaded:
                sp.sem_inc(e.sem, e.per)

            def step(it, pp, b, h2):
                for u in range(2):
                    g = b * HG + h2 * 2 + u
                    gk = pp * HG + h2 * 2 + u if shared else g
                    sp.wait_ge(st_done.sem, st_done.at(it, 4 * u + 3 - 8, NC))
                    sp.nop(nofuse=True)
                    for which, (src, dst, row) in enumerate(((q, Q[u], g), (k, K[u], gk))):
                        order = ((0, 0, 1), (1, 0, 2)) if which == 0 else ((0, 1, 0), (1, 2, 0))
                        for s in range(2):
                            for j in range(3):
                                part = src[order[s][j]]
                                sp.dma_start(dst[s][32 * j:32 * j + 32, :, :],
                                             part[bass.ds(row * 128, 128), :].rearrange("(h p) t -> p h t", p=32)
                                             ).then_inc(qk_loaded[u].sem, 16)
                    sp.wait_ge(av_done.sem, av_done.at(it, 4 * u + 3 - 8, 1))
                    sp.nop(nofuse=True)
                    sp.dma_start(V[u][:, :, :, :], v[bass.ds(gk, 1), :, :].rearrange("o (t p) (h d) -> p (o t) h d", p=kt, h=4)
                                 ).then_inc(v_loaded[u].sem, 16)

            if npast > 1:
                with sp.Fori(0, npast) as pp:
                    with sp.Fori(0, B) as b:
                        with sp.Fori(0, 2) as h2:
                            step(pp * (2 * B) + b * 2 + h2, pp, b, h2)
            else:
                with sp.Fori(0, B) as b:
                    with sp.Fori(0, 2) as h2:
                        step(b * 2 + h2, 0, b, h2)

        @block.gpsimd
        def _(pool):
            for u in range(2):
                pool.memset(K[u][1][96:98, :, :], 1.0).then_inc(ones_set, 1)
                pool.sem_inc(out_free[u].sem, 1)
            with pool.Fori(0, steps) as it:
                for u in range(2):
                    pool.wait_ge(o_out.sem, o_out.at(it, 4 * u + 3, 1))
                    pool.nop(nofuse=True)
                    pool.dma_start(out[bass.ds(it * 2 + u, 1), :, :].rearrange("o (a p) d -> p (o a) d", p=TP),
                                   o_sb[u][:, :, :]).then_inc(out_stored[u].sem, 16)
                    pool.wait_ge(out_stored[u].sem, out_stored[u].now(it, 16))
                    pool.sem_inc(out_free[u].sem, 1)

        @block.tensor
        def _(pe):
            for f in (s_done, row_done, st_done, av_done, o_done):
                pe.sem_inc(f.sem, 8 * f.k)
            pe.wait_ge(fixed_made, n_fixed)
            pe.wait_ge(ones_set, 4)

            def scores(it, n, a):
                u, h = n // 4 % 2, n % 4
                if h == 0 and a == 0:
                    e = qk_loaded[u]
                    pe.wait_ge(e.sem, e.now(it, e.per + (e.per if n == 8 else 0)))
                pe.wait_ge(max_done.sem, max_done.at(it, n if a else n - 1, 1 if a else NA))
                for s in range(nb):
                    ins = nc.tensor.matmul(S[:, s, 0:ncb], Q[u][0][0:96, h, a * TP:(a + 1) * TP],
                                           K[u][0][0:96, h, s * ncb:(s + 1) * ncb], start=True, stop=mask is None)
                if mask is not None:
                    ins = nc.tensor.matmul(S[:, 0, 0:nk], identb[:TP, :TP], mask_q[:, a, :], start=False, stop=True)
                ins.then_inc(s_done.sem, 1)

            def rows_of_max(it, n, first=False):
                pe.wait_ge(shift_done.sem, shift_done.at(it, n, 1))
                pe.wait_ge(row_out.sem, row_out.at(it, n - 1, 1))
                if n >= 3 or not first:
                    pe.wait_ge(o_out.sem, o_out.at(it, n - 3, 1))
                for a in range(NA):
                    ins = nc.tensor.transpose(R[96:98, a * TP:(a + 1) * TP], shift[n % 2][:, a, :], identb[:TP, :TP])
                ins.then_inc(row_done.sem, 1)

            def scores_T(it, n, c):
                u, h = n // 4, n % 4
                bank = ST[c if NC > 1 else n % 2]
                if c == 0:
                    pe.wait_ge(row_out.sem, row_out.at(it, n, 1))
                pe.wait_ge(exp_done.sem, exp_done.at(it, n - 1, c + 1) if NC > 1 else exp_done.at(it, n - 2, 1))
                for i, t in enumerate(chunks[c]):
                    dst = bank[:, i // 2, i % 2 * T:(i % 2 + 1) * T]
                    nc.tensor.matmul(dst, K[u][0][0:96, h, t * kt:(t + 1) * kt], Q[u][0][0:96, h, :], start=True, stop=False)
                    if mask is not None:
                        nc.tensor.matmul(dst, identb[:kt, :kt], mask_k[:, t, :], start=False, stop=False)
                    ins = nc.tensor.matmul(dst, K[u][1][0:98, h, t * kt:(t + 1) * kt], Q[u][1][0:98, h, :], start=False, stop=True)
                ins.then_inc(st_done.sem, 1)

            def values(it, n, part):
                u, h = n // 4 % 2, n % 4
                if part == 0:
                    if h == 0:
                        pe.wait_ge(v_loaded[u].sem, v_loaded[u].now(it, 16))
                    pe.wait_ge(exp_done.sem, exp_done.at(it, n, NC))
                    pe.wait_ge(ot_out.sem, ot_out.at(it, n - 1, NA))
                for t in range(nt)[part * nt // 2:(part + 1) * nt // 2]:
                    for a in range(NA):
                        ins = nc.tensor.matmul(O[64 * a:64 * a + V1, 0:TP], V[u][:, t, h, :], PT[n % 2][:, t, a * TP:(a + 1) * TP],
                                               start=(t == 0), stop=(t == nt - 1))
                if part == 1:
                    ins.then_inc(av_done.sem, 1)

            def turned_back(it, n, last=False):
                pe.wait_ge(ot_out.sem, ot_out.at(it, n, NA))
                pe.wait_ge(row_out.sem, row_out.at(it, min(n + 2, 7) if last else n + 2, 1))
                pe.wait_ge(o_out.sem, o_out.at(it, n - 1, 1))
                nc.tensor.transpose(Oq[:TP, 0:128], OT[n % 2][:, :], ident[:, :]).then_inc(o_done.sem, 1)

            def body(it, first, last):
                for n in range(8):
                    more = not (last and n == 7)
                    if more:
                        scores(it, n + 1, 0)
                    if not (first and n < 2):
                        turned_back(it, n - 2, last)
                    scores_T(it, n, 0)
                    if more:
                        scores(it, n + 1, 1)
                    if NC > 1:
                        scores_T(it, n, 1)
                    if not (first and n == 0):
                        values(it, n - 1, 0)
                    if more:
                        rows_of_max(it, n + 1, first)
                    if not (first and n == 0):
                        values(it, n - 1, 1)
                if last:
                    turned_back(it, 6, True)
                    values(it, 7, 0)
                    values(it, 7, 1)
                    turned_back(it, 7, True)

            for a in range(NA):
                scores(0, 0, a)
            rows_of_max(0, 0, True)
            body(0, True, False)
            with pe.Fori(1, steps - 1) as it:
                body(it, False, False)
            body(steps - 1, False, True)

        @block.scalar
        def _(act):
            act.sem_inc(exp_done.sem, 8 * exp_done.k)
            act.sem_inc(ot_out.sem, 8 * ot_out.k)
            act.wait_ge(ones_set, 4)

            def exponential(it, n, c):
                act.wait_ge(st_done.sem, st_done.at(it, n, c + 1))
                ts = chunks[c]
                bank = ST[c if NC > 1 else n % 2]
                full = len(ts) // 2
                dst = PT[n % 2][:, ts[0]:ts[0] + 2 * full, :].rearrange("p (b t) q -> p b (t q)", t=2)
                ins = nc.scalar.activation(dst, bank[:, 0:full, 0:2 * T], ACT.Exp)
                assert len(ts) % 2 == 0
                ins.then_inc(exp_done.sem, 1)

            def take_OT(it, n):
                act.wait_ge(av_done.sem, av_done.at(it, n, 1))
                act.wait_ge(o_done.sem, o_done.at(it, n - 2, 1))
                for a in range(NA):
                    nc.scalar.activation(OT[n % 2][64 * a:64 * a + V1, :], O[64 * a:64 * a + V1, 0:TP],
                                         ACT.Copy).then_inc(ot_out.sem, 1)

            def body(it, first, last):
                for n in range(8):
                    for c in range(NC):
                        exponential(it, n, c)
                    if not (first and n == 0):
                        take_OT(it, n - 1)
                if last:
                    take_OT(it, 7)

            body(0, True, False)
            with act.Fori(1, steps - 1) as it:
                body(it, False, False)
            body(steps - 1, False, True)

        @block.vector
        def _(dve):
            for f in (max_done, shift_done, row_out, o_out, cast_done, rinv_done):
                dve.sem_inc(f.sem, 8 * f.k)
            dve.wait_ge(fixed_loaded, 16 * n_fixed)
            for i in range(2):
                nc.vector.memset(OT[i][:, :], 0.0).then_inc(ones_set, 1)
            nc.vector.tensor_copy(identb[:, :], ident[:, :]).then_inc(fixed_made, 1)
            if mask is not None:
                nc.vector.tensor_copy(mask_q[:, :, :], mask_f[:, :, :]).then_inc(fixed_made, 1)
                nc.vector.tensor_copy(mask_k[:, :, :], maskT_f[:, :, :]).then_inc(fixed_made, 1)

            def maximum(it, n, a):
                if a == 0:
                    dve.wait_ge(shift_done.sem, shift_done.at(it, n - 2, 1))
                dve.wait_ge(s_done.sem, s_done.at(it, n, a + 1))
                nc.vector.tensor_reduce(nmax[n % 2][:, a:a + 1], S[:, :, 0:ncb], mybir.AxisListType.XY if nb > 1 else X, ALU.max,
                                        negate=True).then_inc(max_done.sem, 1)

            def shifts(it, n):
                dve.wait_ge(max_done.sem, max_done.at(it, n, NA))
                dve.wait_ge(row_done.sem, row_done.at(it, n - 2, 1))
                nc.vector.tensor_copy(shift[n % 2][:, :, 0], nmax[n % 2][:, :]).then_inc(cast_done.sem, 1)
                dve.wait_ge(cast_done.sem, cast_done.at(it, n, 1))
                nc.vector.tensor_tensor(shift[n % 2][:, :, 1], nmax[n % 2][:, :], shift[n % 2][:, :, 0],
                                        ALU.subtract).then_inc(shift_done.sem, 1)

            def into_stack(it, n):
                u, h = n // 4 % 2, n % 4
                dve.wait_ge(row_done.sem, row_done.at(it, n, 1))
                nc.vector.tensor_copy(Q[u][1][96:98, h, :], R[96:98, 0:T]).then_inc(row_out.sem, 1)

            def outputs(it, n):
                u, h = n // 4 % 2, n % 4
                dve.wait_ge(o_done.sem, o_done.at(it, n, 1))
                dve.wait_ge(o_out.sem, o_out.at(it, n - 1, 1))
                both = Oq[:TP, 0:128].rearrange("p (a d) -> p a d", a=NA)
                nc.vector.reciprocal(rinv[:, n % 2, :], both[:, :, HD]).then_inc(rinv_done.sem, 1)
                if h == 0:
                    dve.wait_ge(out_free[u].sem, out_free[u].before(it))
                dve.wait_ge(rinv_done.sem, rinv_done.at(it, n, 1))
                nc.vector.tensor_tensor(o_sb[u][:, :, h * HD:(h + 1) * HD], both[:, :, 0:HD],
                                        rinv[:, n % 2, :].unsqueeze(2).broadcast_to([TP, NA, HD]), ALU.mult).then_inc(o_out.sem, 1)

            def body(it, first, last):
                for n in range(8):
                    more = not (last and n == 7)
                    if more:
                        maximum(it, n + 1, 0)
                    if not (first and n < 2):
                        outputs(it, n - 2)
                    if more:
                        maximum(it, n + 1, 1)
                        shifts(it, n + 1)
                        into_stack(it, n + 1)
                if last:
                    outputs(it, 6)
                    outputs(it, 7)

            for a in range(NA):
                maximum(0, 0, a)
            shifts(0, 0)
            into_stack(0, 0)
            body(0, True, False)
            with dve.Fori(1, steps - 1) as it:
                body(it, False, False)
            body(steps - 1, False, True)


def route(nc, stage, first_layer, logits, cap, consts, table, slots, weights):
    NT, NB = NTOK // 128, (2 if first_layer else 1) * (NTOK // 128)
    OUT = 16384.0
    with ExitStack() as ctx:
        r = Room(nc, ctx, stage)
        lg, gates = r.sb("lg", [128, NT, NE]), r.sb("gates", [128, NT, NE])
        top, topi = r.sb("top", [128, NT, NE]), r.sb("topi", [128, NT, NE], U32)
        topf = r.sb("topf", [128, NT, NE])
        m, s = r.sb("m", [128, NT]), r.sb("s", [128, NT])
        iota, tri, ones = r.sb("iota", [128, NT, NE]), r.sb("tri", [128, 128]), r.sb("ones", [128, 128])
        tok = r.sb("tok", [128, NT], U32)
        hot = r.sb("hot", [128, 2, NT, NE])
        both = r.sb("both", [128, 2, NT, NE])
        pre = r.sb("pre", [128, NB + 1, NE])
        rank = r.sb("rank", [128, 2, NT, NE])
        place, ok, slot = r.sb("place", [128, 2, NT]), r.sb("ok", [128, 2, NT]), r.sb("slot", [128, 2, NT])
        sc_f, sc_i = r.sb("sc_f", [128, 2, NT]), r.sb("sc_i", [128, 2, NT], U32)
        ga_i = r.sb("ga_i", [128, NT, 2], U32)
        wt = r.sb("wt", [128, NT, 2])
        zero = r.sb("zero", [112, NE * cap // 112], U32)
        pos = r.ps("pos", [128, NB, NE])
        loaded, zero_set, zeroed, counted = (r.sem(x) for x in ("loaded", "zero_set", "zeroed", "counted"))
        dve_step, exp_in, exp_out, hot_ready = (r.sem(x) for x in ("dve_step", "exp_in", "exp_out", "hot_ready"))
        ready, scattered, kept = r.sem("ready"), r.sem("scattered"), r.sem("kept")
        block = ctx.enter_context(nc.Block())

        @block.sync
        def _(sp):
            sp.dma_start(lg[:, :, :], logits.rearrange("(t p) e -> p t e", p=128)).then_inc(loaded, 16)
            sp.dma_start(iota[:, :, :], consts["iota"]).then_inc(loaded, 16)
            sp.dma_start(tri[:, :], consts["tri"]).then_inc(loaded, 16)
            sp.dma_start(tok[:, :], consts["tok"]).then_inc(loaded, 16)
            sp.wait_ge(zero_set, 1)
            sp.dma_start(table.rearrange("(p n) o -> p (n o)", p=112), zero[:, :]).then_inc(zeroed, 16)
            sp.wait_ge(ready, 1)
            sp.dma_start(slots.rearrange("t p k -> p t k"), ga_i[:, :, :]).then_inc(kept, 16)
            sp.dma_start(weights.rearrange("t p k -> p t k"), wt[:, :, :]).then_inc(kept, 16)
            sp.wait_ge(kept, 32)

        @block.gpsimd
        def _(pool):
            pool.memset(zero[:, :], 0).then_inc(zero_set, 1)
            pool.memset(ones[:, :], 1.0).then_inc(zero_set, 1)
            pool.wait_ge(zeroed, 16)
            pool.wait_ge(ready, 1)
            for k in range(2):
                for t in range(NT):
                    pool.indirect_dma_start(out=table, out_offset=bass.IndirectOffsetOnAxis(ap=sc_i[:, k, t:t + 1], axis=0),
                                            in_=tok[:, t:t + 1], in_offset=None, bounds_check=NE * cap - 1,
                                            oob_is_err=False).then_inc(scattered, 16)
            pool.wait_ge(scattered, 16 * 2 * NT)

        @block.tensor
        def _(pe):
            pe.wait_ge(zero_set, 2)
            pe.wait_ge(hot_ready, 1)
            src = hot[:, :, :, :].rearrange("p k t e -> p (k t e)") if first_layer else both[:, 0, :, :].rearrange("p t e -> p (t e)")
            out = pos[:, :, :].rearrange("p t e -> p (t e)")
            nc.tensor.matmul(out, tri[:, :], src, start=True, stop=False)
            nc.tensor.matmul(out, ones[:, :], pre[:, 0:NB, :].rearrange("p t e -> p (t e)"), start=False, stop=True).then_inc(counted, 1)

        @block.scalar
        def _(act):
            act.wait_ge(exp_in, 1)
            src = s[:, :] if first_layer else gates[:, :, :]
            nc.scalar.activation(src, src, ACT.Exp).then_inc(exp_out, 1)

        @block.vector
        def _(dve):
            step = [0]

            def then(ins):
                ins.then_inc(dve_step, 1)
                step[0] += 1
                dve.wait_ge(dve_step, step[0])

            dve.wait_ge(loaded, 64)
            if first_layer:
                chosen = lg
            else:
                then(nc.vector.tensor_reduce(m[:, :], lg[:, :, :], X, ALU.max))
                nc.vector.tensor_tensor(gates[:, :, :], lg[:, :, :], m[:, :].unsqueeze(2).broadcast_to([128, NT, NE]),
                                        ALU.subtract).then_inc(exp_in, 1)
                dve.wait_ge(exp_out, 1)
                then(nc.vector.tensor_reduce(s[:, :], gates[:, :, :], X, ALU.add))
                then(nc.vector.reciprocal(m[:, :], s[:, :]))
                then(nc.vector.tensor_tensor(gates[:, :, :], gates[:, :, :], m[:, :].unsqueeze(2).broadcast_to([128, NT, NE]), ALU.mult))
                chosen = gates
            for t in range(NT):
                then(nc.vector.max(top[:, t, :], chosen[:, t, :]))
                then(nc.vector.max_index(topi[:, t, :], top[:, t, :], chosen[:, t, :]))
            then(nc.vector.tensor_copy(topf[:, :, :], topi[:, :, :]))
            for k in range(2):
                then(nc.vector.tensor_tensor(hot[:, k, :, :], iota[:, :, :], topf[:, :, k:k + 1].broadcast_to([128, NT, NE]), ALU.is_equal))
            if not first_layer:
                then(nc.vector.tensor_tensor(both[:, 0, :, :], hot[:, 0, :, :], hot[:, 1, :, :], ALU.add))
            blocks = [hot[:, j // NT, j % NT, :] if first_layer else both[:, 0, j, :] for j in range(NB)]
            then(nc.vector.memset(pre[:, 0, :], 0.0))
            for j in range(NB):
                ins = nc.vector.tensor_tensor(pre[:, j + 1, :], pre[:, j, :], blocks[j], ALU.add)
                if j < NB - 1:
                    then(ins)
            ins.then_inc(hot_ready, 1)
            if first_layer:
                nc.vector.tensor_tensor(s[:, :], top[:, :, 1], top[:, :, 0], ALU.subtract).then_inc(exp_in, 1)
                dve.wait_ge(exp_out, 1)
                then(nc.vector.tensor_scalar(m[:, :], s[:, :], 1.0, None, ALU.add))
                then(nc.vector.reciprocal(wt[:, :, 0], m[:, :]))
                then(nc.vector.tensor_tensor(wt[:, :, 1], s[:, :], wt[:, :, 0], ALU.mult))
            else:
                then(nc.vector.tensor_copy(wt[:, :, :], top[:, :, 0:2]))
            dve.wait_ge(counted, 1)
            for k in range(2):
                p = pos[:, k * NT:(k + 1) * NT, :] if first_layer else pos[:, :, :]
                then(nc.vector.tensor_tensor(rank[:, k, :, :], p, hot[:, k, :, :], ALU.mult))
                then(nc.vector.tensor_reduce(place[:, k, :], rank[:, k, :, :], X, ALU.add))
            then(nc.vector.tensor_scalar(place[:, :, :], place[:, :, :], -1.0, None, ALU.add))
            then(nc.vector.tensor_scalar(ok[:, :, :], place[:, :, :], float(cap), None, ALU.is_lt))
            for k in range(2):
                then(nc.vector.scalar_tensor_tensor(slot[:, k, :], topf[:, :, k], float(cap), place[:, k, :], ALU.mult, ALU.add))
            then(nc.vector.scalar_tensor_tensor(sc_f[:, :, :], slot[:, :, :], -OUT, ok[:, :, :], ALU.add, ALU.mult))
            then(nc.vector.tensor_scalar(sc_i[:, :, :], sc_f[:, :, :], OUT, None, ALU.add))
            then(nc.vector.tensor_tensor(slot[:, :, :], slot[:, :, :], ok[:, :, :], ALU.mult))
            for k in range(2):
                then(nc.vector.tensor_copy(ga_i[:, :, k], slot[:, k, :]))
                ins = nc.vector.tensor_tensor(wt[:, :, k], wt[:, :, k], ok[:, k, :], ALU.mult)
                if k == 0:
                    then(ins)
            ins.then_inc(ready, 1)


def experts(nc, stage, cap, tiles, x, w1, w2, b1, b2, table, out, consts):
    gelu = b1 is not None
    FC = FF // 128
    nh = 2 if cap > 512 else 1
    hc = cap // nh
    jobs = [("tp", i) for i in range(len(tiles))] + [("h", (f, s)) for f in range(FC) for s in range(nh)] \
        + [("o", i) for i in range(len(tiles))]
    NJ, RING, NTL = len(jobs), 6, len(tiles)
    on_act = [j[0] != "o" for j in jobs]
    nth = lambda m: sum(1 for k in range(m + 1) if on_act[k] == on_act[m])
    first_o = NJ - NTL
    with ExitStack() as ctx:
        r = Room(nc, ctx, stage)
        ident = r.sb("ident", [128, 128])
        idx = r.sb("idx", [128, NTL], U32)
        xg = r.sb("xg", [TP, NTL, D])
        xT = r.sb("xT", [128, C, cap])
        w1s, w2s = r.sb("w1", [128, C, FF]), r.sb("w2", [128, FC, D])
        hT = r.sb("hT", [128, FC, cap])
        o = r.sb("o", [TP, NTL, D])
        if gelu:
            b1s, b2s = r.sb("b1", [128, FC]), r.sb("b2", [TP, D])
        ring = [r.ps(f"ring{i}", [128, 512]) for i in range(RING)]
        fixed = r.sem("fixed")
        idx_loaded, gathered = r.event("idx_loaded", 16 * NTL, False), r.event("gathered", 16 * NTL, False)
        w1_loaded, w2_loaded = r.event("w1_loaded", 16 * (C + gelu)), r.event("w2_loaded", 16 * (4 + gelu))
        mm_done = r.event("mm_done", NJ)
        act_out, dve_out = r.event("act_out", NJ - NTL), r.event("dve_out", NTL)
        squared = r.event("squared", FC * nh)
        stored = r.event("stored", 16 * NTL)
        block = ctx.enter_context(nc.Block())

        @block.sync
        def _(sp):
            sp.dma_start(ident[:, :], consts["ident"]).then_inc(fixed, 16)
            for e in (w1_loaded, w2_loaded):
                sp.sem_inc(e.sem, e.per)
            with sp.Fori(0, NE) as it:
                sp.wait_ge(mm_done.sem, mm_done.before(it, first_o))
                sp.nop(nofuse=True)
                for c in range(C):
                    sp.dma_start(w1s[:, c, :], w1[bass.ds(it * D + c * 128, 128), :]).then_inc(w1_loaded.sem, 16)
                if gelu:
                    sp.wait_ge(act_out.sem, act_out.before(it))
                    sp.nop(nofuse=True)
                    sp.dma_start(b1s[:, :], b1[bass.ds(it * 128, 128), :]).then_inc(w1_loaded.sem, 16)
                sp.wait_ge(mm_done.sem, mm_done.before(it))
                sp.nop(nofuse=True)
                for c in range(4):
                    sp.dma_start(w2s[:, c * 4:(c + 1) * 4, :],
                                 w2[bass.ds(it * FF + c * 512, 512), :].rearrange("(f p) n -> p f n", p=128)).then_inc(w2_loaded.sem, 16)
                if gelu:
                    sp.wait_ge(dve_out.sem, dve_out.before(it))
                    sp.nop(nofuse=True)
                    sp.dma_start(b2s[:, :], b2[bass.ds(it, 1), :].broadcast_to([TP, D])).then_inc(w2_loaded.sem, 16)

        @block.gpsimd
        def _(pool):

            def gather(it):
                for i, (r0, n) in enumerate(tiles):
                    pool.dma_start(idx[:n, i:i + 1], table[bass.ds(it * cap + r0, n), :]).then_inc(idx_loaded.sem, 16)
                pool.wait_ge(idx_loaded.sem, idx_loaded.now(it, idx_loaded.per))
                pool.wait_ge(mm_done.sem, mm_done.before(it, NTL))
                pool.nop(nofuse=True)
                for i, (r0, n) in enumerate(tiles):
                    pool.indirect_dma_start(out=xg[:n, i, :], out_offset=None, in_=x,
                                            in_offset=bass.IndirectOffsetOnAxis(ap=idx[:n, i:i + 1], axis=0)).then_inc(gathered.sem, 16)
                pool.wait_ge(gathered.sem, gathered.now(it, gathered.per))
                pool.nop(nofuse=True)

            with pool.Fori(0, NE) as it:
                gather(it)

        @block.tensor
        def _(pe):
            pe.sem_inc(mm_done.sem, NJ)
            pe.wait_ge(fixed, 16)
            with pe.Fori(0, NE) as it:
                for m, (kind, i) in enumerate(jobs):
                    bank = ring[m % RING]
                    if m >= RING:
                        k, v = m - RING, 1
                    else:
                        k, v = max(k for k in range(NJ) if k % RING == m), 0
                    e = act_out if on_act[k] else dve_out
                    pe.wait_ge(e.sem, e.now(it, nth(k)) if v else e.before(it, nth(k)))
                    if kind == "tp":
                        n = tiles[i][1]
                        pe.wait_ge(gathered.sem, gathered.now(it, gathered.per))
                        pe.nop(nofuse=True)
                        for c in range(C):
                            ins = nc.tensor.transpose(bank[:, c * n:(c + 1) * n], xg[:n, i, c * 128:(c + 1) * 128], ident[:n, :n])
                    elif kind == "h":
                        f, s = i
                        if m == NTL:
                            pe.wait_ge(w1_loaded.sem, w1_loaded.now(it, w1_loaded.per))
                            pe.wait_ge(act_out.sem, act_out.now(it, NTL))
                        for c in range(C):
                            ins = nc.tensor.matmul(bank[:, :hc], w1s[:, c, f * 128:(f + 1) * 128], xT[:, c, s * hc:(s + 1) * hc],
                                                   start=(c == 0), stop=(c == C - 1))
                    else:
                        r0, n = tiles[i]
                        if m == first_o:
                            pe.wait_ge(w2_loaded.sem, w2_loaded.now(it, w2_loaded.per))
                            e = act_out if gelu else squared
                            pe.wait_ge(e.sem, e.now(it, e.per))
                        for f in range(FC):
                            ins = nc.tensor.matmul(bank[:n, :], hT[:, f, r0:r0 + n], w2s[:, f, :], start=(f == 0), stop=(f == FC - 1))
                    ins.then_inc(mm_done.sem, 1)

        @block.scalar
        def _(act):
            act.sem_inc(act_out.sem, act_out.per)
            act.sem_inc(stored.sem, stored.per)
            with act.Fori(0, NE) as it:
                for m, (kind, i) in enumerate(jobs):
                    bank = ring[m % RING]
                    if kind == "o":
                        r0, n = tiles[i]
                        act.wait_ge(dve_out.sem, dve_out.now(it, i + 1))
                        act.dma_start(out[bass.ds(it * cap + r0, n), :], o[:n, i, :]).then_inc(stored.sem, 16)
                        continue
                    act.wait_ge(mm_done.sem, mm_done.now(it, m + 1))
                    if kind == "tp":
                        r0, n = tiles[i]
                        nc.scalar.activation(xT[:, :, r0:r0 + n], bank[:, :C * n].rearrange("p (c t) -> p c t", c=C),
                                             ACT.Copy).then_inc(act_out.sem, 1)
                    elif gelu:
                        f, s = i
                        if m == NTL:
                            act.wait_ge(w1_loaded.sem, w1_loaded.now(it, w1_loaded.per))
                        nc.scalar.activation(hT[:, f, s * hc:(s + 1) * hc], bank[:, :hc], ACT.Gelu,
                                             bias=b1s[:, f:f + 1]).then_inc(act_out.sem, 1)
                    else:
                        f, s = i
                        nc.scalar.activation(hT[:, f, s * hc:(s + 1) * hc], bank[:, :hc], ACT.Relu).then_inc(act_out.sem, 1)
            act.wait_ge(stored.sem, stored.end(NE))

        @block.vector
        def _(dve):
            dve.sem_inc(dve_out.sem, dve_out.per)
            dve.sem_inc(squared.sem, squared.per)
            with dve.Fori(0, NE) as it:
                for m, (kind, i) in enumerate(jobs):
                    if kind == "h" and not gelu:
                        f, s = i
                        dve.wait_ge(act_out.sem, act_out.now(it, m + 1))
                        dst = hT[:, f, s * hc:(s + 1) * hc]
                        nc.vector.tensor_tensor(dst, dst, dst, ALU.mult).then_inc(squared.sem, 1)
                    elif kind == "o":
                        r0, n = tiles[i]
                        dve.wait_ge(mm_done.sem, mm_done.now(it, m + 1))
                        if i == 0:
                            dve.wait_ge(stored.sem, stored.before(it))
                        if gelu:
                            if i == 0:
                                dve.wait_ge(w2_loaded.sem, w2_loaded.now(it, w2_loaded.per))
                            nc.vector.tensor_tensor(o[:n, i, :], ring[m % RING][:n, :], b2s[:n, :], ALU.add).then_inc(dve_out.sem, 1)
                        else:
                            nc.vector.tensor_copy(o[:n, i, :], ring[m % RING][:n, :]).then_inc(dve_out.sem, 1)


def combine(nc, stage, x, rows, slots, weights, out):
    steps = NTOK // 128 // 2
    with ExitStack() as ctx:
        r = Room(nc, ctx, stage)
        xs = [r.sb(f"x{u}", [128, D]) for u in range(2)]
        idx = [r.sb(f"idx{u}", [128, 2], U32) for u in range(2)]
        wt = [r.sb(f"wt{u}", [128, 2]) for u in range(2)]
        g = [[r.sb(f"g{u}{k}", [128, D]) for k in range(2)] for u in range(2)]
        y = [r.sb(f"y{u}", [128, D]) for u in range(2)]
        t = [r.sb(f"t{u}", [128, D]) for u in range(2)]
        stats, mv = r.sb("stats", [128, 2, 6]), r.sb("mv", [128, 2, 2])
        std, rstd, eps = r.sb("std", [128, 2]), r.sb("rstd", [128, 2]), r.sb("eps", [128, 1])
        eps_set = r.sem("eps_set")
        idx_loaded, x_loaded = [[r.event(f"{s}{u}", per) for u in range(2)] for s, per in (("idx_loaded", 16), ("x_loaded", 32))]
        gathered = [r.event(f"gathered{u}", 32, False) for u in range(2)]
        y_ready, var_ready, std_ready, stored = (r.event(s, p) for s, p in (("y_ready", 2), ("var_ready", 2), ("std_ready", 2), ("stored", 32)))
        dve_step = r.sem("dve_step")
        block = ctx.enter_context(nc.Block())

        @block.sync
        def _(sp):
            for e in idx_loaded + x_loaded:
                sp.sem_inc(e.sem, e.per)
            with sp.Fori(0, steps) as it:
                for u in range(2):
                    sp.wait_ge(y_ready.sem, y_ready.before(it, u + 1))
                    sp.dma_start(idx[u][:, :], slots[bass.ds(it * 2 + u, 1), :, :].rearrange("t p k -> (t p) k")).then_inc(idx_loaded[u].sem, 16)
                    sp.dma_start(wt[u][:, :], weights[bass.ds(it * 2 + u, 1), :, :].rearrange("t p k -> (t p) k")).then_inc(x_loaded[u].sem, 16)
                    sp.dma_start(xs[u][:, :], x[bass.ds((it * 2 + u) * 128, 128), :]).then_inc(x_loaded[u].sem, 16)

        @block.gpsimd
        def _(pool):
            pool.memset(eps[:, :], EPS).then_inc(eps_set, 1)
            with pool.Fori(0, steps) as it:
                for u in range(2):
                    pool.wait_ge(idx_loaded[u].sem, idx_loaded[u].now(it, 16))
                    pool.wait_ge(y_ready.sem, y_ready.before(it, u + 1))
                    pool.nop(nofuse=True)
                    for k in range(2):
                        pool.indirect_dma_start(out=g[u][k][:, :], out_offset=None, in_=rows,
                                                in_offset=bass.IndirectOffsetOnAxis(ap=idx[u][:, k:k + 1], axis=0)).then_inc(gathered[u].sem, 16)

        @block.scalar
        def _(act):
            for e in (std_ready, stored):
                act.sem_inc(e.sem, e.per)
            act.wait_ge(eps_set, 1)
            with act.Fori(0, steps) as it:
                for u in range(2):
                    act.wait_ge(var_ready.sem, var_ready.now(it, u + 1))
                    nc.scalar.activation(std[:, u:u + 1], mv[:, u, 1:2], ACT.Sqrt, bias=eps[:, :]).then_inc(std_ready.sem, 1)
                    act.wait_ge(y_ready.sem, y_ready.now(it, u + 1))
                    act.dma_start(out[bass.ds((it * 2 + u) * 128, 128), :], y[u][:, :]).then_inc(stored.sem, 16)
            act.wait_ge(stored.sem, stored.end(steps))

        @block.vector
        def _(dve):
            for e in (y_ready, var_ready):
                dve.sem_inc(e.sem, e.per)
            with dve.Fori(0, steps) as it:
                own = Chain(dve, dve_step, it, 8)
                for u in range(2):
                    dve.wait_ge(x_loaded[u].sem, x_loaded[u].now(it, 32))
                    dve.wait_ge(gathered[u].sem, gathered[u].now(it, 32))
                    own.done(nc.vector.scalar_tensor_tensor(t[u][:, :], g[u][0][:, :], wt[u][:, 0:1], xs[u][:, :], ALU.mult, ALU.add))
                    dve.wait_ge(dve_step, own.last())
                    own.done(nc.vector.scalar_tensor_tensor(t[u][:, :], g[u][1][:, :], wt[u][:, 1:2], t[u][:, :], ALU.mult, ALU.add))
                    dve.wait_ge(dve_step, own.last())
                    own.done(nc.vector.bn_stats(stats[:, u, :], t[u][:, :]))
                    dve.wait_ge(dve_step, own.last())
                    dve.nop(nofuse=True)
                    nc.vector.bn_aggr(mv[:, u, :], stats[:, u, :]).then_inc(var_ready.sem, 1)
                    dve.wait_ge(std_ready.sem, std_ready.now(it, u + 1))
                    own.done(nc.vector.reciprocal(rstd[:, u:u + 1], std[:, u:u + 1]))
                    dve.wait_ge(dve_step, own.last())
                    if u == 0:
                        dve.wait_ge(stored.sem, stored.before(it))
                    nc.vector.tensor_scalar(y[u][:, :], t[u][:, :], mv[:, u, 0:1], rstd[:, u:u + 1],
                                            ALU.subtract, ALU.mult).then_inc(y_ready.sem, 1)


def decoder(nc, a, out, kind="Internal", upto=99):
    def scratch(name, shape, dt=FP32):
        return nc.dram_tensor(f"scr_{name}", shape, dt, kind=kind).ap() if kind != "Internal" else nc.dram_tensor(f"scr_{name}", shape, dt).ap()

    G = B * HG
    qT, kT, v = scratch("qT", [G * 128, T]), scratch("kT", [G * 128, T]), scratch("v", [G, T, 128])
    V4 = 4 * (HD + 1)
    parts = lambda name, shape: [scratch(f"{name}_{i}", shape, BF16) for i in "hml"]
    q3, k3 = parts("q3", [G * 128, T]), parts("k3", [G * 128, T])
    ck, cv = parts("ck", [G * 128, CTXN]), scratch("cv", [G, CTXN, V4])
    pk, pv = parts("pk", [2 * HG * 128, PASTN]), scratch("pv", [2 * HG, PASTN, V4])
    wk, wv = parts("wk", [G * 128, T]), scratch("wv", [G, T, V4])
    ctx0, ctx1, ctx2 = (scratch(s, [G, T, 128]) for s in ("ctx0", "ctx1", "ctx2"))
    ctx3, ctx4 = scratch("ctx3", [2 * G, T, 128]), scratch("ctx4", [G, T, 128])
    x1, x2, x3, o1, x4, x5 = (scratch(s, [NTOK, D]) for s in ("x1", "x2", "x3", "o1", "x4", "x5"))
    lg0, lg1 = scratch("lg0", [NTOK, NE]), scratch("lg1", [NTOK, NE])
    table0, table1 = scratch("table0", [NE * CAP0, 1], U32), scratch("table1", [NE * CAP1, 1], U32)
    slots0, slots1 = (scratch(s, [NTOK // 128, 128, 2], U32) for s in ("slots0", "slots1"))
    wts0, wts1 = (scratch(s, [NTOK // 128, 128, 2]) for s in ("wts0", "wts1"))
    rows0, rows1 = scratch("rows0", [NE * CAP0, D]), scratch("rows1", [NE * CAP1, D])
    bands = [[nc.dram_tensor(f"band{u}{s}", [4, T * (PADW + 1)], FP32).ap() for s in range(2)] for u in range(2)]
    pband = [nc.dram_tensor(f"pband{u}", [4, T * (PADW + 1)], FP32).ap() for u in range(2)]

    def heads_T(dst, n=T):
        return lambda it: dst[bass.ds(it * D, D), :].rearrange("(c p) t -> p c t", p=128)

    def three(dst):
        return tuple(heads_T(d) for d in dst)

    def heads_v(dst, tk):
        return lambda it, t: dst[bass.ds(it * HG, HG), t * tk:(t + 1) * tk, :].rearrange("g p d -> p g d")

    def grouped(src, off=0):
        return (True, lambda it, t: src[bass.ds(it * HG + off, HG), t * TP:(t + 1) * TP, :].rearrange("g p d -> p g d"))

    def rows(src):
        return lambda it: src[bass.ds(it * T, T), :].rearrange("(a p) d -> p a d", p=TP)

    def tile_rows(src):
        return (False, lambda it, t: src[bass.ds(it * T + t * TP, TP), :])

    def router(dst):
        return lambda it, t: dst[bass.ds(it * T + t * TP, TP), :]

    def cols_of(src):
        return lambda it: src[bass.ds(it * D, D), :].rearrange("(c p) t -> p c t", p=128)

    s32 = float(HD ** -0.5)
    stages = [
        lambda: token_stage(nc, "qkv0", B, T, TP, T, a, xT=cols_of(a["xT"]),
                            fm=[(a["wq0"], None, s32, None, heads_T(qT)), (a["wk0"], None, 1.0, None, heads_T(kT))],
                            tm=[(a["wv0"], None, D, heads_v(v, TP))]),
        lambda: attention(nc, "att0", 1, T, TP, qT, kT, v, ctx0, a,
                          rpe=((a["rpe_k"], a["rpe_q"]), a["rpe_v"], bands, pband)),
        lambda: token_stage(nc, "out0", B, T, TP, T, a, zs=[grouped(ctx0)], wz=a["wo0"], bz=a["bo0"], res=rows(a["x"]),
                            norm=True, y_out=rows(x1), fm=[(a["xq0"], None, float(D ** -0.5), None, three(q3))]),
        lambda: token_stage(nc, "ckv0", B, CTXN, 125, 375, a, xT=cols_of(a["ctxT"]),
                            fm=[(a["xk0"], None, 1.0, None, three(ck))], tm=[(a["xv0"], None, VW, heads_v(cv, 125))]),
        lambda: split_attention(nc, "xat0", 1, CTXN, 125, q3, ck, cv, ctx1, a),
        lambda: token_stage(nc, "out1", B, T, TP, T, a, zs=[grouped(ctx1)], wz=a["xo0"], bz=a["xbo0"], res=rows(x1),
                            norm=True, y_out=rows(x2), tm=[(a["wg0"], None, NE, router(lg0))]),
        lambda: route(nc, "rte0", True, lg0, CAP0, a, table0, slots0, wts0),
        lambda: experts(nc, "exp0", CAP0, [(i * TP, TP) for i in range(5)], x2, a["fc0"], a["pj0"], None, None, table0, rows0, a),
        lambda: combine(nc, "cmb0", x2, rows0, slots0, wts0, x3),
        lambda: token_stage(nc, "qkv1", B, T, TP, T, a, y_in=rows(x3),
                            fm=[(a["Wq"], a["bq"], s32, None, three(q3)), (a["Wk"], a["bk"], 1.0, None, three(k3))],
                            tm=[(a["Wv"], a["bv"], VW, heads_v(wv, TP))]),
        lambda: split_attention(nc, "att1", 1, T, TP, q3, k3, wv, ctx2, a),
        lambda: token_stage(nc, "out2", B, T, TP, T, a, zs=[grouped(ctx2)], wz=a["Wo"], bz=a["bo"], y_out=rows(o1),
                            fm=[(a["Wrq"], a["brq"], s32, None, three(q3))]),
        lambda: token_stage(nc, "pkv1", 2, PASTN, 128, 512, a, xT=cols_of(a["pastT"]),
                            fm=[(a["Wrk"], a["brk"], 1.0, None, three(pk))], tm=[(a["Wrv"], a["brv"], VW, heads_v(pv, 128))]),
        lambda: split_attention(nc, "rec1", 2, PASTN, 128, q3, pk, pv, ctx3, a, shared=True),
        lambda: token_stage(nc, "out3", B, T, TP, T, a, zs=[tile_rows(o1), grouped(ctx3), grouped(ctx3, G)], wz=a["Wg"], bz=a["bg"],
                            gate=True, res=rows(x3), norm=True, y_out=rows(x4),
                            fm=[(a["lq"], a["lqb"], None, 1, None), (a["lqr"], a["lqrb"], a["trig_q"], 2, three(q3))]),
        lambda: token_stage(nc, "wkv1", B, T, TP, T, a, xT=cols_of(a["ctx224T"]),
                            fm=[(a["lk"], a["lkb"], None, 1, None), (a["lkr"], a["lkrb"], a["trig_k"], 2, three(wk))],
                            tm=[(a["lv"], a["lvb"], VW, heads_v(wv, TP))]),
        lambda: split_attention(nc, "win1", 1, T, TP, q3, wk, wv, ctx4, a, mask=(a["window"], a["window_k"])),
        lambda: token_stage(nc, "out4", B, T, TP, T, a, zs=[grouped(ctx4)], wz=a["lo"], bz=a["lob"], res=rows(x4),
                            norm=True, y_out=rows(x5), tm=[(a["rw1"], a["rb1"], NE, router(lg1))]),
        lambda: route(nc, "rte1", False, lg1, CAP1, a, table1, slots1, wts1),
        lambda: experts(nc, "exp1", CAP1, [(0, TP), (TP, TP), (2 * TP, 56)], x5, a["w1"], a["w2"], a["b1"], a["b2"], table1, rows1, a),
        lambda: combine(nc, "cmb1", x5, rows1, slots1, wts1, out),
    ]
    for stage in stages[:upto]:
        stage()


def shape_constants():
    i = np.arange(T)
    rel = i[None, :] - i[:, None]
    tiled = lambda m: np.ascontiguousarray(m.reshape(NA, TP, T).transpose(1, 0, 2))
    far = np.stack([tiled(rel < -HALF), tiled(rel > HALF)], 1)
    window = np.where((rel <= 0) & (rel >= -64), 0.0, NEG)
    half = HD // 2
    freqs = (1.0 / 10000.0 ** (np.arange(half, dtype=np.float32) / half)).astype(np.float32)
    ang = (np.arange(T, dtype=np.float32)[:, None] * freqs[None, :]).astype(np.float32)
    cos = np.tile(np.cos(ang).T, (8, 1))
    sin = np.sin(ang).T
    sin = np.tile(np.concatenate([-sin, sin], 0), (4, 1))
    s = HD ** -0.5
    return {
        "ident": np.eye(128), "tri": np.triu(np.ones((128, 128))), "far": far, "window": tiled(window), "window_k": tiled(window.T),
        "trig_q": np.stack([cos * s, sin * s]), "trig_k": np.stack([cos, sin]),
        "iota": np.broadcast_to(np.arange(NE), (128, NTOK // 128, NE)),
        "tok": np.arange(NTOK).reshape(-1, 128).T,
    }


def laid_out(x, n):
    T2 = lambda w: w.T
    turned = lambda w: w.reshape(B if w.shape[0] == B else 2, w.shape[1], D).transpose(0, 2, 1).reshape(-1, w.shape[1])
    bias = lambda b: b.reshape(C, 128).T.reshape(-1)
    swap = (np.arange(D).reshape(H, 2, HD // 2)[:, ::-1]).reshape(-1)

    def blocks(w):
        m = np.zeros((128, 128), w.dtype)
        for h in range(4):
            m[h * HD:(h + 1) * HD, h * HD:(h + 1) * HD] = w.T
        return m

    w = n["L0_attn_w_qkv"]

    def per_head(t):
        m = np.zeros((HG, 4, HD, 4, 64), t.dtype)
        for h in range(4):
            m[:, h, :, h, :NBUCK] = t.reshape(HG, 4, HD, NBUCK)[:, h]
        return m.reshape(HG * 128, 256)

    d = {
        "x": x.reshape(NTOK, D), "xT": turned(x), "ctxT": turned(n["ctx_1024"]), "ctx224T": turned(n["ctx_1024"][:, :T]),
        "pastT": turned(n["L1_attn_past_states"].reshape(2, PASTN, D)),
        "wq0": T2(w[:D]), "wk0": T2(w[D:2 * D]), "wv0": T2(w[2 * D:]),
        "wo0": T2(n["L0_attn_w_proj"]), "bo0": n["L0_attn_b_proj"],
        "rpe_k": per_head(n["L0_attn_rpe_k_table"]), "rpe_q": per_head(n["L0_attn_rpe_q_table"]),
        "rpe_v": n["L0_attn_rpe_v_table"].reshape(HG, 4, NBUCK, HD).transpose(0, 2, 1, 3).reshape(HG * NBUCK, 128),
        "xq0": blocks(n["L0_xattn_Wq"]), "xk0": blocks(n["L0_xattn_Wk"]), "xv0": blocks(n["L0_xattn_Wv"]),
        "xo0": T2(n["L0_xattn_Wo"]), "xbo0": n["L0_xattn_bo"],
        "wg0": T2(n["L0_ffn_w_g"]), "fc0": n["L0_ffn_c_fc"].reshape(NE * D, FF), "pj0": n["L0_ffn_c_proj"].reshape(NE * FF, D),
        "lo": T2(n["L1_xattn_o_w"]), "lob": n["L1_xattn_o_b"], "lv": T2(n["L1_xattn_v_w"]), "lvb": n["L1_xattn_v_b"],
        "rw1": n["L1_ffn_router_w"], "rb1": n["L1_ffn_router_b"],
        "w1": n["L1_ffn_w1"].reshape(NE * D, FF), "w2": n["L1_ffn_w2"].reshape(NE * FF, D),
        "b1": n["L1_ffn_b1"].reshape(NE, FF // 128, 128).transpose(0, 2, 1).reshape(NE * 128, FF // 128), "b2": n["L1_ffn_b2"],
    }
    for s in ("Wq", "Wk", "Wv", "Wo", "Wrq", "Wrk", "Wrv", "Wg"):
        d[s] = n["L1_attn_" + s]
    for s in ("bq", "bk", "brq", "brk"):
        d[s] = bias(n["L1_attn_" + s])
    for s in ("bv", "bo", "brv", "bg"):
        d[s] = n["L1_attn_" + s]
    for s in ("q", "k"):
        wt, b = n[f"L1_xattn_{s}_w"], n[f"L1_xattn_{s}_b"]
        d["l" + s], d["l" + s + "b"] = T2(wt), bias(b)
        d["l" + s + "r"], d["l" + s + "rb"] = T2(wt[swap]), bias(b[swap])
    return d


def kernel(**inputs):
    import numpy as _np
    import concourse.bacc as _bacc
    from concourse import mybir as _mybir
    from concourse.bass_utils import run_bass_kernel_spmd as _run

    n = {k: _np.asarray(v) for k, v in inputs.items()}
    nc = _bacc.Bacc("TRN2", target_bir_lowering=False, num_devices=1)
    arrays, handles = {}, {}
    consts = {k: v.astype(_np.uint32 if k == "tok" else _np.float32) for k, v in shape_constants().items()}
    for name, v in {**laid_out(n["x"], n), **consts}.items():
        v = _np.ascontiguousarray(v)
        arrays["in_" + name] = v
        handles[name] = nc.dram_tensor("in_" + name, v.shape, _mybir.dt.from_np(v.dtype), kind="ExternalInput").ap()
    out = nc.dram_tensor("out_dram", (NTOK, D), FP32, kind="ExternalOutput").ap()
    decoder(nc, handles, out)
    r = _run(nc, [arrays], core_ids=[0])
    return r.results[0]["out_dram"].reshape(B, T, D)
```

```python
import concourse.bass as bass
from concourse import mybir
from concourse.alu_op_type import AluOpType as ALU
from contextlib import ExitStack
import numpy as np

FP32 = mybir.dt.float32
BF16 = mybir.dt.bfloat16
U32 = mybir.dt.uint32
ACT = mybir.ActivationFunctionType
X = mybir.AxisListType.X

B, T, D = 8, 224, 512
NTOK = B * T
H, HD = 16, 32
HG = 4
TP = 112
NA = T // TP
C = D // 128
CTXN = 750
PASTN = 1024
NE, FF = 8, 2048
CAP0, CAP1 = 560, 280
EPS = 1e-5
HALF = 31
NBUCK = 2 * HALF + 1
WIDE = T + TP - 1
BANDW = WIDE + TP - 1
PADW = T + 2 * HALF
NEG = -1.0e30
VW = H * (HD + 1)


class Event:

    def __init__(self, sem, per, primed=True):
        self.sem, self.per, self.primed = sem, per, primed

    def now(self, it, k):
        return (it + self.primed) * self.per + k

    def before(self, it, k=None):
        return it * self.per + (self.per if k is None else k)

    def end(self, steps):
        return (steps + self.primed) * self.per


class Chain:

    def __init__(self, eng, sem, it, per):
        self.eng, self.sem, self.it, self.per, self.n = eng, sem, it, per, 0

    def done(self, ins):
        ins.then_inc(self.sem, 1)
        self.n += 1

    def last(self):
        return self.it * self.per + self.n

    def close(self):
        assert self.n == self.per, (self.n, self.per)


class Room:

    def __init__(self, nc, ctx, stage):
        self.nc, self.ctx, self.stage, self.sems = nc, ctx, stage, []
        ctx.callback(self.leave)

    def sb(self, name, shape, dt=FP32):
        return self.ctx.enter_context(self.nc.sbuf_tensor(f"{self.stage}_{name}", shape, dt))

    def ps(self, name, shape, dt=FP32):
        return self.ctx.enter_context(self.nc.psum_tensor(f"{self.stage}_{name}", shape, dt))

    def sem(self, name):
        self.sems.append(self.nc.alloc_semaphore(name=f"{self.stage}_{name}"))
        return self.sems[-1]

    def leave(self):
        self.nc.clear_and_free_semaphores(self.sems)
        self.nc.all_engine_barrier()

    def event(self, name, per, primed=True):
        return Event(self.sem(name), max(per, 1), primed)


def chunked(w):
    return w.rearrange("(c p) n -> p c n", p=min(128, w.shape[0]))


def rows_of(b, parts):
    return b.rearrange("(o n) -> o n", o=1).broadcast_to([parts, b.shape[0]])


class Flow:

    def __init__(self, sem, k, items=8, primed=True):
        self.sem, self.k, self.items, self.primed = sem, k, items, primed

    def at(self, it, n, j=None):
        j = self.k if j is None else j
        return it * (self.items * self.k) + ((n + self.items * self.primed) * self.k + j)


def token_stage(nc, stage, steps, n, tk, cols, consts, xT=None, zs=None, wz=None, bz=None,
                gate=False, res=None, norm=False, y_out=None, y_in=None, fm=(), tm=()):
    nt, ncol = n // tk, n // cols
    nz = 0 if zs is None else (2 if gate else 1)
    front = [("tpz", z, a) for z in range(nz) for a in range(nt)] + [("lin", 0, a) for a in range(nt if nz else 0)]
    back = [("tpy", 0, a) for a in range(nt if xT is None and (fm or tm) else 0)]
    back += [("fm", w, (c, s)) for c in range(C) for w in range(len(fm)) for s in range(ncol)]
    back += [("tm", w, a) for w in range(len(tm)) for a in range(nt)]
    n_tpz, n_tpy = nz * nt, sum(j[0] == "tpy" for j in back)

    class Part:

        def __init__(self, name, jobs, ring, r):
            self.jobs, self.NJ, self.RING = jobs, len(jobs), min(ring, len(jobs))
            self.on_act = [j[0] in ("tpz", "tpy") or (j[0] == "tm" and tm[j[1]][1] is None) for j in jobs]
            self.place = {j: i for i, j in enumerate(jobs)}
            self.ring = [r.ps(f"{name}{i}", [128, 512]) for i in range(self.RING)]
            self.mm_done = Flow(r.sem(f"{name}_mm_done"), self.NJ, 2)
            self.act_out = Flow(r.sem(f"{name}_act_out"), sum(self.on_act), 2)
            self.dve_out = Flow(r.sem(f"{name}_dve_out"), self.NJ - sum(self.on_act), 2)

        def out(self, m):
            k = sum(1 for i in range(m + 1) if self.on_act[i] == self.on_act[m])
            return (self.act_out if self.on_act[m] else self.dve_out), k

        def last_in_bank(self, m):
            if m >= self.RING:
                return m - self.RING, 0
            return max(k for k in range(self.NJ) if k % self.RING == m), 1

    with ExitStack() as ctx:
        r = Room(nc, ctx, stage)
        F = Part("front", front, 3, r)
        K = Part("back", back, 5 if nz else 6, r)
        ident = r.sb("ident", [128, 128])
        nload = len(zs) if nz else 0
        z_sb = [r.sb(f"z{i}", [tk, nt, D]) for i in range(nload)]
        zT = [r.sb(f"zT{i}", [128, C, n]) for i in range(nz)]
        wz_sb = r.sb("wz", [128, C * nz, D]) if nz else None
        bz_sb = r.sb("bz", [tk, D]) if nz else None
        res_sb = r.sb("res", [tk, nt, D]) if res is not None else None
        y = r.sb("y", [tk, nt, D]) if xT is None else None
        t = r.sb("t", [tk, nt, D]) if nz else None
        stats, mv = r.sb("stats", [tk, nt, 6]), r.sb("mv", [tk, nt, 2])
        std, rstd, eps = r.sb("std", [tk, nt]), r.sb("rstd", [tk, nt]), r.sb("eps", [128, 1])
        yT = [r.sb(f"yT{w}", [128, C, n]) for w in range(2)] if xT is not None else [r.sb("yT", [128, C, n])] * 2
        fm_o = [[r.sb(f"fo{w}{i}", [128, C, n]) for i in range(len(fm))] for w in range(2)]
        tm_o = [[r.sb(f"to{w}{i}", [tk, nt, f[2]]) for i, f in enumerate(tm)] for w in range(2)]
        split = [i for i, f in enumerate(fm) if isinstance(f[4], tuple)]
        parts = [{i: [r.sb(f"part{w}{i}{k}", [128, C, n], BF16) for k in range(3)] for i in split} for w in range(2)]
        fm_w = [r.sb(f"fw{i}", [128, f[0].shape[0] // 128, f[0].shape[1]]) for i, f in enumerate(fm)]
        fm_b = [r.sb(f"fb{i}", [128, C]) if f[1] is not None else None for i, f in enumerate(fm)]
        tm_w = [r.sb(f"tw{i}", [128, f[0].shape[0] // 128, f[0].shape[1]]) for i, f in enumerate(tm)]
        tm_b = [r.sb(f"tb{i}", [tk, min(D, f[2])]) if f[1] is not None else None for i, f in enumerate(tm)]
        pieces = [(c, i) for c in range(C) for i in split]
        NP = len(pieces)
        lead_n = lambda q: max(1, 2 * q)
        rest_n = lambda q: 2 * q + 3 if q < NP - 1 else 2 * NP
        roped = [i for i, f in enumerate(fm) if f[3] == 2]
        if roped:
            trig = [r.sb(f"trig{i}", [128, n]) for i in range(2)]

        stored_fm = [i for i, f in enumerate(fm) if f[4] is not None]
        w_loaded, const_set = r.sem("w_loaded"), r.sem("const_set")
        flow = lambda name, k, primed=True: Flow(r.sem(name), k, 2, primed)
        by_parity = lambda name, k: [Flow(r.sem(f"{name}{w}"), k, 1) for w in range(2)]
        z_loaded, res_loaded, y_loaded = flow("z_loaded", 16 * nload * nt), flow("res_loaded", 16), flow("y_loaded", 16)
        x_loaded = by_parity("x_loaded", 16)
        y_ready = flow("y_ready", nt)
        var_ready, std_ready = flow("var_ready", nt), flow("std_ready", 1)
        mean_ready = flow("mean_ready", nt)
        gate_ready = flow("gate_ready", nt)
        rope_ready = flow("rope_ready", C * len(roped))
        part_act, part_dve = (flow(s, 2 * NP) for s in ("part_act", "part_dve"))
        y_stored = flow("y_stored", 16, False)
        fm_stored = flow("fm_stored", 16 * (len(stored_fm) + 2 * len(split)), False)
        tm_stored = flow("tm_stored", 16 * len(tm) * nt, False)
        y_free, fm_free, tm_free = (flow(s, 1) for s in ("y_free", "fm_free", "tm_free"))
        dve_step = r.sem("dve_step")
        block = ctx.enter_context(nc.Block())
        n_const = 1 + 2 * sum(f[2] == VW for f in tm)

        fixed = [(ident[:, :], consts["ident"])]
        if nz:
            fixed += [(wz_sb[:, :, :], chunked(wz)), (bz_sb[:, :], rows_of(bz, tk))]
        for i, f in enumerate(fm):
            fixed.append((fm_w[i][:, :, :], chunked(f[0])))
            if f[1] is not None:
                fixed.append((fm_b[i][:, :], f[1].rearrange("(p c) -> p c", p=128)))
        for i, f in enumerate(tm):
            fixed.append((tm_w[i][:, :, :], chunked(f[0])))
            if f[1] is not None:
                fixed.append((tm_b[i][:, :], rows_of(f[1], tk)))
        if roped:
            fixed += [(trig[k][:, :], fm[roped[0]][2][k]) for k in range(2)]

        def run(eng, step):
            if nz:
                step(0, -1, True, False)
            if steps > 2:
                with eng.Fori(0, steps // 2 - 1) as it:
                    for s in range(2):
                        step(it, s, bool(nz), True)
            for s in range(2):
                step(steps // 2 - 1, s, bool(nz) and s == 0, True)

        def by_head(w, s, i, bank):
            dst = tm_o[s % 2][w][:, i, :]
            if tm[w][2] < VW:
                return dst, bank[:tk, :tm[w][2]]
            return dst.rearrange("p (h d) -> p h d", h=H)[:, :, 0:HD], bank[:tk, :].rearrange("p (h d) -> p h d", h=H)

        @block.sync
        def _(sp):
            for e in [z_loaded, res_loaded, y_loaded] + x_loaded:
                sp.sem_inc(e.sem, e.items * max(1, e.k))

            def load(it, s):
                if nz:
                    sp.wait_ge(F.mm_done.sem, F.mm_done.at(it, s - 1, n_tpz))
                    sp.nop(nofuse=True)
                    if gate:
                        sp.wait_ge(y_ready.sem, y_ready.at(it, s - 1))
                        sp.nop(nofuse=True)
                    for i, src in enumerate(zs):
                        for a in range(nt):
                            sp.dma_start(z_sb[i][:, a, :].rearrange("p (g d) -> p g d", g=C) if src[0] else z_sb[i][:, a, :],
                                         src[1](it * 2 + s, a)).then_inc(z_loaded.sem, 16)
                if res is not None:
                    sp.wait_ge(y_ready.sem, y_ready.at(it, s - 1))
                    sp.nop(nofuse=True)
                    sp.dma_start(res_sb[:, :, :], res(it * 2 + s)).then_inc(res_loaded.sem, 16)
                if y_in is not None:
                    sp.wait_ge(K.mm_done.sem, K.mm_done.at(it, s - 1, n_tpy))
                    sp.nop(nofuse=True)
                    sp.dma_start(y[:, :, :], y_in(it * 2 + s)).then_inc(y_loaded.sem, 16)
                if xT is not None:
                    sp.wait_ge(K.mm_done.sem, K.mm_done.at(it, s - 2))
                    sp.nop(nofuse=True)
                    sp.dma_start(yT[s % 2][:, :, :], xT(it * 2 + s)).then_inc(x_loaded[s % 2].sem, 16)

            load(0, 0)
            for i, (dst, src) in enumerate(fixed):
                sp.dma_start(dst, src).then_inc(w_loaded, 16)
            load(0, 1)
            if steps > 2:
                with sp.Fori(1, steps // 2) as it:
                    for s in range(2):
                        load(it, s)

        @block.gpsimd
        def _(pool):
            pool.memset(eps[:, :], EPS).then_inc(const_set, 1)
            for i, f in enumerate(tm):
                if f[2] == VW:
                    for w in range(2):
                        pool.memset(tm_o[w][i][:, :, :], 1.0).then_inc(const_set, 1)
            for e in (y_free, fm_free, tm_free):
                pool.sem_inc(e.sem, e.items * e.k)

            def step(it, s, front, back):
                if front and y_out is not None:
                    pool.wait_ge(y_ready.sem, y_ready.at(it, s + 1))
                    pool.nop(nofuse=True)
                    pool.dma_start(y_out(it * 2 + s + 1), y[:, :, :]).then_inc(y_stored.sem, 16)
                for i in stored_fm if back else []:
                    if i in split:
                        pool.wait_ge(part_dve.sem, part_dve.at(it, s))
                        pool.nop(nofuse=True)
                        for part, dst in zip(parts[s % 2][i], fm[i][4]):
                            pool.dma_start(dst(it * 2 + s), part[:, :, :]).then_inc(fm_stored.sem, 16)
                        continue
                    e, k = (rope_ready, rope_ready.k) if i in roped else K.out(K.place[("fm", i, (C - 1, ncol - 1))])
                    pool.wait_ge(e.sem, e.at(it, s, k))
                    pool.nop(nofuse=True)
                    pool.dma_start(fm[i][4](it * 2 + s), fm_o[s % 2][i][:, :, :]).then_inc(fm_stored.sem, 16)
                if front and y_out is not None:
                    pool.wait_ge(y_stored.sem, y_stored.at(it, s + 1))
                    pool.sem_inc(y_free.sem, 1)
                for i in range(len(tm)) if back else []:
                    for a in range(nt):
                        e, k = K.out(K.place[("tm", i, a)])
                        pool.wait_ge(e.sem, e.at(it, s, k))
                        pool.nop(nofuse=True)
                        src = tm_o[s % 2][i][:, a, :]
                        if tm[i][2] >= D:
                            src = src.rearrange("p (g d) -> p g d", g=C)
                        pool.dma_start(tm[i][3](it * 2 + s, a), src).then_inc(tm_stored.sem, 16)
                if back and stored_fm:
                    pool.wait_ge(fm_stored.sem, fm_stored.at(it, s))
                    pool.sem_inc(fm_free.sem, 1)
                if back and tm:
                    pool.wait_ge(tm_stored.sem, tm_stored.at(it, s))
                    pool.sem_inc(tm_free.sem, 1)

            run(pool, step)

        @block.tensor
        def _(pe):
            for p in (F, K):
                pe.sem_inc(p.mm_done.sem, 2 * max(1, p.NJ))
            pe.wait_ge(w_loaded, 16 * len(fixed))

            def job(it, s, p, m):
                kind, w, i = p.jobs[m]
                bank = p.ring[m % p.RING]
                k, before = p.last_in_bank(m)
                e, k = p.out(k)
                pe.wait_ge(e.sem, e.at(it, s - before, k))
                if kind == "tpz":
                    e, k = (mean_ready, i + 1) if gate and w == 1 else (z_loaded, z_loaded.k)
                    pe.wait_ge(e.sem, e.at(it, s, k))
                    for c in range(C):
                        ins = nc.tensor.transpose(bank[:, c * tk:(c + 1) * tk], z_sb[w][:, i, c * 128:(c + 1) * 128], ident[:tk, :tk])
                elif kind == "lin":
                    e, k = F.out(F.place[("tpz", nz - 1, i)])
                    pe.wait_ge(e.sem, e.at(it, s, k))
                    for k in range(C * nz):
                        ins = nc.tensor.matmul(bank[:tk, :], zT[k // C][:, k % C, i * tk:(i + 1) * tk],
                                               wz_sb[:, k, :], start=(k == 0), stop=(k == C * nz - 1))
                elif kind == "tpy":
                    e, k = (y_loaded, 16) if y_in is not None else (y_ready, i + 1)
                    pe.wait_ge(e.sem, e.at(it, s, k))
                    for c in range(C):
                        ins = nc.tensor.transpose(bank[:, c * tk:(c + 1) * tk], y[:, i, c * 128:(c + 1) * 128], ident[:tk, :tk])
                else:
                    if xT is not None:
                        e, j, k = x_loaded[s % 2], 0, 16
                    else:
                        e, j, k = K.act_out, s, n_tpy
                    if m == n_tpy:
                        pe.wait_ge(e.sem, e.at(it, j, k))
                    src = yT[s % 2]
                    if kind == "fm":
                        c, col = i
                        whole = fm[w][0].shape[0] == D
                        for k in range(C) if whole else [c]:
                            lhsT = fm_w[w][:, k, c * 128:(c + 1) * 128] if whole else fm_w[w][:, 0, :]
                            ins = nc.tensor.matmul(bank[:, :cols], lhsT, src[:, k, col * cols:(col + 1) * cols],
                                                   start=(k == 0 or not whole), stop=(k == C - 1 or not whole))
                    elif tm[w][0].shape[0] == 128:
                        for k in range(C):
                            ins = nc.tensor.matmul(bank[:tk, k * 128:(k + 1) * 128], src[:, k, i * tk:(i + 1) * tk],
                                                   tm_w[w][:, 0, :], start=True, stop=True)
                    else:
                        for k in range(C):
                            ins = nc.tensor.matmul(bank[:tk, :min(D, tm[w][2])], src[:, k, i * tk:(i + 1) * tk],
                                                   tm_w[w][:, k, :], start=(k == 0), stop=(k == C - 1))
                ins.then_inc(p.mm_done.sem, 1)

            def step(it, s, front, back):
                for m in range(n_tpz) if front else []:
                    job(it, s + 1, F, m)
                for m in range(n_tpy) if back else []:
                    job(it, s, K, m)
                for m in range(n_tpz, F.NJ) if front else []:
                    job(it, s + 1, F, m)
                for m in range(n_tpy, K.NJ) if back else []:
                    job(it, s, K, m)

            run(pe, step)

        @block.scalar
        def _(act):
            for e in (F.act_out, K.act_out, std_ready, gate_ready, part_act):
                act.sem_inc(e.sem, 2 * max(1, e.k))
            act.wait_ge(const_set, n_const)

            def transposed(it, s, p, m):
                kind, w, i = p.jobs[m]
                act.wait_ge(p.mm_done.sem, p.mm_done.at(it, s, m + 1))
                dst = zT[w] if kind == "tpz" else yT[0]
                nc.scalar.activation(dst[:, :, i * tk:(i + 1) * tk],
                                     p.ring[m % p.RING][:, :C * tk].rearrange("p (c t) -> p c t", c=C),
                                     ACT.Copy).then_inc(p.act_out.sem, 1)

            def first_part(it, s, q):
                c, i = pieces[q]
                if q == 0:
                    act.wait_ge(fm_free.sem, fm_free.at(it, s - 2))
                e, v = (rope_ready, c + 1) if i in roped else K.out(K.place[("fm", i, (c, ncol - 1))])
                act.wait_ge(e.sem, e.at(it, s, v))
                nc.scalar.activation(parts[s % 2][i][0][:, c, :], fm_o[s % 2][i][:, c, :], ACT.Copy).then_inc(part_act.sem, 1)

            def second_part(it, s, q):
                c, i = pieces[q]
                act.wait_ge(part_dve.sem, part_dve.at(it, s, lead_n(q)))
                nc.scalar.activation(parts[s % 2][i][1][:, c, :], fm_o[s % 2][i][:, c, :], ACT.Copy).then_inc(part_act.sem, 1)

            def step(it, s, front, back):
                for m in range(n_tpz) if front else []:
                    transposed(it, s + 1, F, m)
                for m in range(n_tpy) if back else []:
                    transposed(it, s, K, m)
                if front and gate:
                    for a in range(nt):
                        act.wait_ge(F.dve_out.sem, F.dve_out.at(it, s + 1, a + 1))
                        nc.scalar.activation(t[:, a, :], t[:, a, :], ACT.Sigmoid).then_inc(gate_ready.sem, 1)
                if front and norm:
                    act.wait_ge(var_ready.sem, var_ready.at(it, s + 1))
                    nc.scalar.activation(std[:, :], mv[:, :, 1], ACT.Sqrt, bias=eps[:tk, :]).then_inc(std_ready.sem, 1)
                for q in range(NP) if back else []:
                    first_part(it, s, q)
                    if q > 0:
                        second_part(it, s, q - 1)
                if back and NP:
                    second_part(it, s, NP - 1)
                for m in range(n_tpy, K.NJ) if back else []:
                    kind, w, i = K.jobs[m]
                    if not K.on_act[m]:
                        continue
                    if i == 0:
                        act.wait_ge(tm_free.sem, tm_free.at(it, s - 2))
                    act.wait_ge(K.mm_done.sem, K.mm_done.at(it, s, m + 1))
                    dst, src = by_head(w, s, i, K.ring[m % K.RING])
                    nc.scalar.activation(dst, src, ACT.Copy).then_inc(K.act_out.sem, 1)

            run(act, step)

        per = nt * (4 * gate + (res is not None) + norm) + norm

        @block.vector
        def _(dve):
            for e in (F.dve_out, K.dve_out, y_ready, var_ready, mean_ready, rope_ready, part_dve):
                dve.sem_inc(e.sem, 2 * max(1, e.k))
            dve.wait_ge(w_loaded, 16 * len(fixed))
            dve.wait_ge(const_set, n_const)

            def make_y(it, s):
                own = Chain(dve, dve_step, it, 2 * per)
                own.n = start = s * per
                if gate:
                    dve.wait_ge(z_loaded.sem, z_loaded.at(it, s))
                    for a in range(nt):
                        own.done(nc.vector.tensor_tensor(z_sb[1][:, a, :], z_sb[1][:, a, :], z_sb[2][:, a, :], ALU.add))
                    for a in range(nt):
                        dve.wait_ge(dve_step, own.it * own.per + start + a + 1)
                        nc.vector.tensor_scalar(z_sb[1][:, a, :], z_sb[1][:, a, :], 0.5, None,
                                                ALU.mult).then_inc(mean_ready.sem, 1)
                for i in range(nt):
                    m = F.place[("lin", 0, i)]
                    bank = F.ring[m % F.RING]
                    dve.wait_ge(F.mm_done.sem, F.mm_done.at(it, s, m + 1))
                    nc.vector.tensor_tensor(t[:, i, :], bank[:tk, :], bz_sb[:, :], ALU.add).then_inc(F.dve_out.sem, 1)
                    if i == 0:
                        if y_out is not None:
                            dve.wait_ge(y_free.sem, y_free.at(it, s - 1))
                        if n_tpy:
                            dve.wait_ge(K.mm_done.sem, K.mm_done.at(it, s - 1, n_tpy))
                        if res is not None:
                            dve.wait_ge(res_loaded.sem, res_loaded.at(it, s))
                    if gate:
                        if i == 0:
                            dve.wait_ge(mean_ready.sem, mean_ready.at(it, s))
                        own.done(nc.vector.tensor_tensor(y[:, i, :], z_sb[1][:, i, :], z_sb[0][:, i, :], ALU.subtract))
                        dve.wait_ge(gate_ready.sem, gate_ready.at(it, s, i + 1))
                        dve.wait_ge(dve_step, own.last())
                        own.done(nc.vector.tensor_tensor(t[:, i, :], y[:, i, :], t[:, i, :], ALU.mult))
                        dve.wait_ge(dve_step, own.last())
                        own.done(nc.vector.tensor_tensor(t[:, i, :], t[:, i, :], z_sb[0][:, i, :], ALU.add))
                        dve.wait_ge(dve_step, own.last())
                    else:
                        dve.wait_ge(F.dve_out.sem, F.dve_out.at(it, s, i + 1))
                    if res is not None:
                        own.done(nc.vector.tensor_tensor(t[:, i, :], t[:, i, :], res_sb[:, i, :], ALU.add))
                        dve.wait_ge(dve_step, own.last())
                    if norm:
                        own.done(nc.vector.bn_stats(stats[:, i, :], t[:, i, :]))
                        dve.wait_ge(dve_step, own.last())
                        dve.nop(nofuse=True)
                        nc.vector.bn_aggr(mv[:, i, :], stats[:, i, :]).then_inc(var_ready.sem, 1)
                    else:
                        nc.vector.tensor_copy(y[:, i, :], t[:, i, :]).then_inc(y_ready.sem, 1)
                if norm:
                    dve.wait_ge(std_ready.sem, std_ready.at(it, s))
                    own.done(nc.vector.reciprocal(rstd[:, :], std[:, :]))
                    dve.wait_ge(dve_step, own.last())
                    for a in range(nt):
                        nc.vector.tensor_scalar(y[:, a, :], t[:, a, :], mv[:, a, 0:1], rstd[:, a:a + 1],
                                                ALU.subtract, ALU.mult).then_inc(y_ready.sem, 1)
                assert own.n == start + per

            def rest(it, s, q, j):
                c, i = pieces[q]
                dve.wait_ge(part_act.sem, part_act.at(it, s, (lead_n, rest_n)[j](q)))
                whole = fm_o[s % 2][i]
                dst = whole if j == 0 else parts[s % 2][i][2]
                nc.vector.tensor_tensor(dst[:, c, :], whole[:, c, :], parts[s % 2][i][j][:, c, :], ALU.subtract).then_inc(part_dve.sem, 1)

            def step(it, s, front, back):
                if front:
                    make_y(it, s + 1)
                if not back:
                    return
                for m, (kind, w, i) in enumerate(K.jobs):
                    if K.on_act[m]:
                        continue
                    bank = K.ring[m % K.RING]
                    dve.wait_ge(K.mm_done.sem, K.mm_done.at(it, s, m + 1))
                    if kind == "fm":
                        c, col = i
                        if c == 0 and col == 0 and w == 0 and stored_fm:
                            dve.wait_ge(fm_free.sem, fm_free.at(it, s - 2))
                        dst = fm_o[s % 2][w][:, c, col * cols:(col + 1) * cols]
                        if fm[w][3] is not None:
                            nc.vector.scalar_tensor_tensor(dst, bank[:, :cols], fm_b[w][:, c:c + 1],
                                                           trig[fm[w][3] - 1][:, :], ALU.add, ALU.mult).then_inc(K.dve_out.sem, 1)
                            if fm[w][3] == 2:
                                dve.wait_ge(K.dve_out.sem, K.dve_out.at(it, s, K.out(m)[1]))
                                nc.vector.tensor_tensor(dst, dst, fm_o[s % 2][w - 1][:, c, :], ALU.add).then_inc(rope_ready.sem, 1)
                        elif fm[w][1] is not None:
                            nc.vector.tensor_scalar(dst, bank[:, :cols], fm_b[w][:, c:c + 1], fm[w][2],
                                                    ALU.add, ALU.mult).then_inc(K.dve_out.sem, 1)
                        else:
                            nc.vector.tensor_scalar(dst, bank[:, :cols], fm[w][2], None, ALU.mult).then_inc(K.dve_out.sem, 1)
                        if w in split and col == ncol - 1:
                            q = pieces.index((c, w))
                            if q > 0:
                                rest(it, s, q - 1, 0)
                            if q > 1:
                                rest(it, s, q - 2, 1)
                    else:
                        if i == 0 and w == 0:
                            dve.wait_ge(tm_free.sem, tm_free.at(it, s - 2))
                        dst, src = by_head(w, s, i, bank)
                        b = tm_b[w][:, :]
                        if tm[w][2] == VW:
                            b = b.rearrange("p (h d) -> p h d", h=H)
                        nc.vector.tensor_tensor(dst, src, b, ALU.add).then_inc(K.dve_out.sem, 1)
                if NP:
                    rest(it, s, NP - 1, 0)
                    rest(it, s, NP - 2, 1)
                    rest(it, s, NP - 1, 1)

            run(dve, step)


def relative_attention(nc, stage, q, k, v, out, consts, tab_q, tab_k, tab_v, bands, pband):
    UN = 8
    NU = HG * UN
    with ExitStack() as ctx:
        r = Room(nc, ctx, stage)
        ident = r.sb("ident", [128, 128])
        far = r.sb("far", [TP, 2, NA, T])
        zero = r.sb("zero", [TP, 2, PADW + 1])
        tab = [[r.sb(f"tab{s}{g}", [128, 256]) for g in range(HG)] for s in range(2)]
        tabv = [r.sb(f"tabv{g}", [NBUCK, 128]) for g in range(HG)]
        qT = [r.sb(f"qT{w}", [128, T]) for w in range(2)]
        kT = [r.sb(f"kT{w}", [128, T]) for w in range(2)]
        vs = [r.sb(f"v{w}", [TP, NA, 128]) for w in range(2)]
        P = [r.sb(f"P{w}", [TP, NA, 4, T]) for w in range(2)]
        L = [[r.sb(f"L{w}{s}", [TP, NA, 4, WIDE]) for s in range(2)] for w in range(2)]
        Bias = [[r.sb(f"B{w}{s}", [TP, NA, 4, T]) for s in range(2)] for w in range(2)]
        Bd = [r.sb(f"Bd{w}", [TP, NA, 4, 64]) for w in range(2)]
        sums, rinv = r.sb("sums", [TP, 2 * UN]), r.sb("rinv", [TP, 2 * UN])
        PT = [r.sb(f"PT{i}", [TP, NA, TP]) for i in range(2)]
        Z = [r.sb(f"Z{i}", [TP, T]) for i in range(2)]
        nmax = r.sb("nmax", [TP, 2])
        bT = [r.sb(f"bT{a}", [64, 4, TP]) for a in range(NA)]
        junk = r.sb("junk", [TP, 4, T])
        o_sb = [r.sb(f"o{g}", [TP, NA, 128]) for g in range(HG)]
        S = [r.ps(f"S{i}", [TP, 512]) for i in range(2)]
        PTp = r.ps("PTp", [TP, 512])
        O = [r.ps(f"O{i}", [TP, 512]) for i in range(2)]
        Lp = [r.ps(f"Lp{i}", [TP, 512]) for i in range(2)]
        Vp = r.ps("Vp", [TP, 512])

        fixed_loaded, zeroed, zero_set = r.sem("fixed_loaded"), r.sem("zeroed"), r.sem("zero_set")
        by_parity = lambda name, k, primed=True: [Flow(r.sem(f"{name}{w}"), k, HG // 2, primed) for w in range(2)]
        by_group = lambda name, k: Flow(r.sem(name), k, HG)
        by_unit = lambda name: Flow(r.sem(name), 1, NU)
        qk_loaded, v_loaded = by_parity("qk_loaded", 32), by_parity("v_loaded", 16)
        l_done = by_group("l_done", 4)
        l_out = by_group("l_out", 4)
        band_stored = by_parity("band_stored", 64)
        bias_loaded = by_parity("bias_loaded", 64)
        s_done = by_unit("s_done")
        max_done = by_unit("max_done")
        exp_done = by_unit("exp_done")
        pt_done, pt_out = by_unit("pt_done"), by_unit("pt_out")
        av_done, o_done = by_unit("av_done"), by_unit("o_done")
        p_stored, pband_loaded = by_parity("p_stored", 32), by_parity("pband_loaded", 32)
        tail_done = by_group("tail_done", 2)
        bt_done, bt_out = by_group("bt_done", 2), by_group("bt_out", 2)
        v2_done, v2_out = by_group("v2_done", 2), by_group("v2_out", 2)
        out_stored = by_parity("out_stored", 16, False)
        out_free = by_group("out_free", 1)
        dve_step = r.sem("dve_step")
        block = ctx.enter_context(nc.Block())
        n_fixed = 2 + 3 * HG

        before = [TP - 1 - HALF + a * TP for a in range(NA)]

        def sides(i):
            s, a = 1 - i // 2, i % 2
            return s, a, (0, before[a], 0), (before[a] + NBUCK, WIDE - before[a] - NBUCK, NBUCK - 1)

        def scaled(s):
            return 1.0 if s == 0 else -float(HD ** -0.5)

        beyond = [[(0, TP - HALF), (0, T - HALF)], [(HALF, T), (TP + HALF, T)]]

        @block.sync
        def _(sp):
            sp.dma_start(ident[:, :], consts["ident"]).then_inc(fixed_loaded, 16)
            sp.dma_start(far[:, :, :, :], consts["far"]).then_inc(fixed_loaded, 16)
            for g in range(HG):
                for s, t in enumerate((tab_q, tab_k)):
                    sp.dma_start(tab[s][g][:, :], t[g * 128:(g + 1) * 128, :]).then_inc(fixed_loaded, 16)
                sp.dma_start(tabv[g][:, :], tab_v[g * NBUCK:(g + 1) * NBUCK, :]).then_inc(fixed_loaded, 16)
            sp.wait_ge(zero_set, 1)
            for buf in pband:
                for h in range(4):
                    sp.dma_start(buf[h].rearrange("(p a w) -> p a w", p=TP, a=2), zero[:, :, :]).then_inc(zeroed, 16)
            sp.wait_ge(zeroed, 16 * 4 * 2)
            for e in qk_loaded + v_loaded + band_stored + bias_loaded + p_stored + pband_loaded:
                sp.sem_inc(e.sem, e.items * e.k)

            def load_qk(it, g):
                w = g % 2
                sp.wait_ge(s_done.sem, s_done.at(it, UN * (g - 1) - 1))
                sp.nop(nofuse=True)
                sp.dma_start(qT[w][:, :], q[bass.ds((it * HG + g) * 128, 128), :]).then_inc(qk_loaded[w].sem, 16)
                sp.dma_start(kT[w][:, :], k[bass.ds((it * HG + g) * 128, 128), :]).then_inc(qk_loaded[w].sem, 16)

            def load_v(it, g):
                w = g % 2
                sp.wait_ge(av_done.sem, av_done.at(it, UN * (g - 1) - 1))
                sp.nop(nofuse=True)
                sp.dma_start(vs[w][:, :, :], v[bass.ds(it * HG + g, 1), :, :].rearrange("o (t p) d -> p (o t) d", p=TP)
                             ).then_inc(v_loaded[w].sem, 16)

            def store_band(it, g, s):
                w = g % 2
                sp.wait_ge(bias_loaded[w].sem, bias_loaded[w].at(it, g // 2 - 1))
                sp.nop(nofuse=True)
                sp.wait_ge(l_out.sem, l_out.at(it, g, (1 - s) * 2 + 2))
                sp.nop(nofuse=True)
                for a in range(NA):
                    diag = bands[w][s][:, a, :].rearrange("h (p w) -> p h w", w=BANDW + 1)
                    sp.dma_start(diag[:, :, 0:WIDE], L[w][s][:, a, :, :]).then_inc(band_stored[w].sem, 16)

            def load_bias(it, g):
                w = g % 2
                sp.wait_ge(max_done.sem, max_done.at(it, UN * (g - 1) - 1))
                sp.nop(nofuse=True)
                sp.wait_ge(band_stored[w].sem, band_stored[w].at(it, g // 2))
                sp.nop(nofuse=True)
                for s in (1, 0):
                    for a in range(NA):
                        rows = bands[w][s][:, a, 0:TP * BANDW].rearrange("h (p w) -> p h w", w=BANDW)
                        sp.dma_start(Bias[w][s][:, a, :, :], rows[:, :, TP - 1:WIDE]).then_inc(bias_loaded[w].sem, 16)

            def store_p(it, g):
                w = g % 2
                sp.wait_ge(exp_done.sem, exp_done.at(it, UN * (g + 1) - 1))
                sp.nop(nofuse=True)
                sp.wait_ge(pband_loaded[w].sem, pband_loaded[w].at(it, g // 2 - 1))
                sp.nop(nofuse=True)
                rows = pband[w][:, 0:T * PADW].rearrange("h (i w) -> i h w", w=PADW)
                for a in range(NA):
                    sp.dma_start(rows[a * TP:(a + 1) * TP, :, HALF:HALF + T], P[w][:, a, :, :]).then_inc(p_stored[w].sem, 16)

            def load_band(it, g):
                w = g % 2
                sp.wait_ge(bt_done.sem, bt_done.at(it, g - 2))
                sp.nop(nofuse=True)
                sp.wait_ge(p_stored[w].sem, p_stored[w].at(it, g // 2))
                sp.nop(nofuse=True)
                diag = pband[w][:, :].rearrange("h (i w) -> i h w", w=PADW + 1)
                for a in range(NA):
                    sp.dma_start(Bd[w][:, a, :, 0:NBUCK], diag[a * TP:(a + 1) * TP, :, 0:NBUCK]).then_inc(pband_loaded[w].sem, 16)

            def turn(it, g, more, back):
                if more:
                    load_qk(it, g + 1)
                if back:
                    store_p(it, g - 1)
                    load_band(it, g - 1)
                if more:
                    store_band(it, g + 1, 1)
                    load_v(it, g + 1)
                    store_band(it, g + 1, 0)
                    load_bias(it, g + 1)

            def body(it, first, last):
                for g in range(HG):
                    turn(it, g, not (last and g == HG - 1), not (first and g == 0))

            turn(0, -1, True, False)
            body(0, True, False)
            with sp.Fori(1, B - 1) as it:
                body(it, False, False)
            body(B - 1, False, True)
            turn(B - 1, HG, False, True)

        @block.gpsimd
        def _(pool):
            pool.memset(zero[:, :, :], 0.0).then_inc(zero_set, 1)
            pool.sem_inc(out_free.sem, HG)

            def store_out(it, g):
                pool.wait_ge(v2_out.sem, v2_out.at(it, g))
                pool.nop(nofuse=True)
                pool.dma_start(out[bass.ds(it * HG + g, 1), :, :].rearrange("o (a p) d -> p (o a) d", p=TP),
                               o_sb[g % HG][:, :, :]).then_inc(out_stored[g % 2].sem, 16)

            def free_out(it, g):
                pool.wait_ge(out_stored[g % 2].sem, out_stored[g % 2].at(it, g // 2))
                pool.sem_inc(out_free.sem, 1)

            def body(it, first, last):
                for g in range(HG):
                    if not (first and g < 2):
                        free_out(it, g - 2)
                    if not (first and g == 0):
                        store_out(it, g - 1)

            body(0, True, False)
            with pool.Fori(1, B - 1) as it:
                body(it, False, False)
            body(B - 1, False, True)
            store_out(B - 1, HG - 1)
            for w in range(2):
                pool.wait_ge(out_stored[w].sem, out_stored[w].at(B - 1, 1))

        @block.tensor
        def _(pe):
            for e in (l_done, s_done, pt_done, av_done, bt_done, v2_done):
                pe.sem_inc(e.sem, e.items * e.k)
            pe.wait_ge(fixed_loaded, 16 * n_fixed)

            def relative(it, g, jobs):
                w = g % 2
                if 0 in jobs:
                    pe.wait_ge(qk_loaded[w].sem, qk_loaded[w].at(it, g // 2))
                for i in jobs:
                    s, a = 1 - i // 2, i % 2
                    if i < 2:
                        pe.wait_ge(l_out.sem, l_out.at(it, g - 1, i + 3))
                        pe.wait_ge(bt_out.sem, bt_out.at(it, g - 3, i + 1))
                    else:
                        pe.wait_ge(l_out.sem, l_out.at(it, g, i - 1))
                    nc.tensor.matmul(Lp[i % 2][:, 0:256], (qT, kT)[s][w][:, a * TP:(a + 1) * TP], tab[s][g % HG][:, :],
                                     start=True, stop=True).then_inc(l_done.sem, 1)

            def scores(it, n):
                g, h, a = n // UN, n % UN // NA, n % NA
                w = g % 2
                if n % UN == 0:
                    pe.wait_ge(qk_loaded[w].sem, qk_loaded[w].at(it, g // 2))
                    pe.wait_ge(bias_loaded[w].sem, bias_loaded[w].at(it, g // 2))
                pe.wait_ge(max_done.sem, max_done.at(it, n - 2))
                rows = slice(32 * h, 32 * h + 32)
                nc.tensor.matmul(S[n % 2][:, 0:T], qT[w][rows, a * TP:(a + 1) * TP], kT[w][rows, :], start=True, stop=False,
                                 skip_group_check=True)
                for t in range(NA):
                    ins = nc.tensor.matmul(S[n % 2][:, t * TP:(t + 1) * TP], Bias[w][1][:, t, h, a * TP:(a + 1) * TP],
                                           ident[:TP, :TP], start=False, stop=(t == NA - 1), skip_group_check=True)
                ins.then_inc(s_done.sem, 1)

            def transposes(it, n):
                g, h, a = n // UN, n % UN // NA, n % NA
                pe.wait_ge(exp_done.sem, exp_done.at(it, n))
                pe.wait_ge(pt_out.sem, pt_out.at(it, n - 1))
                for t in range(NA):
                    ins = nc.tensor.transpose(PTp[:, t * TP:(t + 1) * TP], P[g % 2][:, a, h, t * TP:(t + 1) * TP], ident[:TP, :TP])
                ins.then_inc(pt_done.sem, 1)

            def values(it, n):
                g, h = n // UN, n % UN // NA
                w = g % 2
                if n % UN == 0:
                    pe.wait_ge(v_loaded[w].sem, v_loaded[w].at(it, g // 2))
                pe.wait_ge(pt_out.sem, pt_out.at(it, n))
                pe.wait_ge(o_done.sem, o_done.at(it, n - 2))
                for t in range(NA):
                    ins = nc.tensor.matmul(O[n % 2][:, 0:HD], PT[n % 2][:, t, :], vs[w][:, t, h * HD:(h + 1) * HD],
                                           start=(t == 0), stop=(t == NA - 1))
                ins.then_inc(av_done.sem, 1)

            def turn_band(it, g, a, more):
                pe.wait_ge(tail_done.sem, tail_done.at(it, g, a + 1))
                if more:
                    pe.wait_ge(l_out.sem, l_out.at(it, g + 2, 3 + a))
                else:
                    pe.wait_ge(bt_out.sem, bt_out.at(it, g - 1, a + 1))
                pe.nop(nofuse=True)
                for h in range(4):
                    ins = nc.tensor.transpose(Lp[a][:NBUCK, h * TP:(h + 1) * TP], Bd[g % 2][:, a, h, 0:NBUCK], ident[:TP, :TP])
                ins.then_inc(bt_done.sem, 1)

            def table_values(it, g, a):
                pe.wait_ge(bt_out.sem, bt_out.at(it, g, a + 1))
                pe.wait_ge(v2_out.sem, v2_out.at(it, g, a))
                for h in range(4):
                    ins = nc.tensor.matmul(Vp[:, h * HD:(h + 1) * HD], bT[a][:NBUCK, h, :],
                                           tabv[g % HG][:, h * HD:(h + 1) * HD], start=True, stop=True)
                ins.then_inc(v2_done.sem, 1)

            def body(it, first, last):
                for n in range(NU):
                    g, j = n // UN, n % UN
                    more = not (last and g == HG - 1)
                    back = not (first and g == 0)
                    transposes(it, n)
                    if more and j == 0:
                        relative(it, g + 1, (2, 3))
                    if j == UN - 1 and not (last and g + 2 >= HG):
                        relative(it, g + 2, (0, 1))
                    if not (last and n + 2 >= NU):
                        scores(it, n + 2)
                    values(it, n)
                    if back and j in (3, 5):
                        turn_band(it, g - 1, j // 4, more)
                    if back and j in (4, 6):
                        table_values(it, g - 1, j // 5)

            relative(0, 0, range(4))
            relative(0, 1, (0, 1))
            scores(0, 0)
            scores(0, 1)
            body(0, True, False)
            with pe.Fori(1, B - 1) as it:
                body(it, False, False)
            body(B - 1, False, True)
            for a in range(NA):
                turn_band(B - 1, HG - 1, a, False)
                table_values(B - 1, HG - 1, a)

        @block.scalar
        def _(act):
            for e in (l_out, exp_done, pt_out, bt_out):
                act.sem_inc(e.sem, e.items * e.k)

            def take_relative(it, g, jobs):
                w = g % 2
                if 0 in jobs:
                    act.wait_ge(bias_loaded[w].sem, bias_loaded[w].at(it, g // 2 - 1))
                for i in jobs:
                    s, a, *ends = sides(i)
                    product = Lp[i % 2][:, 0:256].rearrange("p (h m) -> p h m", h=4)
                    act.wait_ge(l_done.sem, l_done.at(it, g, i + 1))
                    nc.scalar.activation(L[w][s][:, a, :, before[a]:before[a] + NBUCK], product[:, :, 0:NBUCK], ACT.Copy, scale=scaled(s))
                    for c0, n, m in ends:
                        ins = nc.scalar.activation(L[w][s][:, a, :, c0:c0 + n], product[:, :, m:m + 1].broadcast_to([TP, 4, n]),
                                                   ACT.Copy, scale=scaled(s))
                    ins.then_inc(l_out.sem, 1)

            def exponential(it, n):
                g, h, a = n // UN, n % UN // NA, n % NA
                w = g % 2
                if n % UN == 0:
                    act.wait_ge(p_stored[w].sem, p_stored[w].at(it, g // 2 - 1))
                    act.wait_ge(tail_done.sem, tail_done.at(it, g - 2))
                    act.wait_ge(o_done.sem, o_done.at(it, UN * (g - 1) - 1))
                act.wait_ge(max_done.sem, max_done.at(it, n))
                c = w * UN + n % UN
                nc.scalar.activation(P[w][:, a, h, :], Z[n % 2][:, :], ACT.Exp, scale=-1.0, bias=nmax[:, n % 2:n % 2 + 1],
                                     accum_out=sums[:, c:c + 1]).then_inc(exp_done.sem, 1)

            def take_PT(it, n):
                act.wait_ge(pt_done.sem, pt_done.at(it, n))
                act.wait_ge(av_done.sem, av_done.at(it, n - 2))
                nc.scalar.activation(PT[n % 2][:, :, :], PTp[:, 0:T].rearrange("p (t c) -> p t c", t=NA), ACT.Copy).then_inc(pt_out.sem, 1)

            def take_band(it, g, a):
                act.wait_ge(bt_done.sem, bt_done.at(it, g, a + 1))
                act.wait_ge(v2_done.sem, v2_done.at(it, g - 1, a + 1))
                nc.scalar.activation(bT[a][:NBUCK, :, :], Lp[a][:NBUCK, 0:4 * TP].rearrange("p (h c) -> p h c", h=4),
                                     ACT.Copy).then_inc(bt_out.sem, 1)

            def body(it, first, last):
                for n in range(NU):
                    g, j = n // UN, n % UN
                    take_PT(it, n)
                    if j == 0 and not (last and g == HG - 1):
                        take_relative(it, g + 1, (2, 3))
                    if j == UN - 1 and not (last and g + 2 >= HG):
                        take_relative(it, g + 2, (0, 1))
                    if not (last and n + 2 >= NU):
                        exponential(it, n + 2)
                    if j in (3, 5) and not (first and g == 0):
                        take_band(it, g - 1, j // 4)

            take_relative(0, 0, range(4))
            take_relative(0, 1, (0, 1))
            exponential(0, 0)
            exponential(0, 1)
            body(0, True, False)
            with act.Fori(1, B - 1) as it:
                body(it, False, False)
            body(B - 1, False, True)
            for a in range(NA):
                take_band(B - 1, HG - 1, a)

        @block.vector
        def _(dve):
            for e in (max_done, o_done, tail_done, v2_out):
                dve.sem_inc(e.sem, e.items * e.k)
            START = 64
            dve.sem_inc(dve_step, START)
            dve.wait_ge(fixed_loaded, 16 * n_fixed)

            class Own:

                def __init__(self, base, it=0, per=0):
                    self.base, self.it, self.per, self.n = base, it, per, 0

                def done(self, ins):
                    ins.then_inc(dve_step, 1)
                    self.n += 1

                def at(self, back=0):
                    return self.it * self.per + (self.base + self.n - back)

            def maximum(it, own, n):
                g, h, a = n // UN, n % UN // NA, n % NA
                if n % UN == 0:
                    dve.wait_ge(bias_loaded[g % 2].sem, bias_loaded[g % 2].at(it, g // 2))
                dve.wait_ge(s_done.sem, s_done.at(it, n))
                dve.wait_ge(exp_done.sem, exp_done.at(it, n - 2))
                dve.nop(nofuse=True)
                nc.vector.tensor_tensor_reduce(
                    out=Z[n % 2][:, :], in0=S[n % 2][:, 0:T], in1=Bias[g % 2][0][:, a, h, :], scale=1.0, scalar=-NEG,
                    op0=ALU.add, op1=ALU.min, accum_out=nmax[:, n % 2:n % 2 + 1]).then_inc(max_done.sem, 1)

            def outputs(it, own, n):
                g, h, a = n // UN, n % UN // NA, n % NA
                c = g % 2 * UN + n % UN
                if n % UN == 0:
                    dve.wait_ge(out_free.sem, out_free.at(it, g - HG))
                    dve.wait_ge(v2_out.sem, v2_out.at(it, g - 2))
                dve.wait_ge(exp_done.sem, exp_done.at(it, n))
                own.done(nc.vector.reciprocal(rinv[:, c:c + 1], sums[:, c:c + 1]))
                dve.wait_ge(dve_step, own.at())
                dve.wait_ge(av_done.sem, av_done.at(it, n))
                nc.vector.tensor_scalar(o_sb[g % HG][:, a, h * HD:(h + 1) * HD], O[n % 2][:, 0:HD], rinv[:, c:c + 1], None,
                                        ALU.mult).then_inc(o_done.sem, 1)

            def end_sums(it, own, g, a, heads):
                w = g % 2
                if a == 0 and 0 in heads:
                    dve.wait_ge(pband_loaded[w].sem, pband_loaded[w].at(it, g // 2))
                for h in heads:
                    for end in range(2):
                        lo, hi = beyond[end][a]
                        m = end * (NBUCK - 1)
                        dve.wait_ge(dve_step, own.at(3))
                        own.done(nc.vector.tensor_tensor_reduce(
                            out=junk[:, (2 * h + end) % 4, lo:hi], in0=P[w][:, a, h, lo:hi], in1=far[:, end, a, lo:hi], scale=1.0,
                            scalar=Bd[w][:, a, h, m:m + 1], op0=ALU.mult, op1=ALU.add, accum_out=Bd[w][:, a, h, m:m + 1]))
                if 3 in heads:
                    dve.wait_ge(dve_step, own.at())
                    dve.sem_inc(tail_done.sem, 1)

            def add_table_values(it, own, g, a):
                dve.wait_ge(v2_done.sem, v2_done.at(it, g, a + 1))
                if a == 0:
                    dve.wait_ge(o_done.sem, o_done.at(it, UN * (g + 1) - 1))
                for h in range(4):
                    dst = o_sb[g % HG][:, a, h * HD:(h + 1) * HD]
                    c = g % 2 * UN + h * NA + a
                    ins = nc.vector.scalar_tensor_tensor(dst, Vp[:, h * HD:(h + 1) * HD], rinv[:, c:c + 1], dst, ALU.mult, ALU.add)
                    if h < 3:
                        own.done(ins)
                ins.then_inc(v2_out.sem, 1)

            def body(own, it, first, last):
                for n in range(NU):
                    g, j = n // UN, n % UN
                    more = not (last and g == HG - 1)
                    back = not (first and g == 0)
                    if not (last and n + 2 >= NU):
                        maximum(it, own, n + 2)
                    outputs(it, own, n)
                    if back and 1 <= j <= 4:
                        end_sums(it, own, g - 1, (j - 1) // 2, ((0, 1), (2, 3))[(j - 1) % 2])
                    if back and j in (5, 7):
                        add_table_values(it, own, g - 1, j // 7)
                return own.n

            own = Own(START)
            maximum(0, own, 0)
            maximum(0, own, 1)
            body(own, 0, True, False)
            per = NU + HG * (2 * 8 + 2 * 3)
            base = START + own.n - per
            with dve.Fori(1, B - 1) as it:
                assert body(Own(base, it, per), it, False, False) == per
            own = Own(base + (B - 1) * per)
            body(own, B - 1, False, True)
            for a in range(NA):
                end_sums(B - 1, own, HG - 1, a, range(4))
                add_table_values(B - 1, own, HG - 1, a)


def split_attention(nc, stage, npast, nk, kt, q, k, v, out, consts, shared=False, mask=None):
    nt = nk // kt
    nb = 2 if nk > 512 else 1
    ncb = nk // nb
    chunks = [list(range(c, min(c + 4, nt))) for c in range(0, nt, 4)]
    NC = len(chunks)
    GB = HG if NC == 1 else 2
    NH = 4 * GB
    steps = npast * B * HG // GB
    V1 = HD + 1
    AHEAD = 2 if NC == 1 else 1
    SA = 1 if NC == 1 else NA
    with ExitStack() as ctx:
        r = Room(nc, ctx, stage)
        identb = r.sb("identb", [128, 128], BF16)
        Q = [[r.sb(f"Q{u}{s}", [128, 4, T], BF16) for s in range(2)] for u in range(GB)]
        K = [[r.sb(f"K{u}{s}", [128, 4, nk], BF16) for s in range(2)] for u in range(GB)]
        V = [r.sb(f"V{u}", [kt, nt, 4, V1]) for u in range(GB)]
        PT = [r.sb(f"PT{i}", [kt, nt, T]) for i in range(2)]
        nmax = [r.sb(f"nmax{i}", [TP, NA]) for i in range(2)]
        shift = [r.sb(f"shift{i}", [TP, NA, 2], BF16) for i in range(2)]
        rinv = r.sb("rinv", [TP, 2, NA])
        OT = [r.sb(f"OT{i}", [128, TP]) for i in range(2)]
        o_sb = [r.sb(f"o{u}", [TP, NA, 128]) for u in range(GB)]
        S = [r.ps(f"S{i}", [TP, nb, 512]) for i in range(2 if NC == 1 else 1)]
        ST = [r.ps(f"ST{c}", [kt, (len(ts) + 1) // 2, 512]) for c, ts in enumerate(chunks)]
        if NC == 1:
            ST = [ST[0], r.ps("ST1", [kt, 1, 512])]
        O = r.ps("O", [128, 512])
        R = r.ps("R", [128, 1024], BF16)
        one_bank = NC > 1
        Oq = R[:, 512:1024].bitcast(FP32) if one_bank else r.ps("Oq", [128, 512])
        if mask is not None:
            mask_f = r.sb("mask_f", [TP, NA, nk])
            maskT_f = r.sb("maskT_f", [kt, nt, T])
            mask_q, mask_k = r.sb("mask_q", [TP, NA, nk], BF16), r.sb("mask_k", [kt, nt, T], BF16)
        ident = r.sb("ident", [128, 128])
        fixed_loaded, fixed_made, ones_set = r.sem("fixed_loaded"), r.sem("fixed_made"), r.sem("ones_set")
        qk_loaded = [r.event(f"qk_loaded{u}", 16 * 12) for u in range(GB)]
        v_loaded = [r.event(f"v_loaded{u}", 16) for u in range(GB)]
        s_done = Flow(r.sem("s_done"), SA, NH)
        max_done = Flow(r.sem("max_done"), SA, NH)
        shift_done = Flow(r.sem("shift_done"), 1, NH)
        row_done = Flow(r.sem("row_done"), 1, NH)
        row_out = Flow(r.sem("row_out"), 1, NH)
        st_done = Flow(r.sem("st_done"), NC, NH)
        exp_done = Flow(r.sem("exp_done"), NC, NH)
        av_done = Flow(r.sem("av_done"), 1, NH)
        ot_out = Flow(r.sem("ot_out"), NA, NH)
        o_done = Flow(r.sem("o_done"), 1, NH)
        o_out = Flow(r.sem("o_out"), 1, NH)
        cast_done, rinv_done = Flow(r.sem("cast_done"), 1, NH), Flow(r.sem("rinv_done"), 1, NH)
        out_stored = [r.event(f"out_stored{u}", 16, False) for u in range(GB)]
        out_free = [r.event(f"out_free{u}", 1) for u in range(GB)]
        block = ctx.enter_context(nc.Block())
        n_fixed = 1 + 2 * (mask is not None)

        @block.sync
        def _(sp):
            sp.dma_start(ident[:, :], consts["ident"]).then_inc(fixed_loaded, 16)
            if mask is not None:
                sp.dma_start(mask_f[:, :, :], mask[0]).then_inc(fixed_loaded, 16)
                sp.dma_start(maskT_f[:, :, :], mask[1]).then_inc(fixed_loaded, 16)
            for e in qk_loaded + v_loaded:
                sp.sem_inc(e.sem, e.per)

            def step(it, pp, b, h2):
                for u in range(GB):
                    g = b * HG + h2 * GB + u
                    gk = pp * HG + h2 * GB + u if shared else g
                    sp.wait_ge(st_done.sem, st_done.at(it, 4 * u + 3 - NH, NC))
                    sp.nop(nofuse=True)
                    for which, (src, dst, row) in enumerate(((q, Q[u], g), (k, K[u], gk))):
                        order = ((0, 0, 1), (1, 0, 2)) if which == 0 else ((0, 1, 0), (1, 2, 0))
                        for s in range(2):
                            for j in range(3):
                                part = src[order[s][j]]
                                sp.dma_start(dst[s][32 * j:32 * j + 32, :, :],
                                             part[bass.ds(row * 128, 128), :].rearrange("(h p) t -> p h t", p=32)
                                             ).then_inc(qk_loaded[u].sem, 16)
                    sp.wait_ge(av_done.sem, av_done.at(it, 4 * u + 3 - NH, 1))
                    sp.nop(nofuse=True)
                    sp.dma_start(V[u][:, :, :, :], v[bass.ds(gk, 1), :, :].rearrange("o (t p) (h d) -> p (o t) h d", p=kt, h=4)
                                 ).then_inc(v_loaded[u].sem, 16)

            if npast > 1:
                with sp.Fori(0, npast) as pp:
                    with sp.Fori(0, B) as b:
                        with sp.Fori(0, 2) as h2:
                            step(pp * (2 * B) + b * 2 + h2, pp, b, h2)
            elif GB < HG:
                with sp.Fori(0, B) as b:
                    with sp.Fori(0, 2) as h2:
                        step(b * 2 + h2, 0, b, h2)
            else:
                with sp.Fori(0, B) as b:
                    step(b, 0, b, 0)

        @block.gpsimd
        def _(pool):
            for u in range(GB):
                pool.memset(K[u][1][96:98, :, :], 1.0).then_inc(ones_set, 1)
                pool.sem_inc(out_free[u].sem, 1)
            with pool.Fori(0, steps) as it:
                for u in range(GB):
                    pool.wait_ge(o_out.sem, o_out.at(it, 4 * u + 3, 1))
                    pool.nop(nofuse=True)
                    pool.dma_start(out[bass.ds(it * GB + u, 1), :, :].rearrange("o (a p) d -> p (o a) d", p=TP),
                                   o_sb[u][:, :, :]).then_inc(out_stored[u].sem, 16)
                    pool.wait_ge(out_stored[u].sem, out_stored[u].now(it, 16))
                    pool.sem_inc(out_free[u].sem, 1)

        @block.tensor
        def _(pe):
            for f in (s_done, row_done, st_done, av_done, o_done):
                pe.sem_inc(f.sem, NH * f.k)
            pe.wait_ge(fixed_made, n_fixed)
            pe.wait_ge(ones_set, GB + 2)

            def scores(it, n, turn):
                u, h = n // 4 % GB, n % 4
                if h == 0 and turn == 0:
                    e = qk_loaded[u]
                    pe.wait_ge(e.sem, e.now(it, e.per + (e.per if n >= NH else 0)))
                if SA == 1:
                    pe.wait_ge(max_done.sem, max_done.at(it, n - 2, 1))
                else:
                    pe.wait_ge(max_done.sem, max_done.at(it, n if turn else n - 1, 1 if turn else NA))
                for a in range(NA) if SA == 1 else [turn]:
                    bank, c0 = (S[n % 2], a * nk) if SA == 1 else (S[0], 0)
                    for s in range(nb):
                        ins = nc.tensor.matmul(bank[:, s, c0:c0 + ncb], Q[u][0][0:96, h, a * TP:(a + 1) * TP],
                                               K[u][0][0:96, h, s * ncb:(s + 1) * ncb], start=True, stop=mask is None)
                    if mask is not None:
                        ins = nc.tensor.matmul(bank[:, 0, c0:c0 + nk], identb[:TP, :TP], mask_q[:, a, :], start=False, stop=True)
                ins.then_inc(s_done.sem, 1)

            def rows_of_max(it, n):
                pe.wait_ge(shift_done.sem, shift_done.at(it, n, 1))
                pe.wait_ge(row_out.sem, row_out.at(it, n - 1, 1))
                if one_bank:
                    pe.wait_ge(o_out.sem, o_out.at(it, n - AHEAD - 2, 1))
                for a in range(NA):
                    ins = nc.tensor.transpose(R[96:98, a * TP:(a + 1) * TP], shift[n % 2][:, a, :], identb[:TP, :TP])
                ins.then_inc(row_done.sem, 1)

            def scores_T(it, n, c):
                u, h = n // 4, n % 4
                bank = ST[c if NC > 1 else n % 2]
                if c == 0:
                    pe.wait_ge(row_out.sem, row_out.at(it, n, 1))
                pe.wait_ge(exp_done.sem, exp_done.at(it, n - 1, c + 1) if NC > 1 else exp_done.at(it, n - 2, 1))
                for i, t in enumerate(chunks[c]):
                    dst = bank[:, i // 2, i % 2 * T:(i % 2 + 1) * T]
                    nc.tensor.matmul(dst, K[u][0][0:96, h, t * kt:(t + 1) * kt], Q[u][0][0:96, h, :], start=True, stop=False)
                    if mask is not None:
                        nc.tensor.matmul(dst, identb[:kt, :kt], mask_k[:, t, :], start=False, stop=False)
                    ins = nc.tensor.matmul(dst, K[u][1][0:98, h, t * kt:(t + 1) * kt], Q[u][1][0:98, h, :], start=False, stop=True)
                ins.then_inc(st_done.sem, 1)

            def values(it, n, c):
                u, h = n // 4 % GB, n % 4
                if c == 0:
                    if h == 0:
                        pe.wait_ge(v_loaded[u].sem, v_loaded[u].now(it, 16))
                    pe.wait_ge(ot_out.sem, ot_out.at(it, n - 1, NA))
                pe.wait_ge(exp_done.sem, exp_done.at(it, n, c + 1))
                for t in chunks[c]:
                    for a in range(NA):
                        ins = nc.tensor.matmul(O[64 * a:64 * a + V1, 0:TP], V[u][:, t, h, :], PT[n % 2][:, t, a * TP:(a + 1) * TP],
                                               start=(t == 0), stop=(t == nt - 1))
                if c == NC - 1:
                    ins.then_inc(av_done.sem, 1)

            def turned_back(it, n, last=False):
                pe.wait_ge(ot_out.sem, ot_out.at(it, n, NA))
                if one_bank:
                    rows = n + 1 + AHEAD
                    pe.wait_ge(row_out.sem, row_out.at(it, min(rows, NH - 1) if last else rows, 1))
                pe.wait_ge(o_out.sem, o_out.at(it, n - 1, 1))
                nc.tensor.transpose(Oq[:TP, 0:128], OT[n % 2][:, :], ident[:, :]).then_inc(o_done.sem, 1)

            def body(it, first, last):
                for n in range(NH):
                    ahead = not (last and n + AHEAD > NH - 1)
                    if ahead:
                        scores(it, n + AHEAD, 0)
                    if NC == 1:
                        scores_T(it, n, 0)
                    if not (last and n + AHEAD - 1 > NH - 1):
                        rows_of_max(it, n + AHEAD - 1)
                    if not (first and n == 0):
                        values(it, n - 1, 0)
                    if not (first and n < 2):
                        turned_back(it, n - 2, last)
                    if NC > 1:
                        scores_T(it, n, 0)
                        if ahead:
                            scores(it, n + AHEAD, 1)
                        if not (first and n == 0):
                            values(it, n - 1, 1)
                        scores_T(it, n, 1)
                if last:
                    turned_back(it, NH - 2, True)
                    for c in range(NC):
                        values(it, NH - 1, c)
                    turned_back(it, NH - 1, True)

            for n in range(AHEAD):
                for turn in range(SA):
                    scores(0, n, turn)
                if n < AHEAD - 1:
                    rows_of_max(0, n)
            body(0, True, False)
            with pe.Fori(1, steps - 1) as it:
                body(it, False, False)
            body(steps - 1, False, True)

        @block.scalar
        def _(act):
            act.sem_inc(exp_done.sem, NH * exp_done.k)
            act.sem_inc(ot_out.sem, NH * ot_out.k)
            act.sem_inc(row_out.sem, NH * row_out.k)
            act.wait_ge(ones_set, GB + 2)

            def exponential(it, n, c):
                act.wait_ge(st_done.sem, st_done.at(it, n, c + 1))
                ts = chunks[c]
                bank = ST[c if NC > 1 else n % 2]
                full = len(ts) // 2
                dst = PT[n % 2][:, ts[0]:ts[0] + 2 * full, :].rearrange("p (b t) q -> p b (t q)", t=2)
                ins = nc.scalar.activation(dst, bank[:, 0:full, 0:2 * T], ACT.Exp)
                assert len(ts) % 2 == 0
                ins.then_inc(exp_done.sem, 1)

            def into_stack(it, n):
                u, h = n // 4 % GB, n % 4
                act.wait_ge(row_done.sem, row_done.at(it, n, 1))
                nc.scalar.activation(Q[u][1][96:98, h, :], R[96:98, 0:T], ACT.Copy).then_inc(row_out.sem, 1)

            def take_OT(it, n):
                act.wait_ge(av_done.sem, av_done.at(it, n, 1))
                act.wait_ge(o_done.sem, o_done.at(it, n - 2, 1))
                for a in range(NA):
                    nc.scalar.activation(OT[n % 2][64 * a:64 * a + V1, :], O[64 * a:64 * a + V1, 0:TP],
                                         ACT.Copy).then_inc(ot_out.sem, 1)

            def body(it, first, last):
                for n in range(NH):
                    if NC == 1:
                        exponential(it, n, 0)
                    if not (last and n + AHEAD - 1 > NH - 1):
                        into_stack(it, n + AHEAD - 1)
                    if NC > 1:
                        exponential(it, n, 0)
                    if not (first and n == 0):
                        take_OT(it, n - 1)
                    if NC > 1:
                        exponential(it, n, 1)
                if last:
                    take_OT(it, NH - 1)

            if AHEAD > 1:
                into_stack(0, 0)
            body(0, True, False)
            with act.Fori(1, steps - 1) as it:
                body(it, False, False)
            body(steps - 1, False, True)

        @block.vector
        def _(dve):
            for f in (max_done, shift_done, o_out, cast_done, rinv_done):
                dve.sem_inc(f.sem, NH * f.k)
            dve.wait_ge(fixed_loaded, 16 * n_fixed)
            for i in range(2):
                nc.vector.memset(OT[i][:, :], 0.0).then_inc(ones_set, 1)
            nc.vector.tensor_copy(identb[:, :], ident[:, :]).then_inc(fixed_made, 1)
            if mask is not None:
                nc.vector.tensor_copy(mask_q[:, :, :], mask_f[:, :, :]).then_inc(fixed_made, 1)
                nc.vector.tensor_copy(mask_k[:, :, :], maskT_f[:, :, :]).then_inc(fixed_made, 1)

            def maximum(it, n, turn):
                if turn == 0:
                    dve.wait_ge(shift_done.sem, shift_done.at(it, n - 2, 1))
                dve.wait_ge(s_done.sem, s_done.at(it, n, turn + 1))
                if SA == 1:
                    both = S[n % 2][:, 0, 0:NA * nk].rearrange("p (a c) -> p a c", a=NA)
                    nc.vector.tensor_reduce(nmax[n % 2][:, :], both, X, ALU.max, negate=True).then_inc(max_done.sem, 1)
                else:
                    nc.vector.tensor_reduce(nmax[n % 2][:, turn:turn + 1], S[0][:, :, 0:ncb], mybir.AxisListType.XY, ALU.max,
                                            negate=True).then_inc(max_done.sem, 1)

            def shifts(it, n):
                dve.wait_ge(max_done.sem, max_done.at(it, n, SA))
                dve.wait_ge(row_done.sem, row_done.at(it, n - 2, 1))
                nc.vector.tensor_copy(shift[n % 2][:, :, 0], nmax[n % 2][:, :]).then_inc(cast_done.sem, 1)
                dve.wait_ge(cast_done.sem, cast_done.at(it, n, 1))
                nc.vector.tensor_tensor(shift[n % 2][:, :, 1], nmax[n % 2][:, :], shift[n % 2][:, :, 0],
                                        ALU.subtract).then_inc(shift_done.sem, 1)

            def outputs(it, n):
                u, h = n // 4 % GB, n % 4
                dve.wait_ge(o_done.sem, o_done.at(it, n, 1))
                dve.wait_ge(o_out.sem, o_out.at(it, n - 1, 1))
                both = Oq[:TP, 0:128].rearrange("p (a d) -> p a d", a=NA)
                nc.vector.reciprocal(rinv[:, n % 2, :], both[:, :, HD]).then_inc(rinv_done.sem, 1)
                if h == 0:
                    dve.wait_ge(out_free[u].sem, out_free[u].before(it))
                dve.wait_ge(rinv_done.sem, rinv_done.at(it, n, 1))
                nc.vector.tensor_tensor(o_sb[u][:, :, h * HD:(h + 1) * HD], both[:, :, 0:HD],
                                        rinv[:, n % 2, :].unsqueeze(2).broadcast_to([TP, NA, HD]), ALU.mult).then_inc(o_out.sem, 1)

            def body(it, first, last):
                for n in range(NH):
                    more = not (last and n + AHEAD > NH - 1)
                    if more:
                        maximum(it, n + AHEAD, 0)
                        if SA == 1:
                            shifts(it, n + AHEAD)
                    if not (first and n < 2):
                        outputs(it, n - 2)
                    if more and SA > 1:
                        maximum(it, n + AHEAD, 1)
                        shifts(it, n + AHEAD)
                if last:
                    outputs(it, NH - 2)
                    outputs(it, NH - 1)

            for n in range(AHEAD):
                for turn in range(SA):
                    maximum(0, n, turn)
                shifts(0, n)
            body(0, True, False)
            with dve.Fori(1, steps - 1) as it:
                body(it, False, False)
            body(steps - 1, False, True)


def route(nc, stage, first_layer, logits, cap, consts, table, slots, weights):
    NT, NB = NTOK // 128, (2 if first_layer else 1) * (NTOK // 128)
    OUT = 16384.0
    with ExitStack() as ctx:
        r = Room(nc, ctx, stage)
        lg, gates = r.sb("lg", [128, NT, NE]), r.sb("gates", [128, NT, NE])
        top, topi = r.sb("top", [128, NT, NE]), r.sb("topi", [128, NT, NE], U32)
        topf = r.sb("topf", [128, NT, NE])
        m, s = r.sb("m", [128, NT]), r.sb("s", [128, NT])
        iota, tri, ones = r.sb("iota", [128, NT, NE]), r.sb("tri", [128, 128]), r.sb("ones", [128, 128])
        tok = r.sb("tok", [128, NT], U32)
        hot = r.sb("hot", [128, 2, NT, NE])
        both = r.sb("both", [128, 2, NT, NE])
        pre = r.sb("pre", [128, NB + 1, NE])
        rank = r.sb("rank", [128, 2, NT, NE])
        place, ok, slot = r.sb("place", [128, 2, NT]), r.sb("ok", [128, 2, NT]), r.sb("slot", [128, 2, NT])
        sc_f, sc_i = r.sb("sc_f", [128, 2, NT]), r.sb("sc_i", [128, 2, NT], U32)
        ga_i = r.sb("ga_i", [128, NT, 2], U32)
        wt = r.sb("wt", [128, NT, 2])
        zero = r.sb("zero", [112, NE * cap // 112], U32)
        pos = r.ps("pos", [128, NB, NE])
        loaded, zero_set, zeroed, counted = (r.sem(x) for x in ("loaded", "zero_set", "zeroed", "counted"))
        dve_step, exp_in, exp_out, hot_ready = (r.sem(x) for x in ("dve_step", "exp_in", "exp_out", "hot_ready"))
        ready, scattered, kept = r.sem("ready"), r.sem("scattered"), r.sem("kept")
        block = ctx.enter_context(nc.Block())

        @block.sync
        def _(sp):
            sp.dma_start(lg[:, :, :], logits.rearrange("(t p) e -> p t e", p=128)).then_inc(loaded, 16)
            sp.dma_start(iota[:, :, :], consts["iota"]).then_inc(loaded, 16)
            sp.dma_start(tri[:, :], consts["tri"]).then_inc(loaded, 16)
            sp.dma_start(tok[:, :], consts["tok"]).then_inc(loaded, 16)
            sp.wait_ge(zero_set, 1)
            sp.dma_start(table.rearrange("(p n) o -> p (n o)", p=112), zero[:, :]).then_inc(zeroed, 16)
            sp.wait_ge(ready, 1)
            sp.dma_start(slots.rearrange("t p k -> p t k"), ga_i[:, :, :]).then_inc(kept, 16)
            sp.dma_start(weights.rearrange("t p k -> p t k"), wt[:, :, :]).then_inc(kept, 16)
            sp.wait_ge(kept, 32)

        @block.gpsimd
        def _(pool):
            pool.memset(zero[:, :], 0).then_inc(zero_set, 1)
            pool.memset(ones[:, :], 1.0).then_inc(zero_set, 1)
            pool.wait_ge(zeroed, 16)
            pool.wait_ge(ready, 1)
            for k in range(2):
                for t in range(NT):
                    pool.indirect_dma_start(out=table, out_offset=bass.IndirectOffsetOnAxis(ap=sc_i[:, k, t:t + 1], axis=0),
                                            in_=tok[:, t:t + 1], in_offset=None, bounds_check=NE * cap - 1,
                                            oob_is_err=False).then_inc(scattered, 16)
            pool.wait_ge(scattered, 16 * 2 * NT)

        @block.tensor
        def _(pe):
            pe.wait_ge(zero_set, 2)
            pe.wait_ge(hot_ready, 1)
            src = hot[:, :, :, :].rearrange("p k t e -> p (k t e)") if first_layer else both[:, 0, :, :].rearrange("p t e -> p (t e)")
            out = pos[:, :, :].rearrange("p t e -> p (t e)")
            nc.tensor.matmul(out, tri[:, :], src, start=True, stop=False)
            nc.tensor.matmul(out, ones[:, :], pre[:, 0:NB, :].rearrange("p t e -> p (t e)"), start=False, stop=True).then_inc(counted, 1)

        @block.scalar
        def _(act):
            act.wait_ge(exp_in, 1)
            src = s[:, :] if first_layer else gates[:, :, :]
            nc.scalar.activation(src, src, ACT.Exp).then_inc(exp_out, 1)

        @block.vector
        def _(dve):
            step = [0]

            def then(ins):
                ins.then_inc(dve_step, 1)
                step[0] += 1
                dve.wait_ge(dve_step, step[0])

            dve.wait_ge(loaded, 64)
            if first_layer:
                chosen = lg
            else:
                then(nc.vector.tensor_reduce(m[:, :], lg[:, :, :], X, ALU.max))
                nc.vector.tensor_tensor(gates[:, :, :], lg[:, :, :], m[:, :].unsqueeze(2).broadcast_to([128, NT, NE]),
                                        ALU.subtract).then_inc(exp_in, 1)
                dve.wait_ge(exp_out, 1)
                then(nc.vector.tensor_reduce(s[:, :], gates[:, :, :], X, ALU.add))
                then(nc.vector.reciprocal(m[:, :], s[:, :]))
                then(nc.vector.tensor_tensor(gates[:, :, :], gates[:, :, :], m[:, :].unsqueeze(2).broadcast_to([128, NT, NE]), ALU.mult))
                chosen = gates
            for t in range(NT):
                then(nc.vector.max(top[:, t, :], chosen[:, t, :]))
                then(nc.vector.max_index(topi[:, t, :], top[:, t, :], chosen[:, t, :]))
            then(nc.vector.tensor_copy(topf[:, :, :], topi[:, :, :]))
            for k in range(2):
                then(nc.vector.tensor_tensor(hot[:, k, :, :], iota[:, :, :], topf[:, :, k:k + 1].broadcast_to([128, NT, NE]), ALU.is_equal))
            if not first_layer:
                then(nc.vector.tensor_tensor(both[:, 0, :, :], hot[:, 0, :, :], hot[:, 1, :, :], ALU.add))
            blocks = [hot[:, j // NT, j % NT, :] if first_layer else both[:, 0, j, :] for j in range(NB)]
            then(nc.vector.memset(pre[:, 0, :], 0.0))
            for j in range(NB):
                ins = nc.vector.tensor_tensor(pre[:, j + 1, :], pre[:, j, :], blocks[j], ALU.add)
                if j < NB - 1:
                    then(ins)
            ins.then_inc(hot_ready, 1)
            if first_layer:
                nc.vector.tensor_tensor(s[:, :], top[:, :, 1], top[:, :, 0], ALU.subtract).then_inc(exp_in, 1)
                dve.wait_ge(exp_out, 1)
                then(nc.vector.tensor_scalar(m[:, :], s[:, :], 1.0, None, ALU.add))
                then(nc.vector.reciprocal(wt[:, :, 0], m[:, :]))
                then(nc.vector.tensor_tensor(wt[:, :, 1], s[:, :], wt[:, :, 0], ALU.mult))
            else:
                then(nc.vector.tensor_copy(wt[:, :, :], top[:, :, 0:2]))
            dve.wait_ge(counted, 1)
            for k in range(2):
                p = pos[:, k * NT:(k + 1) * NT, :] if first_layer else pos[:, :, :]
                then(nc.vector.tensor_tensor(rank[:, k, :, :], p, hot[:, k, :, :], ALU.mult))
                then(nc.vector.tensor_reduce(place[:, k, :], rank[:, k, :, :], X, ALU.add))
            then(nc.vector.tensor_scalar(place[:, :, :], place[:, :, :], -1.0, None, ALU.add))
            then(nc.vector.tensor_scalar(ok[:, :, :], place[:, :, :], float(cap), None, ALU.is_lt))
            for k in range(2):
                then(nc.vector.scalar_tensor_tensor(slot[:, k, :], topf[:, :, k], float(cap), place[:, k, :], ALU.mult, ALU.add))
            then(nc.vector.scalar_tensor_tensor(sc_f[:, :, :], slot[:, :, :], -OUT, ok[:, :, :], ALU.add, ALU.mult))
            then(nc.vector.tensor_scalar(sc_i[:, :, :], sc_f[:, :, :], OUT, None, ALU.add))
            then(nc.vector.tensor_tensor(slot[:, :, :], slot[:, :, :], ok[:, :, :], ALU.mult))
            for k in range(2):
                then(nc.vector.tensor_copy(ga_i[:, :, k], slot[:, k, :]))
                ins = nc.vector.tensor_tensor(wt[:, :, k], wt[:, :, k], ok[:, k, :], ALU.mult)
                if k == 0:
                    then(ins)
            ins.then_inc(ready, 1)


def experts(nc, stage, cap, tiles, x, w1, w2, b1, b2, table, out, consts):
    gelu = b1 is not None
    FC = FF // 128
    nh = 2 if cap > 512 else 1
    hc = cap // nh
    jobs = [("h", (f, s)) for f in range(FC) for s in range(nh)] \
        + [("o", (c, s)) for c in range(C) for s in range(nh)] + [("tb", i) for i in range(len(tiles))]
    NJ, RING, NTL = len(jobs), 6, len(tiles)
    on_act = [j[0] == "h" for j in jobs]
    NO = C * nh
    nth = lambda m: sum(1 for k in range(m + 1) if on_act[k] == on_act[m])
    first_o = NJ - NTL - NO
    with ExitStack() as ctx:
        r = Room(nc, ctx, stage)
        ident = r.sb("ident", [128, 128])
        idx = r.sb("idx", [128, NTL], U32)
        xg = r.sb("xg", [TP, NTL, D])
        xT = r.sb("xT", [128, C, cap])
        w1s, w2s = r.sb("w1", [128, C, FF]), r.sb("w2", [128, FC, D])
        hT = r.sb("hT", [128, FC, cap])
        oT = r.sb("oT", [128, C, cap])
        o = r.sb("o", [TP, NTL, D])
        if gelu:
            b1s, b2s = r.sb("b1", [128, FC]), r.sb("b2", [128, C])
        ring = [r.ps(f"ring{i}", [128, 512]) for i in range(RING)]
        turned = [r.ps(f"turned{i}", [128, 512]) for i in range(2)]
        fixed = r.sem("fixed")
        idx_loaded, gathered = r.event("idx_loaded", 16 * NTL, False), r.event("gathered", 16 * NTL, False)
        w1_loaded, w2_loaded = r.event("w1_loaded", 16 * (C + gelu)), r.event("w2_loaded", 16 * (4 + gelu))
        tp_done, tp_out = Flow(r.sem("tp_done"), NTL, 1), Flow(r.sem("tp_out"), NTL, 1)
        mm_done = r.event("mm_done", NJ)
        act_out, dve_out = r.event("act_out", first_o), r.event("dve_out", NO + NTL)
        squared = r.event("squared", FC * nh)
        stored = r.event("stored", 16 * NTL)
        block = ctx.enter_context(nc.Block())

        @block.sync
        def _(sp):
            sp.dma_start(ident[:, :], consts["ident"]).then_inc(fixed, 16)
            for e in (w1_loaded, w2_loaded):
                sp.sem_inc(e.sem, e.per)
            with sp.Fori(0, NE) as it:
                sp.wait_ge(mm_done.sem, mm_done.before(it, first_o))
                sp.nop(nofuse=True)
                for c in range(C):
                    sp.dma_start(w1s[:, c, :], w1[bass.ds(it * D + c * 128, 128), :]).then_inc(w1_loaded.sem, 16)
                if gelu:
                    sp.wait_ge(act_out.sem, act_out.before(it))
                    sp.nop(nofuse=True)
                    sp.dma_start(b1s[:, :], b1[bass.ds(it * 128, 128), :]).then_inc(w1_loaded.sem, 16)
                sp.wait_ge(mm_done.sem, mm_done.before(it))
                sp.nop(nofuse=True)
                for c in range(4):
                    sp.dma_start(w2s[:, c * 4:(c + 1) * 4, :],
                                 w2[bass.ds(it * FF + c * 512, 512), :].rearrange("(f p) n -> p f n", p=128)).then_inc(w2_loaded.sem, 16)
                if gelu:
                    sp.wait_ge(dve_out.sem, dve_out.before(it))
                    sp.nop(nofuse=True)
                    sp.dma_start(b2s[:, :], b2[bass.ds(it * 128, 128), :]).then_inc(w2_loaded.sem, 16)

        @block.gpsimd
        def _(pool):

            def gather(it):
                for i, (r0, n) in enumerate(tiles):
                    pool.dma_start(idx[:n, i:i + 1], table[bass.ds(it * cap + r0, n), :]).then_inc(idx_loaded.sem, 16)
                pool.wait_ge(idx_loaded.sem, idx_loaded.now(it, idx_loaded.per))
                pool.wait_ge(tp_done.sem, tp_done.at(it, -1))
                pool.nop(nofuse=True)
                for i, (r0, n) in enumerate(tiles):
                    pool.indirect_dma_start(out=xg[:n, i, :], out_offset=None, in_=x,
                                            in_offset=bass.IndirectOffsetOnAxis(ap=idx[:n, i:i + 1], axis=0)).then_inc(gathered.sem, 16)
                pool.wait_ge(gathered.sem, gathered.now(it, gathered.per))
                pool.nop(nofuse=True)

            with pool.Fori(0, NE) as it:
                gather(it)

        @block.tensor
        def _(pe):
            pe.sem_inc(mm_done.sem, NJ)
            pe.sem_inc(tp_done.sem, NTL)
            pe.wait_ge(fixed, 16)

            def turn_tiles(it, e):
                for i, (r0, n) in enumerate(tiles):
                    pe.wait_ge(tp_out.sem, tp_out.at(it, e, i - 1) if i > 1 else tp_out.at(it, e - 1))
                    if i == 0:
                        pe.wait_ge(gathered.sem, gathered.now(it, gathered.per * (e + 1)))
                    pe.nop(nofuse=True)
                    for c in range(C):
                        ins = nc.tensor.transpose(turned[i % 2][:, c * n:(c + 1) * n], xg[:n, i, c * 128:(c + 1) * 128], ident[:n, :n])
                    ins.then_inc(tp_done.sem, 1)

            def body(it, last):
                for m, (kind, i) in enumerate(jobs):
                    if m == first_o + 2 and not last:
                        turn_tiles(it, 1)
                    bank = ring[m % RING]
                    if m >= RING:
                        k, v = m - RING, 1
                    else:
                        k, v = max(k for k in range(NJ) if k % RING == m), 0
                    e = act_out if on_act[k] else dve_out
                    if kind != "tb" or e is not dve_out:
                        pe.wait_ge(e.sem, e.now(it, nth(k)) if v else e.before(it, nth(k)))
                    if kind == "h":
                        f, s = i
                        if m == 0:
                            pe.wait_ge(w1_loaded.sem, w1_loaded.now(it, w1_loaded.per))
                            pe.wait_ge(tp_out.sem, tp_out.at(it, 0))
                        for c in range(C):
                            ins = nc.tensor.matmul(bank[:, :hc], w1s[:, c, f * 128:(f + 1) * 128], xT[:, c, s * hc:(s + 1) * hc],
                                                   start=(c == 0), stop=(c == C - 1))
                    elif kind == "tb":
                        r0, n = tiles[i]
                        pe.wait_ge(dve_out.sem, dve_out.now(it, NO))
                        pe.nop(nofuse=True)
                        for c in range(C):
                            ins = nc.tensor.transpose(bank[:n, c * 128:(c + 1) * 128], oT[:, c, r0:r0 + n], ident[:, :])
                    else:
                        c, s = i
                        if m == first_o:
                            pe.wait_ge(w2_loaded.sem, w2_loaded.now(it, w2_loaded.per))
                            e = act_out if gelu else squared
                            pe.wait_ge(e.sem, e.now(it, e.per))
                        for f in range(FC):
                            ins = nc.tensor.matmul(bank[:, :hc], w2s[:, f, c * 128:(c + 1) * 128], hT[:, f, s * hc:(s + 1) * hc],
                                                   start=(f == 0), stop=(f == FC - 1))
                    ins.then_inc(mm_done.sem, 1)

            turn_tiles(0, 0)
            with pe.Fori(0, NE - 1) as it:
                body(it, False)
            body(NE - 1, True)

        @block.scalar
        def _(act):
            act.sem_inc(act_out.sem, act_out.per)
            act.sem_inc(stored.sem, stored.per)
            act.sem_inc(tp_out.sem, NTL)

            def take_tiles(it, e):
                for i, (r0, n) in enumerate(tiles):
                    act.wait_ge(tp_done.sem, tp_done.at(it, e, i + 1))
                    nc.scalar.activation(xT[:, :, r0:r0 + n], turned[i % 2][:, :C * n].rearrange("p (c t) -> p c t", c=C),
                                         ACT.Copy).then_inc(tp_out.sem, 1)

            def body(it, last):
                for m, (kind, i) in enumerate(jobs):
                    if m == first_o and not last:
                        take_tiles(it, 1)
                    bank = ring[m % RING]
                    if kind == "o":
                        continue
                    if kind == "tb":
                        r0, n = tiles[i]
                        act.wait_ge(dve_out.sem, dve_out.now(it, NO + i + 1))
                        act.dma_start(out[bass.ds(it * cap + r0, n), :], o[:n, i, :]).then_inc(stored.sem, 16)
                        continue
                    act.wait_ge(mm_done.sem, mm_done.now(it, m + 1))
                    if gelu:
                        f, s = i
                        if m == 0:
                            act.wait_ge(w1_loaded.sem, w1_loaded.now(it, w1_loaded.per))
                        nc.scalar.activation(hT[:, f, s * hc:(s + 1) * hc], bank[:, :hc], ACT.Gelu,
                                             bias=b1s[:, f:f + 1]).then_inc(act_out.sem, 1)
                    else:
                        f, s = i
                        nc.scalar.activation(hT[:, f, s * hc:(s + 1) * hc], bank[:, :hc], ACT.Relu).then_inc(act_out.sem, 1)

            take_tiles(0, 0)
            with act.Fori(0, NE - 1) as it:
                body(it, False)
            body(NE - 1, True)
            act.wait_ge(stored.sem, stored.end(NE))

        @block.vector
        def _(dve):
            dve.sem_inc(dve_out.sem, dve_out.per)
            dve.sem_inc(squared.sem, squared.per)
            with dve.Fori(0, NE) as it:
                for m, (kind, i) in enumerate(jobs):
                    if kind == "h" and not gelu:
                        f, s = i
                        dve.wait_ge(act_out.sem, act_out.now(it, m + 1))
                        dst = hT[:, f, s * hc:(s + 1) * hc]
                        nc.vector.tensor_tensor(dst, dst, dst, ALU.mult).then_inc(squared.sem, 1)
                    elif kind == "o":
                        c, s = i
                        dve.wait_ge(mm_done.sem, mm_done.now(it, m + 1))
                        dst = oT[:, c, s * hc:(s + 1) * hc]
                        if gelu:
                            if m == first_o:
                                dve.wait_ge(w2_loaded.sem, w2_loaded.now(it, w2_loaded.per))
                            nc.vector.tensor_scalar(dst, ring[m % RING][:, :hc], b2s[:, c:c + 1], None, ALU.add).then_inc(dve_out.sem, 1)
                        else:
                            nc.vector.tensor_copy(dst, ring[m % RING][:, :hc]).then_inc(dve_out.sem, 1)
                    elif kind == "tb":
                        r0, n = tiles[i]
                        dve.wait_ge(mm_done.sem, mm_done.now(it, m + 1))
                        if i == 0:
                            dve.wait_ge(stored.sem, stored.before(it))
                        nc.vector.tensor_copy(o[:n, i, :], ring[m % RING][:n, :]).then_inc(dve_out.sem, 1)


def combine(nc, stage, x, rows, slots, weights, out):
    NT = NTOK // 128
    UB = NT // 2
    steps = NT // UB
    with ExitStack() as ctx:
        r = Room(nc, ctx, stage)
        xs = [r.sb(f"x{u}", [128, D]) for u in range(UB)]
        idx = [r.sb(f"idx{u}", [128, 2], U32) for u in range(UB)]
        wt = [r.sb(f"wt{u}", [128, 2]) for u in range(UB)]
        g = [[r.sb(f"g{u}{k}", [128, D]) for k in range(2)] for u in range(UB)]
        y = [r.sb(f"y{u}", [128, D]) for u in range(UB)]
        t = [r.sb(f"t{u}", [128, D]) for u in range(UB)]
        stats, mv = r.sb("stats", [128, UB, 6]), r.sb("mv", [128, UB, 2])
        std, rstd, eps = r.sb("std", [128, UB]), r.sb("rstd", [128, UB]), r.sb("eps", [128, 1])
        eps_set = r.sem("eps_set")
        idx_loaded, x_loaded = [[r.event(f"{s}{u}", per) for u in range(UB)] for s, per in (("idx_loaded", 16), ("x_loaded", 32))]
        gathered = [r.event(f"gathered{u}", 32, False) for u in range(UB)]
        y_ready, var_ready, std_ready = (r.event(s, UB) for s in ("y_ready", "var_ready", "std_ready"))
        stored = [r.event(f"stored{u}", 16) for u in range(UB)]
        dve_step = r.sem("dve_step")
        block = ctx.enter_context(nc.Block())

        @block.sync
        def _(sp):
            for e in idx_loaded + x_loaded:
                sp.sem_inc(e.sem, e.per)
            with sp.Fori(0, steps) as it:
                for u in range(UB):
                    sp.wait_ge(y_ready.sem, y_ready.before(it, u + 1))
                    sp.dma_start(idx[u][:, :], slots[bass.ds(it * UB + u, 1), :, :].rearrange("t p k -> (t p) k")).then_inc(idx_loaded[u].sem, 16)
                    sp.dma_start(wt[u][:, :], weights[bass.ds(it * UB + u, 1), :, :].rearrange("t p k -> (t p) k")).then_inc(x_loaded[u].sem, 16)
                    sp.dma_start(xs[u][:, :], x[bass.ds((it * UB + u) * 128, 128), :]).then_inc(x_loaded[u].sem, 16)

        @block.gpsimd
        def _(pool):
            pool.memset(eps[:, :], EPS).then_inc(eps_set, 1)
            with pool.Fori(0, steps) as it:
                for u in range(UB):
                    pool.wait_ge(idx_loaded[u].sem, idx_loaded[u].now(it, 16))
                    pool.wait_ge(y_ready.sem, y_ready.before(it, u + 1))
                    pool.nop(nofuse=True)
                    for k in range(2):
                        pool.indirect_dma_start(out=g[u][k][:, :], out_offset=None, in_=rows,
                                                in_offset=bass.IndirectOffsetOnAxis(ap=idx[u][:, k:k + 1], axis=0)).then_inc(gathered[u].sem, 16)

        @block.scalar
        def _(act):
            for e in [std_ready] + stored:
                act.sem_inc(e.sem, e.per)
            act.wait_ge(eps_set, 1)
            with act.Fori(0, steps) as it:
                for u in range(UB):
                    act.wait_ge(var_ready.sem, var_ready.now(it, u + 1))
                    nc.scalar.activation(std[:, u:u + 1], mv[:, u, 1:2], ACT.Sqrt, bias=eps[:, :]).then_inc(std_ready.sem, 1)
                    act.wait_ge(y_ready.sem, y_ready.now(it, u + 1))
                    act.dma_start(out[bass.ds((it * UB + u) * 128, 128), :], y[u][:, :]).then_inc(stored[u].sem, 16)
            for e in stored:
                act.wait_ge(e.sem, e.end(steps))

        @block.vector
        def _(dve):
            for e in (y_ready, var_ready):
                dve.sem_inc(e.sem, e.per)
            with dve.Fori(0, steps) as it:
                own = Chain(dve, dve_step, it, 4 * UB)
                for u in range(UB):
                    dve.wait_ge(x_loaded[u].sem, x_loaded[u].now(it, 32))
                    dve.wait_ge(gathered[u].sem, gathered[u].now(it, 32))
                    own.done(nc.vector.scalar_tensor_tensor(t[u][:, :], g[u][0][:, :], wt[u][:, 0:1], xs[u][:, :], ALU.mult, ALU.add))
                    dve.wait_ge(dve_step, own.last())
                    own.done(nc.vector.scalar_tensor_tensor(t[u][:, :], g[u][1][:, :], wt[u][:, 1:2], t[u][:, :], ALU.mult, ALU.add))
                    dve.wait_ge(dve_step, own.last())
                    own.done(nc.vector.bn_stats(stats[:, u, :], t[u][:, :]))
                    dve.wait_ge(dve_step, own.last())
                    dve.nop(nofuse=True)
                    nc.vector.bn_aggr(mv[:, u, :], stats[:, u, :]).then_inc(var_ready.sem, 1)
                    dve.wait_ge(std_ready.sem, std_ready.now(it, u + 1))
                    own.done(nc.vector.reciprocal(rstd[:, u:u + 1], std[:, u:u + 1]))
                    dve.wait_ge(dve_step, own.last())
                    dve.wait_ge(stored[u].sem, stored[u].before(it))
                    nc.vector.tensor_scalar(y[u][:, :], t[u][:, :], mv[:, u, 0:1], rstd[:, u:u + 1],
                                            ALU.subtract, ALU.mult).then_inc(y_ready.sem, 1)


def decoder(nc, a, out, kind="Internal", upto=99):
    def scratch(name, shape, dt=FP32):
        return nc.dram_tensor(f"scr_{name}", shape, dt, kind=kind).ap() if kind != "Internal" else nc.dram_tensor(f"scr_{name}", shape, dt).ap()

    G = B * HG
    qT, kT, v = scratch("qT", [G * 128, T]), scratch("kT", [G * 128, T]), scratch("v", [G, T, 128])
    V4 = 4 * (HD + 1)
    parts = lambda name, shape: [scratch(f"{name}_{i}", shape, BF16) for i in "hml"]
    q3, k3 = parts("q3", [G * 128, T]), parts("k3", [G * 128, T])
    ck, cv = parts("ck", [G * 128, CTXN]), scratch("cv", [G, CTXN, V4])
    pk, pv = parts("pk", [2 * HG * 128, PASTN]), scratch("pv", [2 * HG, PASTN, V4])
    wk, wv = parts("wk", [G * 128, T]), scratch("wv", [G, T, V4])
    ctx0, ctx1, ctx2 = (scratch(s, [G, T, 128]) for s in ("ctx0", "ctx1", "ctx2"))
    ctx3, ctx4 = scratch("ctx3", [2 * G, T, 128]), scratch("ctx4", [G, T, 128])
    x1, x2, x3, o1, x4, x5 = (scratch(s, [NTOK, D]) for s in ("x1", "x2", "x3", "o1", "x4", "x5"))
    lg0, lg1 = scratch("lg0", [NTOK, NE]), scratch("lg1", [NTOK, NE])
    table0, table1 = scratch("table0", [NE * CAP0, 1], U32), scratch("table1", [NE * CAP1, 1], U32)
    slots0, slots1 = (scratch(s, [NTOK // 128, 128, 2], U32) for s in ("slots0", "slots1"))
    wts0, wts1 = (scratch(s, [NTOK // 128, 128, 2]) for s in ("wts0", "wts1"))
    rows0, rows1 = scratch("rows0", [NE * CAP0, D]), scratch("rows1", [NE * CAP1, D])
    bands = [[nc.dram_tensor(f"band{u}{s}", [4, NA, TP * (BANDW + 1)], FP32).ap() for s in range(2)] for u in range(2)]
    pband = [nc.dram_tensor(f"pband{u}", [4, T * (PADW + 1)], FP32).ap() for u in range(2)]

    def heads_T(dst, n=T):
        return lambda it: dst[bass.ds(it * D, D), :].rearrange("(c p) t -> p c t", p=128)

    def three(dst):
        return tuple(heads_T(d) for d in dst)

    def heads_v(dst, tk):
        return lambda it, t: dst[bass.ds(it * HG, HG), t * tk:(t + 1) * tk, :].rearrange("g p d -> p g d")

    def grouped(src, off=0):
        return (True, lambda it, t: src[bass.ds(it * HG + off, HG), t * TP:(t + 1) * TP, :].rearrange("g p d -> p g d"))

    def rows(src):
        return lambda it: src[bass.ds(it * T, T), :].rearrange("(a p) d -> p a d", p=TP)

    def tile_rows(src):
        return (False, lambda it, t: src[bass.ds(it * T + t * TP, TP), :])

    def router(dst):
        return lambda it, t: dst[bass.ds(it * T + t * TP, TP), :]

    def cols_of(src):
        return lambda it: src[bass.ds(it * D, D), :].rearrange("(c p) t -> p c t", p=128)

    s32 = float(HD ** -0.5)
    stages = [
        lambda: token_stage(nc, "qkv0", B, T, TP, T, a, xT=cols_of(a["xT"]),
                            fm=[(a["wq0"], None, -s32, None, heads_T(qT)), (a["wk0"], None, 1.0, None, heads_T(kT))],
                            tm=[(a["wv0"], None, D, heads_v(v, TP))]),
        lambda: relative_attention(nc, "att0", qT, kT, v, ctx0, a, a["rpe_k"], a["rpe_q"], a["rpe_v"], bands, pband),
        lambda: token_stage(nc, "out0", B, T, TP, T, a, zs=[grouped(ctx0)], wz=a["wo0"], bz=a["bo0"], res=rows(a["x"]),
                            norm=True, y_out=rows(x1), fm=[(a["xq0"], None, float(D ** -0.5), None, three(q3))]),
        lambda: token_stage(nc, "ckv0", B, CTXN, 125, 375, a, xT=cols_of(a["ctxT"]),
                            fm=[(a["xk0"], None, 1.0, None, three(ck))], tm=[(a["xv0"], None, VW, heads_v(cv, 125))]),
        lambda: split_attention(nc, "xat0", 1, CTXN, 125, q3, ck, cv, ctx1, a),
        lambda: token_stage(nc, "out1", B, T, TP, T, a, zs=[grouped(ctx1)], wz=a["xo0"], bz=a["xbo0"], res=rows(x1),
                            norm=True, y_out=rows(x2), tm=[(a["wg0"], None, NE, router(lg0))]),
        lambda: route(nc, "rte0", True, lg0, CAP0, a, table0, slots0, wts0),
        lambda: experts(nc, "exp0", CAP0, [(i * TP, TP) for i in range(5)], x2, a["fc0"], a["pj0"], None, None, table0, rows0, a),
        lambda: combine(nc, "cmb0", x2, rows0, slots0, wts0, x3),
        lambda: token_stage(nc, "qkv1", B, T, TP, T, a, y_in=rows(x3),
                            fm=[(a["Wq"], a["bq"], s32, None, three(q3)), (a["Wk"], a["bk"], 1.0, None, three(k3))],
                            tm=[(a["Wv"], a["bv"], VW, heads_v(wv, TP))]),
        lambda: split_attention(nc, "att1", 1, T, TP, q3, k3, wv, ctx2, a),
        lambda: token_stage(nc, "out2", B, T, TP, T, a, zs=[grouped(ctx2)], wz=a["Wo"], bz=a["bo"], y_out=rows(o1),
                            fm=[(a["Wrq"], a["brq"], s32, None, three(q3))]),
        lambda: token_stage(nc, "pkv1", 2, PASTN, 128, 512, a, xT=cols_of(a["pastT"]),
                            fm=[(a["Wrk"], a["brk"], 1.0, None, three(pk))], tm=[(a["Wrv"], a["brv"], VW, heads_v(pv, 128))]),
        lambda: split_attention(nc, "rec1", 2, PASTN, 128, q3, pk, pv, ctx3, a, shared=True),
        lambda: token_stage(nc, "out3", B, T, TP, T, a, zs=[tile_rows(o1), grouped(ctx3), grouped(ctx3, G)], wz=a["Wg"], bz=a["bg"],
                            gate=True, res=rows(x3), norm=True, y_out=rows(x4),
                            fm=[(a["lq"], a["lqb"], None, 1, None), (a["lqr"], a["lqrb"], a["trig_q"], 2, three(q3))]),
        lambda: token_stage(nc, "wkv1", B, T, TP, T, a, xT=cols_of(a["ctx224T"]),
                            fm=[(a["lk"], a["lkb"], None, 1, None), (a["lkr"], a["lkrb"], a["trig_k"], 2, three(wk))],
                            tm=[(a["lv"], a["lvb"], VW, heads_v(wv, TP))]),
        lambda: split_attention(nc, "win1", 1, T, TP, q3, wk, wv, ctx4, a, mask=(a["window"], a["window_k"])),
        lambda: token_stage(nc, "out4", B, T, TP, T, a, zs=[grouped(ctx4)], wz=a["lo"], bz=a["lob"], res=rows(x4),
                            norm=True, y_out=rows(x5), tm=[(a["rw1"], a["rb1"], NE, router(lg1))]),
        lambda: route(nc, "rte1", False, lg1, CAP1, a, table1, slots1, wts1),
        lambda: experts(nc, "exp1", CAP1, [(0, TP), (TP, TP), (2 * TP, 56)], x5, a["w1"], a["w2"], a["b1"], a["b2"], table1, rows1, a),
        lambda: combine(nc, "cmb1", x5, rows1, slots1, wts1, out),
    ]
    for stage in stages[:upto]:
        stage()


def shape_constants():
    i = np.arange(T)
    rel = i[None, :] - i[:, None]
    tiled = lambda m: np.ascontiguousarray(m.reshape(NA, TP, T).transpose(1, 0, 2))
    far = np.stack([tiled(rel < -HALF), tiled(rel > HALF)], 1)
    window = np.where((rel <= 0) & (rel >= -64), 0.0, NEG)
    half = HD // 2
    freqs = (1.0 / 10000.0 ** (np.arange(half, dtype=np.float32) / half)).astype(np.float32)
    ang = (np.arange(T, dtype=np.float32)[:, None] * freqs[None, :]).astype(np.float32)
    cos = np.tile(np.cos(ang).T, (8, 1))
    sin = np.sin(ang).T
    sin = np.tile(np.concatenate([-sin, sin], 0), (4, 1))
    s = HD ** -0.5
    return {
        "ident": np.eye(128), "tri": np.triu(np.ones((128, 128))), "far": far, "window": tiled(window), "window_k": tiled(window.T),
        "trig_q": np.stack([cos * s, sin * s]), "trig_k": np.stack([cos, sin]),
        "iota": np.broadcast_to(np.arange(NE), (128, NTOK // 128, NE)),
        "tok": np.arange(NTOK).reshape(-1, 128).T,
    }


def laid_out(x, n):
    T2 = lambda w: w.T
    turned = lambda w: w.reshape(B if w.shape[0] == B else 2, w.shape[1], D).transpose(0, 2, 1).reshape(-1, w.shape[1])
    bias = lambda b: b.reshape(C, 128).T.reshape(-1)
    swap = (np.arange(D).reshape(H, 2, HD // 2)[:, ::-1]).reshape(-1)

    def blocks(w):
        m = np.zeros((128, 128), w.dtype)
        for h in range(4):
            m[h * HD:(h + 1) * HD, h * HD:(h + 1) * HD] = w.T
        return m

    w = n["L0_attn_w_qkv"]

    def per_head(t):
        m = np.zeros((HG, 4, HD, 4, 64), t.dtype)
        for h in range(4):
            m[:, h, :, h, :NBUCK] = t.reshape(HG, 4, HD, NBUCK)[:, h]
        return m.reshape(HG * 128, 256)

    d = {
        "x": x.reshape(NTOK, D), "xT": turned(x), "ctxT": turned(n["ctx_1024"]), "ctx224T": turned(n["ctx_1024"][:, :T]),
        "pastT": turned(n["L1_attn_past_states"].reshape(2, PASTN, D)),
        "wq0": T2(w[:D]), "wk0": T2(w[D:2 * D]), "wv0": T2(w[2 * D:]),
        "wo0": T2(n["L0_attn_w_proj"]), "bo0": n["L0_attn_b_proj"],
        "rpe_k": per_head(n["L0_attn_rpe_k_table"]), "rpe_q": per_head(n["L0_attn_rpe_q_table"]),
        "rpe_v": n["L0_attn_rpe_v_table"].reshape(HG, 4, NBUCK, HD).transpose(0, 2, 1, 3).reshape(HG * NBUCK, 128),
        "xq0": blocks(n["L0_xattn_Wq"]), "xk0": blocks(n["L0_xattn_Wk"]), "xv0": blocks(n["L0_xattn_Wv"]),
        "xo0": T2(n["L0_xattn_Wo"]), "xbo0": n["L0_xattn_bo"],
        "wg0": T2(n["L0_ffn_w_g"]), "fc0": n["L0_ffn_c_fc"].reshape(NE * D, FF), "pj0": n["L0_ffn_c_proj"].reshape(NE * FF, D),
        "lo": T2(n["L1_xattn_o_w"]), "lob": n["L1_xattn_o_b"], "lv": T2(n["L1_xattn_v_w"]), "lvb": n["L1_xattn_v_b"],
        "rw1": n["L1_ffn_router_w"], "rb1": n["L1_ffn_router_b"],
        "w1": n["L1_ffn_w1"].reshape(NE * D, FF), "w2": n["L1_ffn_w2"].reshape(NE * FF, D),
        "b1": n["L1_ffn_b1"].reshape(NE, FF // 128, 128).transpose(0, 2, 1).reshape(NE * 128, FF // 128), "b2": n["L1_ffn_b2"].reshape(NE, C, 128).transpose(0, 2, 1).reshape(NE * 128, C),
    }
    for s in ("Wq", "Wk", "Wv", "Wo", "Wrq", "Wrk", "Wrv", "Wg"):
        d[s] = n["L1_attn_" + s]
    for s in ("bq", "bk", "brq", "brk"):
        d[s] = bias(n["L1_attn_" + s])
    for s in ("bv", "bo", "brv", "bg"):
        d[s] = n["L1_attn_" + s]
    for s in ("q", "k"):
        wt, b = n[f"L1_xattn_{s}_w"], n[f"L1_xattn_{s}_b"]
        d["l" + s], d["l" + s + "b"] = T2(wt), bias(b)
        d["l" + s + "r"], d["l" + s + "rb"] = T2(wt[swap]), bias(b[swap])
    return d


def kernel(**inputs):
    import numpy as _np
    import concourse.bacc as _bacc
    from concourse import mybir as _mybir
    from concourse.bass_utils import run_bass_kernel_spmd as _run

    n = {k: _np.asarray(v) for k, v in inputs.items()}
    nc = _bacc.Bacc("TRN2", target_bir_lowering=False, num_devices=1)
    arrays, handles = {}, {}
    consts = {k: v.astype(_np.uint32 if k == "tok" else _np.float32) for k, v in shape_constants().items()}
    for name, v in {**laid_out(n["x"], n), **consts}.items():
        v = _np.ascontiguousarray(v)
        arrays["in_" + name] = v
        handles[name] = nc.dram_tensor("in_" + name, v.shape, _mybir.dt.from_np(v.dtype), kind="ExternalInput").ap()
    out = nc.dram_tensor("out_dram", (NTOK, D), FP32, kind="ExternalOutput").ap()
    decoder(nc, handles, out)
    r = _run(nc, [arrays], core_ids=[0])
    return r.results[0]["out_dram"].reshape(B, T, D)
```
